# Optimizing a Trainium2 kernel written in Bass

```python
import numpy as np
import jax
import jax.numpy as jnp

def _softmax(x, axis=-1):
    return jax.nn.softmax(x, axis=axis)

def _gelu(x):
    return jax.nn.gelu(x, approximate=True)

def _silu(x):
    return jax.nn.silu(x)

def _sigmoid(x):
    return jax.nn.sigmoid(x)

def _layernorm(x, axis=-1, eps=1e-05):
    m = jnp.mean(x, axis=axis, keepdims=True)
    v = jnp.var(x, axis=axis, keepdims=True)
    return (x - m) / jnp.sqrt(v + eps)

def _scatter_add(tgt, idx, src, axis=0):
    return tgt.at[idx].add(src)

def _segment_sum(src, seg, n):
    return jax.ops.segment_sum(src, seg, n)
kernel_name = 'mk_flamingo_gated_d2_seqx_r8_eb6572'

def setup_inputs(seed: int=0):
    np.random.seed(seed)
    _w = jnp.asarray

    def _rec_inputs():
        import jax
        import jax.numpy as jnp
        _rk = jax.random.key(seed)
        x = -0.000125 + 0.9999 * jax.random.normal(jax.random.fold_in(_rk, 1), (128, 64, 128), jnp.float32)
        _lenS = 64 - jax.random.randint(jax.random.fold_in(_rk, 7), (128,), 0, max(1, 64 // 4) + 1, jnp.int32)
        _lenS2 = 64 - jax.random.randint(jax.random.fold_in(_rk, 8), (128,), 0, max(1, 64 // 4) + 1, jnp.int32)
        _ctx_768P = jax.random.normal(jax.random.fold_in(_rk, 11), (128, 16, 96), jnp.float32)
        _ctx_768c = jax.random.dirichlet(jax.random.fold_in(_rk, 511), 0.3 * jnp.ones((16,), jnp.float32), (128, 64))
        _ctx_768t = jnp.einsum('bsk,bkd->bsd', _ctx_768c, _ctx_768P)
        _ctx_768t = _ctx_768t * jax.lax.rsqrt(jnp.mean(jnp.square(_ctx_768t)) + 1e-12) * 0.953939
        ctx_768 = 0.00272024 + 0.999456 * (_ctx_768t + 0.3 * jax.random.normal(jax.random.fold_in(_rk, 611), (128, 64, 96), jnp.float32))
        _g = jax.random.normal(jax.random.fold_in(_rk, 9001), (2, 2), jnp.float32)
        _g = jnp.sign(_g) * jnp.maximum(jnp.abs(_g), 1.0) + (_g == 0) * 1.0
        g_xattn = _g[0]
        g_ffn = _g[1]
        return (x, ctx_768, g_xattn, g_ffn)
    x, ctx_768, g_xattn, g_ffn = _rec_inputs()

    def _L0_xattn_setup():
        import jax, jax.numpy as jnp
        import numpy as np
        QUERY_DIM = 128
        CONTEXT_DIM = 96
        HEADS = 8
        DIM_HEAD = 64
        INNER = HEADS * DIM_HEAD
        key = jax.random.key(seed)
        ks = jax.random.split(key, 7)
        B, S, L = (8, 512, 77)
        x = jax.random.normal(ks[0], (B, S, QUERY_DIM), dtype=jnp.float32)
        context = jax.random.normal(ks[1], (B, L, CONTEXT_DIM), dtype=jnp.float32)
        Wq = jax.random.normal(ks[2], (QUERY_DIM, INNER), dtype=jnp.float32) * QUERY_DIM ** (-0.5)
        Wk = jax.random.normal(ks[3], (CONTEXT_DIM, INNER), dtype=jnp.float32) * CONTEXT_DIM ** (-0.5)
        Wv = jax.random.normal(ks[4], (CONTEXT_DIM, INNER), dtype=jnp.float32) * CONTEXT_DIM ** (-0.5)
        Wo = jax.random.normal(ks[5], (INNER, QUERY_DIM), dtype=jnp.float32) * INNER ** (-0.5)
        bo = jax.random.normal(ks[6], (QUERY_DIM,), dtype=jnp.float32) * 0.01
        return {'x': x, 'context': context, 'Wq': Wq, 'Wk': Wk, 'Wv': Wv, 'Wo': Wo, 'bo': bo}
    _L0_xattn_all = _L0_xattn_setup()
    _L0_xattn_in = {k: v for k, v in _L0_xattn_all.items() if k in ('Wq', 'Wk', 'Wv', 'Wo', 'bo')}
    del _L0_xattn_all

    def _L0_ffn_setup():
        import jax, jax.numpy as jnp
        import numpy as np
        B, N, D, E, DFF = (4, 256, 128, 16, 512)
        CAPACITY_FACTOR = 2.0
        CAP = int(N * CAPACITY_FACTOR / E)
        SINKHORN_ITERS = 6

        def _sinkhorn(logits, n_iters=SINKHORN_ITERS, tau=1.0):
            t = logits / tau
            for _ in range(n_iters):
                t = t - jax.scipy.special.logsumexp(t, axis=-2, keepdims=True)
                t = t - jax.scipy.special.logsumexp(t, axis=-1, keepdims=True)
            return jnp.exp(t)
        key = jax.random.key(seed)
        ks = jax.random.split(key, 6)
        scaled = lambda k, sh, fan: (jax.random.normal(k, sh, jnp.float32) / np.sqrt(fan)).astype(jnp.float32)
        return {'x': jax.random.normal(ks[0], (B, N, D), jnp.float32), 'gate_query': scaled(ks[1], (E, D), D), 'log_temp': jnp.asarray(np.log(0.5), jnp.float32), 'w1': scaled(ks[2], (E, D, DFF), D), 'b1': jnp.zeros((E, DFF), jnp.float32), 'w2': scaled(ks[3], (E, DFF, D), DFF), 'b2': jnp.zeros((E, D), jnp.float32)}
    _L0_ffn_all = _L0_ffn_setup()
    _L0_ffn_in = {k: v for k, v in _L0_ffn_all.items() if k in ('gate_query', 'log_temp', 'w1', 'b1', 'w2', 'b2')}
    del _L0_ffn_all

    def _L1_xattn_setup():
        import jax, jax.numpy as jnp
        import numpy as np
        HEADS = 16
        DIM_HEAD = 64
        SCALE = DIM_HEAD ** (-0.5)
        key = jax.random.key(seed)
        ks = jax.random.split(key, 7)
        B, Nq, Dq = (16, 512, 128)
        Nc, Dc = (77, 96)
        inner = HEADS * DIM_HEAD
        return {'x': jax.random.normal(ks[0], (B, Nq, Dq), jnp.float32), 'context': jax.random.normal(ks[1], (B, Nc, Dc), jnp.float32), 'Wq': jax.random.normal(ks[2], (Dq, inner), jnp.float32) * Dq ** (-0.5), 'Wk': jax.random.normal(ks[3], (Dc, inner), jnp.float32) * Dc ** (-0.5), 'Wv': jax.random.normal(ks[4], (Dc, inner), jnp.float32) * Dc ** (-0.5), 'Wo': jax.random.normal(ks[5], (inner, Dq), jnp.float32) * inner ** (-0.5), 'bo': jnp.zeros((Dq,), jnp.float32)}
    _L1_xattn_all = _L1_xattn_setup()
    _L1_xattn_in = {k: v for k, v in _L1_xattn_all.items() if k in ('Wq', 'Wk', 'Wv', 'Wo', 'bo')}
    del _L1_xattn_all

    def _L1_ffn_setup():
        import jax, jax.numpy as jnp
        import numpy as np
        TOP_K = 2
        key = jax.random.key(seed)
        ks = jax.random.split(key, 6)
        B, S, D, E = (8, 512, 128, 8)
        s = 1.0 / np.sqrt(D)
        return {'x': jax.random.normal(ks[0], (B, S, D), dtype=jnp.float32), 'Wr': jax.random.normal(ks[1], (D, E), dtype=jnp.float32) * s, 'br': jnp.zeros((E,), dtype=jnp.float32), 'W1': jax.random.normal(ks[2], (E, D, D), dtype=jnp.float32) * s, 'b1': jnp.zeros((E, D), dtype=jnp.float32), 'W2': jax.random.normal(ks[3], (E, D, D), dtype=jnp.float32) * s, 'b2': jnp.zeros((E, D), dtype=jnp.float32)}
    _L1_ffn_all = _L1_ffn_setup()
    _L1_ffn_in = {k: v for k, v in _L1_ffn_all.items() if k in ('Wr', 'br', 'W1', 'b1', 'W2', 'b2')}
    del _L1_ffn_all
    return {'x': x, 'ctx_768': ctx_768, 'g_xattn': g_xattn, 'g_ffn': g_ffn, 'L0_xattn_Wq': _L0_xattn_in['Wq'], 'L0_xattn_Wk': _L0_xattn_in['Wk'], 'L0_xattn_Wv': _L0_xattn_in['Wv'], 'L0_xattn_Wo': _L0_xattn_in['Wo'], 'L0_xattn_bo': _L0_xattn_in['bo'], 'L0_ffn_gate_query': _L0_ffn_in['gate_query'], 'L0_ffn_log_temp': _L0_ffn_in['log_temp'], 'L0_ffn_w1': _L0_ffn_in['w1'], 'L0_ffn_b1': _L0_ffn_in['b1'], 'L0_ffn_w2': _L0_ffn_in['w2'], 'L0_ffn_b2': _L0_ffn_in['b2'], 'L1_xattn_Wq': _L1_xattn_in['Wq'], 'L1_xattn_Wk': _L1_xattn_in['Wk'], 'L1_xattn_Wv': _L1_xattn_in['Wv'], 'L1_xattn_Wo': _L1_xattn_in['Wo'], 'L1_xattn_bo': _L1_xattn_in['bo'], 'L1_ffn_Wr': _L1_ffn_in['Wr'], 'L1_ffn_br': _L1_ffn_in['br'], 'L1_ffn_W1': _L1_ffn_in['W1'], 'L1_ffn_b1': _L1_ffn_in['b1'], 'L1_ffn_W2': _L1_ffn_in['W2'], 'L1_ffn_b2': _L1_ffn_in['b2']}

def reference(x, ctx_768, g_xattn, g_ffn, L0_xattn_Wq, L0_xattn_Wk, L0_xattn_Wv, L0_xattn_Wo, L0_xattn_bo, L0_ffn_gate_query, L0_ffn_log_temp, L0_ffn_w1, L0_ffn_b1, L0_ffn_w2, L0_ffn_b2, L1_xattn_Wq, L1_xattn_Wk, L1_xattn_Wv, L1_xattn_Wo, L1_xattn_bo, L1_ffn_Wr, L1_ffn_br, L1_ffn_W1, L1_ffn_b1, L1_ffn_W2, L1_ffn_b2):
    import jax
    import jax.numpy as jnp

    def _L0_xattn_ref(x, context, Wq, Wk, Wv, Wo, bo):
        import jax, jax.numpy as jnp
        import numpy as np
        QUERY_DIM = 128
        CONTEXT_DIM = 96
        HEADS = 8
        DIM_HEAD = 64
        INNER = HEADS * DIM_HEAD
        B, S, _ = x.shape
        L = context.shape[1]
        scale = DIM_HEAD ** (-0.5)
        q = (x @ Wq).reshape(B, S, HEADS, DIM_HEAD).transpose(0, 2, 1, 3)
        k = (context @ Wk).reshape(B, L, HEADS, DIM_HEAD).transpose(0, 2, 1, 3)
        v = (context @ Wv).reshape(B, L, HEADS, DIM_HEAD).transpose(0, 2, 1, 3)
        attn = jnp.einsum('bhsd,bhld->bhsl', q, k) * scale
        attn = jax.nn.softmax(attn, axis=-1)
        out = jnp.einsum('bhsl,bhld->bhsd', attn, v)
        out = out.transpose(0, 2, 1, 3).reshape(B, S, INNER)
        return out @ Wo + bo

    def _L0_ffn_ref(x, gate_query, log_temp, w1, b1, w2, b2):
        import jax, jax.numpy as jnp
        import numpy as np
        B, N, D, E, DFF = (4, 256, 128, 16, 512)
        CAPACITY_FACTOR = 2.0
        CAP = int(N * CAPACITY_FACTOR / E)
        SINKHORN_ITERS = 6

        def _sinkhorn(logits, n_iters=SINKHORN_ITERS, tau=1.0):
            t = logits / tau
            for _ in range(n_iters):
                t = t - jax.scipy.special.logsumexp(t, axis=-2, keepdims=True)
                t = t - jax.scipy.special.logsumexp(t, axis=-1, keepdims=True)
            return jnp.exp(t)
        b, n, d = x.shape
        gate_logits = jnp.einsum('bnd,ed->ben', x, gate_query)
        affinity_logits = gate_logits / jnp.exp(log_temp)
        affinity = _sinkhorn(affinity_logits)
        gates, idx = jax.lax.top_k(affinity, CAP)
        expert_in = jnp.take_along_axis(x[:, None, :, :], idx[..., None], axis=2)
        h = jax.nn.gelu(jnp.einsum('becd,edf->becf', expert_in, w1) + b1[None, :, None, :])
        expert_out = jnp.einsum('becf,efd->becd', h, w2) + b2[None, :, None, :]
        out = jnp.zeros_like(x)
        out = out.at[jnp.arange(b)[:, None, None], idx].add(gates[..., None] * expert_out)
        return out

    def _L1_xattn_ref(x, context, Wq, Wk, Wv, Wo, bo):
        import jax, jax.numpy as jnp
        import numpy as np
        HEADS = 16
        DIM_HEAD = 64
        SCALE = DIM_HEAD ** (-0.5)
        B, Nq, _ = x.shape
        Nc = context.shape[1]
        q = (x @ Wq).reshape(B, Nq, HEADS, DIM_HEAD).transpose(0, 2, 1, 3)
        k = (context @ Wk).reshape(B, Nc, HEADS, DIM_HEAD).transpose(0, 2, 1, 3)
        v = (context @ Wv).reshape(B, Nc, HEADS, DIM_HEAD).transpose(0, 2, 1, 3)
        sim = jnp.einsum('bhid,bhjd->bhij', q, k) * SCALE
        attn = jax.nn.softmax(sim, axis=-1)
        out = jnp.einsum('bhij,bhjd->bhid', attn, v)
        out = out.transpose(0, 2, 1, 3).reshape(B, Nq, HEADS * DIM_HEAD)
        return out @ Wo + bo

    def _L1_ffn_ref(x, Wr, br, W1, b1, W2, b2):
        import jax, jax.numpy as jnp
        import numpy as np
        TOP_K = 2
        k = TOP_K
        scores0 = x[:, 0, :] @ Wr + br
        _, idx = jax.lax.top_k(scores0, k)
        W1g, b1g = (W1[idx], b1[idx])
        W2g, b2g = (W2[idx], b2[idx])
        h = jnp.einsum('bsd,bkde->bkse', x, W1g) + b1g[:, :, None, :]
        h = jax.nn.gelu(h, approximate=False)
        o = jnp.einsum('bkse,bkef->bksf', h, W2g) + b2g[:, :, None, :]
        return jnp.sum(o, axis=1) / k
    x = x + jnp.tanh(g_xattn[0]) * _L0_xattn_ref(_layernorm(x, axis=-1), ctx_768, L0_xattn_Wq, L0_xattn_Wk, L0_xattn_Wv, L0_xattn_Wo, L0_xattn_bo)
    x = x + jnp.tanh(g_ffn[0]) * _L0_ffn_ref(_layernorm(x, axis=-1), L0_ffn_gate_query, L0_ffn_log_temp, L0_ffn_w1, L0_ffn_b1, L0_ffn_w2, L0_ffn_b2)
    x = x + jnp.tanh(g_xattn[1]) * _L1_xattn_ref(_layernorm(x, axis=-1), ctx_768, L1_xattn_Wq, L1_xattn_Wk, L1_xattn_Wv, L1_xattn_Wo, L1_xattn_bo)
    x = x + jnp.tanh(g_ffn[1]) * _L1_ffn_ref(_layernorm(x, axis=-1), L1_ffn_Wr, L1_ffn_br, L1_ffn_W1, L1_ffn_b1, L1_ffn_W2, L1_ffn_b2)
    return x

_drawn_inputs = setup_inputs


def setup_inputs(seed=0):
    import zlib

    import numpy as np

    out = dict(_drawn_inputs(seed))
    spreads = {'g_ffn': (-1.0, 0.6),
     'L0_ffn_b1': (0.0, 0.321),
     'L0_ffn_b2': (0.0, 0.1),
     'L1_xattn_bo': (0.0, 0.1),
     'L1_ffn_br': (0.0, 0.1),
     'L1_ffn_b1': (0.0, 0.1),
     'L1_ffn_b2': (0.0, 0.1)}
    factors = {}
    for name, (base, spread) in spreads.items():
        noise = np.random.default_rng([zlib.crc32(name.encode()), seed]).standard_normal(out[name].shape)
        drawn = base * np.exp(spread * noise) if base else spread * noise
        out[name] = jnp.asarray(drawn.astype(out[name].dtype))
    for name, factor in factors.items():
        out[name] = (out[name] * factor).astype(out[name].dtype)
    return out
```

```python
from contextlib import ExitStack

import concourse.bass as bass
from concourse import mybir

F32 = mybir.dt.float32
F16 = mybir.dt.float16
U32 = mybir.dt.uint32
I32 = mybir.dt.int32
ALU = mybir.AluOpType
ACT = mybir.ActivationFunctionType
AX = mybir.AxisListType

P = 128
B, N, D, DC = 128, 64, 128, 96
NT = B * N // P
DH = 64
NE, CAP, DFF = 16, 32, 512
FT = DFF // P
ITERS = 6
NE1, TOPK = 8, 2
EPS = 1e-5


class Step:

    def __init__(self, reg, mult, off):
        self.reg, self.mult, self.off = reg, mult, off

    def __add__(self, k):
        return Step(self.reg, self.mult, self.off + k)

    def __sub__(self, k):
        return self + (-k)

    def div(self, g):
        return Step(self.reg, self.mult // g, self.off // g)

    def mod(self, m):
        assert self.reg is None or self.mult % m == 0
        return self.off % m

    def inside(self, n):
        return True if self.reg is not None else 0 <= self.off < n

    def upto(self, n):
        return self if self.reg is not None or self.off <= n else Step(None, 0, n)

    def times(self, k, add=0):
        if self.reg is None:
            return self.off * k + add
        return self.reg * (self.mult * k) + (self.off * k + add)

    @property
    def value(self):
        return self.times(1)


class Counter:

    def __init__(self, handle, start):
        self.handle, self.start = handle, start


def wait(eng, sem, step, per=1, add=0):
    if isinstance(sem, Counter):
        sem, add = sem.handle, add + sem.start
    if step.reg is None and step.times(per, per + add) <= 0:
        return
    eng.wait_ge(sem, step.times(per, per + add))


def pipeline(eng, body, first, last, lo, hi, unroll):
    a = -(-lo // unroll) * unroll
    n = max(0, (hi - a) // unroll)
    b = a + n * unroll
    for j in range(first, a):
        body(Step(None, 0, j))
    if n:
        with eng.Fori(0, n) as i:
            for u in range(unroll):
                body(Step(i, unroll, a + u))
    for j in range(b, last):
        body(Step(None, 0, j))


def program(nc, I, out):
    with ExitStack() as whole:
        _build(nc, whole, I, out)


def _build(nc, whole, I, out):
    made = {}

    def sb(ctx, name, shape, dt):
        made[name] = made.get(name, 0) + 1
        return ctx.enter_context(nc.sbuf_tensor(f"{name}_{made[name]}", shape, dt))

    def ps(ctx, name, shape, dt):
        made[name] = made.get(name, 0) + 1
        return ctx.enter_context(nc.psum_tensor(f"{name}_{made[name]}", shape, dt))

    def sem(name):
        return nc.alloc_semaphore(name=name)

    class Sems:

        def __init__(self, stage):
            self.stage, self.all = stage, {}

        def __getitem__(self, name):
            if name not in self.all:
                self.all[name] = sem(f"{self.stage}_{name}")
            return self.all[name]

        def close(self):
            nc.clear_and_free_semaphores(list(self.all.values()))
            nc.all_engine_barrier()

    def load_all(eng, s, pairs):
        for to, frm in pairs:
            eng.dma_start(to, frm).then_inc(s, 16)
        return 16 * len(pairs)

    x = sb(whole, "x", [P, NT, D], F32)
    ident16 = sb(whole, "ident16", [P, P], F16)
    ident32 = sb(whole, "ident32", [P, P], F32)
    token_of_p = sb(whole, "token_of_p", [P, 1], F32)
    block_of_p = sb(whole, "block_of_p", [P, 1], F32)
    iota256 = sb(whole, "iota256", [P, 256], F16)
    eps_col = sb(whole, "eps_col", [P, 1], F32)
    zero_col = sb(whole, "zero_col", [P, 1], F32)
    gates = sb(whole, "gates", [P, 4], F32)
    tanh_g = sb(whole, "tanh_g", [P, 4], F32)
    half_g = sb(whole, "half_g", [P, 1], F32)
    stats = sb(whole, "stats", [P, NT, 6], F32)
    mean = sb(whole, "mean", [P, NT], F32)
    rstd = sb(whole, "rstd", [P, NT], F32)
    lnt = sb(whole, "lnt", [P, 3, NT], F32)

    xv = I["x"].rearrange("b n d -> (b n) d").rearrange("(t p) d -> p t d", p=P)
    cv = I["ctx_768"].rearrange("b n d -> (b n) d").rearrange("(t p) d -> p t d", p=P)
    ov = out.rearrange("b n d -> (b n) d").rearrange("(t p) d -> p t d", p=P)

    S0 = Sems("init")
    with nc.Block() as block:
        @block.sync
        def _(e):
            n = load_all(e, S0["x"], [(x[:, c:c + 16, :], xv[:, c:c + 16, :]) for c in range(0, NT, 16)])
            e.wait_ge(S0["x"], n)

        @block.scalar
        def _(e):
            n = load_all(e, S0["gates"], [(gates[:, 0:2], I["g_xattn"].partition_broadcast(P)),
                                        (gates[:, 2:4], I["g_ffn"].partition_broadcast(P))])
            e.wait_ge(S0["gates"], n)
            e.wait_ge(S0["zero"], 1)
            e.activation(tanh_g[:], gates[:], ACT.Tanh, bias=zero_col[:]).then_inc(S0["tanh"], 1)
            e.wait_ge(S0["tanh"], 1)
            e.activation(half_g[:], tanh_g[:, 3:4], ACT.Copy, scale=1.0 / TOPK)

        @block.vector
        def _(e):
            e.memset(zero_col[:], 0.0).then_inc(S0["zero"], 1)
            e.memset(eps_col[:], EPS)
            for q in range(4):
                e.memset(block_of_p[32 * q:32 * q + 32, :], float(N * q))
            e.wait_ge(S0["iota"], 1)
            e.tensor_scalar(token_of_p[64:P, :], token_of_p[64:P, :], -float(N), None, ALU.add)

        @block.gpsimd
        def _(e):
            e.memset(ident16[:], 0.0).then_inc(S0["id"], 1)
            e.memset(ident32[:], 0.0).then_inc(S0["id"], 1)
            e.wait_ge(S0["id"], 2)
            for m in (ident16, ident32):
                e.affine_select(out=m[:], in_=m[:], compare_op=ALU.not_equal, fill=1.0, base=0,
                                pattern=[[-1, P]], channel_multiplier=1)
            e.iota(token_of_p[:], [[0, 1]], base=0, channel_multiplier=1,
                   allow_small_or_imprecise_dtypes=True).then_inc(S0["iota"], 1)
            e.iota(iota256[:], [[1, 256]], base=0, channel_multiplier=0,
                   allow_small_or_imprecise_dtypes=True)

    def split(e_act, e_dve, s, k, raw, hi, lo):
        if e_act is not None:
            e_act.activation(hi, raw, ACT.Copy).then_inc(s["w_hi"], 1)
        if e_dve is not None:
            e_dve.wait_ge(s["w_hi"], k + 1)
            e_dve.tensor_tensor(lo, raw, hi, ALU.subtract).then_inc(s["w_lo"], 1)

    def products(pairs):
        (lh, ll), (rh, rl) = pairs
        return [(lh, rh), (lh, rl), (ll, rh)]

    def matmul3(e, to, left, right, start=True, stop=True):
        three = products((left, right))
        for n, (a, b) in enumerate(three):
            last = e.matmul(to, a, b, start=start and n == 0, stop=stop and n == 2)
        return last

    def norm_statistics(tag):
        s = Sems(tag)
        with nc.Block() as block:
            @block.vector
            def _(e):
                with e.Fori(0, NT // 4) as i:
                    for u in range(4):
                        e.bn_stats(stats[:, bass.ds(i * 4 + u, 1), :].rearrange("p o s -> p (o s)"),
                                   x[:, bass.ds(i * 4 + u, 1), :].rearrange("p o d -> p (o d)"))\
                         .then_inc(s["bn"], 1)
                e.wait_ge(s["bn"], NT)
                me, mo = stats[:, :, 1], stats[:, :, 4]
                e.tensor_tensor(lnt[:, 0, :], me, mo, ALU.subtract).then_inc(s["v"], 1)
                e.tensor_tensor(lnt[:, 1, :], stats[:, :, 2], stats[:, :, 5], ALU.add).then_inc(s["v"], 1)
                e.tensor_tensor(lnt[:, 2, :], me, mo, ALU.add).then_inc(s["v"], 1)
                e.wait_ge(s["v"], 3)
                e.tensor_scalar(mean[:], lnt[:, 2, :], 0.5, None, ALU.mult)
                e.scalar_tensor_tensor(lnt[:, 0, :], lnt[:, 0, :], D / 4.0, lnt[:, 0, :],
                                       ALU.mult, ALU.mult).then_inc(s["v"], 1)
                e.wait_ge(s["v"], 4)
                e.tensor_tensor(lnt[:, 1, :], lnt[:, 1, :], lnt[:, 0, :], ALU.add).then_inc(s["v"], 1)
                e.wait_ge(s["sqrt"], 1)
                e.reciprocal(rstd[:], lnt[:, 2, :])

            @block.scalar
            def _(e):
                e.wait_ge(s["v"], 5)
                e.activation(lnt[:, 2, :], lnt[:, 1, :], ACT.Sqrt, bias=eps_col[:], scale=1.0 / D)\
                 .then_inc(s["sqrt"], 1)
        s.close()

    def tile_of(t, tensor):
        return tensor[:, bass.ds(t.value, 1), :].rearrange("p o d -> p (o d)")

    def column_of(t, tensor):
        return tensor[:, bass.ds(t.value, 1)]

    def attention(tag, G, Wq, Wk, Wv, Wo, bo, gate):
        U = NT * G
        INNER = 512 * G
        norm_statistics(tag + "n")
        s = Sems(tag)
        with ExitStack() as c:
            ctx32 = sb(c, "ctx32", [P, NT, DC], F32)
            raw = sb(c, "raw", [P, 4, INNER], F32)
            wq = sb(c, "wq", [P, 2, INNER], F16)
            wk = sb(c, "wk", [DC, 2, INNER], F16)
            wv = sb(c, "wv", [DC, 2, INNER], F16)
            wo = sb(c, "wo", [P, 2, 4 * G, D], F16)
            bo_rep = sb(c, "bo_rep", [P, D], F32)
            xcf = sb(c, "xcf", [P, 2, D + DC], F32)
            xc = sb(c, "xc", [P, 2, 2, D + DC], F16)
            xT = sb(c, "xT", [P, 2, 2, P], F16)
            cT = sb(c, "cT", [DC, 2, 2, P], F16)
            qT = sb(c, "qT", [P, 2, 4, P], F16)
            kT = sb(c, "kT", [P, 2, 4, P], F16)
            vB = sb(c, "vB", [P, 2, 2, 8, P], F16)
            E = sb(c, "E", [P, 2, 4, 2, N], F32)
            Ph = sb(c, "Ph", [P, 2, 2, 4, P], F16)
            PT = sb(c, "PT", [P, 2, 4, P], F16)
            top = sb(c, "top", [P, 2, 4], F32)
            den = sb(c, "den", [P, 2, 8], F32)
            rden = sb(c, "rden", [P, 2, 8], F32)
            o32 = sb(c, "oT", [P, G, 2, 4, P], F16)
            ysum = sb(c, "ysum", [P, D], F32)
            psQ = ps(c, "psQ", [P, 4, P], F32)
            psK = ps(c, "psK", [P, 4, P], F32)
            psV = ps(c, "psV", [P, 8, DH], F32)
            psS = ps(c, "psS", [P, 2, 512], F32)
            psT = ps(c, "psT", [P, 2, 4, P], F16)
            psO = ps(c, "psO", [P, 4, P], F32)
            psXY = ps(c, "psXY", [P, 512], F32)
            psX = psXY[:, 0:256].bitcast(F16).rearrange("p (k t) -> p k t", k=4)
            psY = psXY[:, 256:384]

            with nc.Block() as block:
                weights = [(raw[:, 0, :], Wq), (raw[0:DC, 1, :], Wk), (raw[0:DC, 2, :], Wv),
                           (raw[:, 3, :].rearrange("p (k d) -> p k d", d=D), Wo.rearrange("(k p) d -> p k d", p=P))]
                parts = [(raw[:, 0, :], wq[:, 0, :], wq[:, 1, :]),
                         (raw[0:DC, 1, :], wk[:, 0, :], wk[:, 1, :]),
                         (raw[0:DC, 2, :], wv[:, 0, :], wv[:, 1, :]),
                         (raw[:, 3, :], wo[:, 0].rearrange("p k d -> p (k d)"), wo[:, 1].rearrange("p k d -> p (k d)"))]

                @block.sync
                def _(e):
                    load_all(e, s["w"], weights + [(bo_rep[:], bo.partition_broadcast(P))])
                    n = load_all(e, s["ctx"], [(ctx32[:, k:k + 16, :], cv[:, k:k + 16, :]) for k in range(0, NT, 16)])
                    e.wait_ge(s["ctx"], n)

                @block.scalar
                def _(e):
                    e.wait_ge(s["w"], 16 * 5)
                    for k, p in enumerate(parts):
                        split(e, None, s, k, *p)

                @block.vector
                def _(e):
                    e.memset(vB[:].rearrange("p a b c d -> p (a b c d)").bitcast(U32), 0)
                    e.wait_ge(s["w"], 16 * 5)
                    for k, p in enumerate(parts):
                        split(None, e, s, k, *p)

            def half(hp):
                return slice(64 * hp, 64 * hp + 64)

            def vblock(hl, par, hp):
                return vB[half(hp), par, hl, :, half(hp)]

            with nc.Block() as block:
                @block.tensor
                def _(e):
                    def body(j):
                        if j.inside(U):
                            wait(e, s["q_lo"], j)
                            wait(e, s["k_lo"], j)
                            wait(e, s["sub"], j - 1)
                            t = j.div(G)
                            g, tp = j.mod(2 * G) % G, j.mod(2 * G) // G
                            wait(e, s["cT"], t)
                            wait(e, s["v_lo"], j - 1, 2)
                            for hp in range(2):
                                for b in range(2):
                                    w = [wv[:, hl, 512 * g:512 * g + 512].rearrange(
                                        "p (k h d) -> p k h d", h=2, d=DH)[:, :, hp, :] for hl in range(2)]
                                    last = matmul3(e, psV[half(hp), 4 * b:4 * b + 4, :],
                                                   (cT[:, tp, 0, half(b)], cT[:, tp, 1, half(b)]), w)
                            last.then_inc(s["V"], 1)
                            for hp in range(2):
                                for pair in range(4):
                                    for b in range(2):
                                        tok = half(b)
                                        last = matmul3(e, psS[tok, hp, 64 * pair:64 * pair + 64],
                                                       (qT[half(hp), 0, pair, tok], qT[half(hp), 1, pair, tok]),
                                                       (kT[half(hp), 0, pair, tok], kT[half(hp), 1, pair, tok]))
                            last.then_inc(s["S"], 1)
                        if (j - 1).inside(U):
                            par = (j - 1).mod(2)
                            wait(e, s["p_lo"], j - 1)
                            wait(e, s["pt"], j - 2)
                            for hl in range(2):
                                for pair in range(4):
                                    last = e.transpose(psT[:, hl, pair, :], Ph[:, par, hl, pair, :], ident16[:])
                            last.then_inc(s["T"], 1)
                        if (j - 2).inside(U) and (j - 2).mod(2 * G) % G == G - 1:
                            t = (j - 2).div(G)
                            wait(e, s["o_lo"], j - 2)
                            wait(e, s["cT"], (t + 4 - G).upto(NT - 1))
                            for g in range(G):
                                for pair in range(4):
                                    last = matmul3(e, psY, (o32[:, g, 0, pair, :], o32[:, g, 1, pair, :]),
                                                   (wo[:, 0, 4 * g + pair, :], wo[:, 1, 4 * g + pair, :]),
                                                   g == 0 and pair == 0, g == G - 1 and pair == 3)
                            last.then_inc(s["Y"], 1)
                        if (j + 1).inside(U):
                            t = (j + 1).div(G)
                            g, tp = (j + 1).mod(2 * G) % G, (j + 1).mod(2 * G) // G
                            wait(e, s["xT"], t)
                            wait(e, s["cT"], t)
                            for dst, w, src, lo, name in ((psQ, wq, xT, "q_lo", "Q"), (psK, wk, cT, "k_lo", "K")):
                                wait(e, s[lo], j)
                                for pair in range(4):
                                    a = 512 * g + 128 * pair
                                    last = matmul3(e, dst[:, pair, :], (w[:, 0, a:a + P], w[:, 1, a:a + P]),
                                                   (src[:, tp, 0, :], src[:, tp, 1, :]))
                                last.then_inc(s[name], 1)
                        if (j + 2).inside(U) and (j + 2).mod(2 * G) % G == 0:
                            t, tp = (j + 2).div(G), (j + 2).mod(2 * G) // G
                            wait(e, s["x_lo"], t)
                            wait(e, s["y"], t - 5 + G)
                            for hl in range(2):
                                e.transpose(psX[:, hl, :], xc[:, tp, hl, 0:D], ident16[:])
                            for hl in range(2):
                                last = e.transpose(psX[0:DC, 2 + hl, :], xc[:, tp, hl, D:D + DC], ident16[:])
                            last.then_inc(s["X"], 1)
                        if (j - 1).inside(U):
                            par = (j - 1).mod(2)
                            wait(e, s["pt"], j - 1)
                            wait(e, s["v_lo"], j - 1, 2)
                            wait(e, s["o_lo"], j - 2)
                            for pair in range(4):
                                for b in range(2):
                                    last = matmul3(e, psO[:, pair, half(b)],
                                                   (vB[:, par, 0, 4 * b + pair, :], vB[:, par, 1, 4 * b + pair, :]),
                                                   (PT[:, 0, pair, half(b)], PT[:, 1, pair, half(b)]))
                            last.then_inc(s["PV"], 1)
                    pipeline(e, body, -2, U + 2, 4, U - 4, 2 * G)

                @block.scalar
                def _(e):
                    def body(j):
                        if j.inside(U):
                            par = j.mod(2)
                            wait(e, s["V"], j)
                            wait(e, s["PV"], j - 2)
                            for hp in range(2):
                                e.activation(vblock(0, par, hp), psV[half(hp)], ACT.Copy).then_inc(s["v_hi"], 1)
                        if (j - 1).inside(U):
                            wait(e, s["T"], j - 1)
                            wait(e, s["PV"], j - 2)
                            e.activation(PT[:], psT[:], ACT.Copy).then_inc(s["pt"], 1)
                        if j.inside(U):
                            par = j.mod(2)
                            wait(e, s["sub"], j)
                            e.activation(E[:, par], E[:, par], ACT.Exp, bias=zero_col[:], scale=DH ** -0.5)\
                             .then_inc(s["exp"], 1)
                        if (j + 1).inside(U):
                            wait(e, s["Q"], j + 1)
                            e.activation(qT[:, 0], psQ[:], ACT.Copy).then_inc(s["q_hi"], 1)
                            wait(e, s["K"], j + 1)
                            e.activation(kT[:, 0], psK[:], ACT.Copy).then_inc(s["k_hi"], 1)
                        if j.inside(U):
                            par = j.mod(2)
                            wait(e, s["mul"], j)
                            wait(e, s["T"], j - 2)
                            e.activation(Ph[:, par, 0].rearrange("p k (h l) -> p k h l", h=2), E[:, par],
                                         ACT.Copy).then_inc(s["p_hi"], 1)
                        if (j - 1).inside(U):
                            g = (j - 1).mod(2 * G) % G
                            wait(e, s["PV"], j - 1)
                            e.activation(o32[:, g, 0], psO[:], ACT.Copy).then_inc(s["o_hi"], 1)
                        if (j + 3).inside(U) and (j + 3).mod(2 * G) % G == 0:
                            t, tp = (j + 3).div(G), (j + 3).mod(2 * G) // G
                            wait(e, s["ln"], t)
                            wait(e, s["cc"], t)
                            wait(e, s["X"], t - 2)
                            e.activation(xc[:, tp, 0], xcf[:, tp], ACT.Copy).then_inc(s["x_hi"], 1)
                    pipeline(e, body, -3, U + 1, 4, U - 4, 2 * G)

                @block.gpsimd
                def _(e):
                    def body(j):
                        if (j + 3).inside(U) and (j + 3).mod(2 * G) % G == 0:
                            t, tp = (j + 3).div(G), (j + 3).mod(2 * G) // G
                            wait(e, s["x_lo"], t - 2)
                            e.tensor_copy(xcf[:, tp, D:D + DC], tile_of(t, ctx32)).then_inc(s["cc"], 1)
                        if j.inside(U):
                            par = j.mod(2)
                            wait(e, s["rden"], j)
                            e.tensor_tensor(E[:, par].rearrange("p k h l -> p (k h) l"),
                                            E[:, par].rearrange("p k h l -> p (k h) l"),
                                            rden[:, par, :].unsqueeze(2).broadcast_to([P, 8, N]), ALU.mult)\
                             .then_inc(s["mul"], 1)
                            wait(e, s["p_hi"], j)
                            e.tensor_tensor(Ph[:, par, 1].rearrange("p k t -> p (k t)"),
                                            E[:, par].rearrange("p k h l -> p (k h l)"),
                                            Ph[:, par, 0].rearrange("p k t -> p (k t)"), ALU.subtract)\
                             .then_inc(s["p_lo"], 1)
                    pipeline(e, body, -3, U, 4, U - 4, 2 * G)

                @block.vector
                def _(e):
                    def body(j):
                        if j.inside(U):
                            par = j.mod(2)
                            for hp in range(2):
                                wait(e, s["v_hi"], j, 2, hp - 1)
                                e.tensor_tensor(vblock(1, par, hp), psV[half(hp)], vblock(0, par, hp),
                                                ALU.subtract).then_inc(s["v_lo"], 1)
                            S = psS[:, :, 0:256].rearrange("p h (k l) -> p h k l", l=N)
                            wait(e, s["S"], j)
                            e.tensor_reduce(top[:], S, AX.X, ALU.max).then_inc(s["max"], 1)
                            wait(e, s["max"], j)
                            wait(e, s["p_lo"], j - 2)
                            e.tensor_tensor(E[:, par].rearrange("p k h l -> p h k l"), S,
                                            top[:].unsqueeze(3).broadcast_to([P, 2, 4, N]), ALU.subtract)\
                             .then_inc(s["sub"], 1)
                            wait(e, s["exp"], j)
                            e.tensor_reduce(den[:, par, :], E[:, par].rearrange("p k h l -> p (k h) l"),
                                            AX.X, ALU.add).then_inc(s["den"], 1)
                            wait(e, s["den"], j)
                            e.reciprocal(rden[:, par, :], den[:, par, :]).then_inc(s["rden"], 1)
                        if (j - 2).inside(U) and (j - 2).mod(2 * G) % G == G - 1:
                            t = (j - 2).div(G)
                            wait(e, s["Y"], t)
                            wait(e, s["res"], t - 1)
                            e.tensor_tensor(ysum[:], psY, bo_rep[:], ALU.add).then_inc(s["y"], 1)
                            wait(e, s["y"], t)
                            e.scalar_tensor_tensor(tile_of(t, x), ysum[:], gate, tile_of(t, x),
                                                   ALU.mult, ALU.add).then_inc(s["res"], 1)
                        if (j + 1).inside(U):
                            wait(e, s["q_hi"], j + 1)
                            e.tensor_tensor(qT[:, 1], psQ[:], qT[:, 0], ALU.subtract).then_inc(s["q_lo"], 1)
                            wait(e, s["k_hi"], j + 1)
                            e.tensor_tensor(kT[:, 1], psK[:], kT[:, 0], ALU.subtract).then_inc(s["k_lo"], 1)
                        if (j + 2).inside(U) and (j + 2).mod(2 * G) % G == 0:
                            t, tp = (j + 2).div(G), (j + 2).mod(2 * G) // G
                            wait(e, s["X"], t)
                            e.tensor_copy(xT[:, tp], psX[:, 0:2, :]).then_inc(s["xT"], 1)
                            e.tensor_copy(cT[:, tp], psX[0:DC, 2:4, :]).then_inc(s["cT"], 1)
                        if (j - 1).inside(U):
                            g = (j - 1).mod(2 * G) % G
                            wait(e, s["o_hi"], j - 1)
                            e.tensor_tensor(o32[:, g, 1], psO[:], o32[:, g, 0], ALU.subtract)\
                             .then_inc(s["o_lo"], 1)
                        if (j + 3).inside(U) and (j + 3).mod(2 * G) % G == 0:
                            t, tp = (j + 3).div(G), (j + 3).mod(2 * G) // G
                            wait(e, s["x_lo"], t - 2)
                            e.tensor_scalar(xcf[:, tp, 0:D], tile_of(t, x), column_of(t, mean), column_of(t, rstd),
                                            ALU.subtract, ALU.mult).then_inc(s["ln"], 1)
                            wait(e, s["x_hi"], t)
                            e.tensor_tensor(xc[:, tp, 1], xcf[:, tp], xc[:, tp, 0], ALU.subtract)\
                             .then_inc(s["x_lo"], 1)
                    pipeline(e, body, -3, U + 2, 4, U - 4, 2 * G)

        s.close()

    def queue_norm(e_dve, e_act, s, t, par, raw, pairs, read, x_lo=None):
        if e_dve is not None:
            wait(e_dve, x_lo or s["x_lo"], t - 2)
            e_dve.tensor_scalar(raw[:, par], tile_of(t, x), column_of(t, mean), column_of(t, rstd),
                                ALU.subtract, ALU.mult).then_inc(s["ln"], 1)
        if e_act is not None:
            wait(e_act, s["ln"], t)
            wait(e_act, read, t - 2)
            e_act.activation(pairs[:, par, 0], raw[:, par], ACT.Copy).then_inc(s["x_hi"], 1)
        if e_dve is not None:
            wait(e_dve, s["x_hi"], t)
            e_dve.tensor_tensor(pairs[:, par, 1], raw[:, par], pairs[:, par, 0], ALU.subtract)\
                 .then_inc(s["x_lo"], 1)

    def expert_choice(tag, gate):
        norm_statistics(tag + "n")
        with ExitStack() as c:
            w1 = sb(c, "ew1", [P, 2, NE, DFF], F16)
            w2 = sb(c, "ew2", [P, 2, NE, FT, D], F16)
            idx16 = sb(c, "idx16", [P, NE * CAP], F16)
            gate_slot = sb(c, "gate_slot", [P, NE, 32], F32)
            tok_slot = sb(c, "tok_slot", [P, NE, 32], F32)
            b1T = sb(c, "eb1T", [P, NE * FT], F32)
            select_tokens(tag + "s", w1, w2, idx16, gate_slot, tok_slot, b1T)
            run_experts(tag + "e", gate, w1, w2, idx16, gate_slot, tok_slot, b1T)

    def select_tokens(tag, w1, w2, idx16, gate_slot, tok_slot, b1T):
        s = Sems(tag)
        with ExitStack() as c:
            lg = sb(c, "lg", [P, NE, N], F32)
            with ExitStack() as cl:
                gq32 = sb(cl, "gq32", [P, NE], F32)
                gq = sb(cl, "gq", [P, 2, NE], F16)
                xnf = sb(cl, "xnf", [P, 2, D], F32)
                xn = sb(cl, "xn", [P, 2, 2, D], F16)
                xT = sb(cl, "xTs", [P, 2, 2, P], F16)
                L = sb(cl, "L", [NE, NT, P], F32)
                psX = ps(cl, "psXs", [P, 2, 2, 512], F16)
                psL = ps(cl, "psL", [NE, 2, 512], F32)
                with nc.Block() as block:
                    @block.sync
                    def _(e):
                        with nc.allow_non_contiguous_dma("a small weight, transposed once"):
                            e.dma_start(gq32[:], I["L0_ffn_gate_query"].rearrange("e d -> d e")).then_inc(s["gq"], 16)
                        wait(e, s["l"], Step(None, 0, NT - 1))
                        for k in range(NE):
                            e.dma_start(lg[:, k, :], L[k:k + 1].rearrange("e t p -> e (t p)").rearrange(
                                "e (b n) -> e b n", n=N)).then_inc(s["lg"], 16)
                        e.wait_ge(s["lg"], 16 * NE)

                    @block.tensor
                    def _(e):
                        def body(j):
                            if (j + 1).inside(NT):
                                par = (j + 1).mod(2)
                                wait(e, s["x_lo"], j + 1)
                                wait(e, s["xT"], j - 1)
                                for hl in range(2):
                                    last = e.transpose(psX[:, par, hl, 0:P], xn[:, par, hl, :], ident16[:])
                                last.then_inc(s["X"], 1)
                            if j.inside(NT):
                                par = j.mod(2)
                                if j.reg is None:
                                    wait(e, s["gq_lo"], Step(None, 0, 0))
                                wait(e, s["xT"], j)
                                wait(e, s["l"], j - 2)
                                matmul3(e, psL[:, par, 0:P], (gq[:, 0, :], gq[:, 1, :]),
                                        (xT[:, par, 0, :], xT[:, par, 1, :])).then_inc(s["L"], 1)
                        pipeline(e, body, -1, NT, 2, NT - 4, 2)

                    @block.scalar
                    def _(e):
                        e.wait_ge(s["gq"], 16)
                        e.activation(gq[:, 0, :], gq32[:], ACT.Copy).then_inc(s["gq_hi"], 1)

                        def body(j):
                            if (j + 2).inside(NT):
                                queue_norm(None, e, s, j + 2, (j + 2).mod(2), xnf, xn, s["X"])
                            if j.inside(NT):
                                wait(e, s["L"], j)
                                e.activation(tile_of(j, L), psL[:, j.mod(2), 0:P], ACT.Copy).then_inc(s["l"], 1)
                        pipeline(e, body, -2, NT, 4, NT - 4, 2)

                    @block.vector
                    def _(e):
                        e.wait_ge(s["gq_hi"], 1)
                        e.tensor_tensor(gq[:, 1, :], gq32[:], gq[:, 0, :], ALU.subtract).then_inc(s["gq_lo"], 1)

                        def body(j):
                            if (j + 2).inside(NT):
                                queue_norm(e, None, s, j + 2, (j + 2).mod(2), xnf, xn, None)
                            if (j + 1).inside(NT):
                                par = (j + 1).mod(2)
                                wait(e, s["X"], j + 1)
                                wait(e, s["L"], j - 1)
                                e.tensor_copy(xT[:, par], psX[:, par, :, 0:P]).then_inc(s["xT"], 1)
                        pipeline(e, body, -2, NT, 4, NT - 4, 2)

            z = sb(c, "z", [P, NE, N], F32)
            m = sb(c, "m", [P, N], F32)
            total = sb(c, "total", [P, N], F32)
            temp = sb(c, "temp", [P, 3], F32)
            row = sb(c, "row", [P, N], F32)
            seen = sb(c, "seen", [P, 1], F32)
            v32 = sb(c, "v32", [P, CAP], F32)
            i32 = sb(c, "i32", [P, CAP], U32)
            vals = sb(c, "vals", [P, NE, CAP], F32)
            idx32 = sb(c, "idx32", [P, NE, CAP], F32)
            raw = sb(c, "rawe", [P, 2, 4, DFF], F32)
            psG = ps(c, "psG", [P, NE, 32], F32)
            psI = ps(c, "psI", [P, NE, 32], F32)
            w1v = I["L0_ffn_w1"].rearrange("e d f -> d e f")
            w2v = I["L0_ffn_w2"].rearrange("e (k p) d -> p e k d", p=P)
            with nc.Block() as block:
                @block.sync
                def _(e):
                    e.dma_start(temp[:, 0:1], I["L0_ffn_log_temp"].partition_broadcast(P)).then_inc(s["temp"], 16)
                    with nc.allow_non_contiguous_dma("a small bias, transposed once"):
                        e.dma_start(b1T[:], I["L0_ffn_b1"].rearrange("e (k p) -> p (e k)", p=P)).then_inc(s["b1"], 16)
                    for k in range(8):
                        if k >= 2:
                            e.wait_ge(s["w_lo"], k - 1)
                        g = 4 * (k % 4)
                        if k < 4:
                            e.dma_start(raw[:, k % 2], w1v[:, g:g + 4, :]).then_inc(s[f"raw{k % 2}"], 16)
                        else:
                            e.dma_start(raw[:, k % 2].rearrange("p e (k d) -> p e k d", d=D),
                                        w2v[:, g:g + 4]).then_inc(s[f"raw{k % 2}"], 16)
                    e.wait_ge(s["b1"], 16)

                @block.gpsimd
                def _(e):
                    for k in range(8):
                        g = 4 * (k % 4)
                        to = [w1[:, hl, g:g + 4, :] if k < 4 else
                              w2[:, hl, g:g + 4].rearrange("p e k d -> p e (k d)") for hl in range(2)]
                        e.wait_ge(s[f"raw{k % 2}"], 16 * (k // 2 + 1))
                        e.tensor_copy(to[0], raw[:, k % 2]).then_inc(s["w_hi"], 1)
                        e.wait_ge(s["w_hi"], k + 1)
                        e.tensor_tensor(to[1], raw[:, k % 2], to[0], ALU.subtract).then_inc(s["w_lo"], 1)

                views = []
                for axis, n in ((0, N), (1, NE)):
                    order = "p e n -> p n e" if axis == 0 else "p e n -> p e n"
                    views.append((axis, n, lg[:].rearrange(order), z[:].rearrange(order),
                                  m[:, 0:n].unsqueeze(2).broadcast_to([P, n, NE * N // n])))

                @block.scalar
                def _(e):
                    e.wait_ge(s["temp"], 16)
                    e.activation(temp[:, 1:2], temp[:, 0:1], ACT.Exp, bias=zero_col[:]).then_inc(s["et"], 1)
                    with e.Fori(0, ITERS) as i:
                        j = Step(i, 1, 0)
                        for axis, n, tv, zv, mb in views:
                            wait(e, s[f"z{axis}"], j)
                            e.activation(z[:], z[:], ACT.Exp, bias=zero_col[:]).then_inc(s[f"e{axis}"], 1)
                            wait(e, s[f"s{axis}"], j)
                            e.activation(total[:, 0:n], total[:, 0:n], ACT.Ln, bias=zero_col[:])\
                             .then_inc(s[f"l{axis}"], 1)
                    e.wait_ge(s["t1"], ITERS)
                    e.activation(lg[:], lg[:], ACT.Exp, bias=zero_col[:]).then_inc(s["aff"], 1)

                @block.vector
                def _(e):
                    e.wait_ge(s["et"], 1)
                    e.reciprocal(temp[:, 2:3], temp[:, 1:2]).then_inc(s["rt"], 1)
                    e.wait_ge(s["rt"], 1)
                    e.tensor_scalar(lg[:], lg[:], temp[:, 2:3], None, ALU.mult).then_inc(s["t"], 1)
                    e.wait_ge(s["t"], 1)
                    with e.Fori(0, ITERS) as i:
                        j = Step(i, 1, 0)
                        for axis, n, tv, zv, mb in views:
                            e.tensor_reduce(m[:, 0:n], tv, AX.X, ALU.max).then_inc(s[f"m{axis}"], 1)
                            wait(e, s[f"m{axis}"], j)
                            e.tensor_tensor(zv, tv, mb, ALU.subtract).then_inc(s[f"z{axis}"], 1)
                            wait(e, s[f"e{axis}"], j)
                            e.tensor_reduce(total[:, 0:n], zv, AX.X, ALU.add).then_inc(s[f"s{axis}"], 1)
                            wait(e, s[f"l{axis}"], j)
                            e.tensor_tensor(m[:, 0:n], m[:, 0:n], total[:, 0:n], ALU.add).then_inc(s[f"u{axis}"], 1)
                            wait(e, s[f"u{axis}"], j)
                            e.tensor_tensor(tv, tv, mb, ALU.subtract).then_inc(s[f"t{axis}"], 1)
                            wait(e, s[f"t{axis}"], j)
                    e.wait_ge(s["aff"], 1)
                    with e.Fori(0, NE) as i:
                        j = Step(i, 1, 0)
                        e.tensor_copy(row[:], tile_of(j, lg)).then_inc(s["row"], 1)
                        wait(e, s["row"], j)
                        e.tensor_copy(seen[:], row[:, 0:1])
                        for r in range(CAP // 8):
                            eight = slice(8 * r, 8 * r + 8)
                            e.max(v32[:, eight], row[:]).then_inc(s["top"], 1)
                            wait(e, s["top"], j, CAP // 8, r + 1 - CAP // 8)
                            e.tensor_copy(vals[:, bass.ds(j.value, 1), eight], v32[:, eight].unsqueeze(1))\
                             .then_inc(s["vals"], 1)
                            e.max_index(i32[:, eight], v32[:, eight], row[:]).then_inc(s["ti"], 1)
                            e.match_replace(row[:], v32[:, eight], row[:], -1.0).then_inc(s["rep"], 1)
                            wait(e, s["ti"], j, CAP // 8, r + 1 - CAP // 8)
                            wait(e, s["rep"], j, CAP // 8, r + 1 - CAP // 8)
                            e.tensor_copy(idx32[:, bass.ds(j.value, 1), eight], i32[:, eight].unsqueeze(1))\
                             .then_inc(s["idx"], 1)
                    e.wait_ge(s["idx"], NE * CAP // 8)
                    e.tensor_copy(idx16[:], idx32[:].rearrange("p e c -> p (e c)"))
                    e.wait_ge(s["slots"], 1)
                    e.tensor_copy(gate_slot[:], psG[:])
                    e.tensor_scalar(tok_slot[:], psI[:], block_of_p[:], None, ALU.add)

                @block.tensor
                def _(e):
                    e.wait_ge(s["vals"], NE * CAP // 8)
                    e.wait_ge(s["idx"], NE * CAP // 8)
                    for k in range(NE):
                        for q in range(4):
                            e.matmul(psG[32 * q:32 * q + 32, k, :], vals[:, k, :], ident32[:, q::4],
                                     start=True, stop=True)
                            last = e.matmul(psI[32 * q:32 * q + 32, k, :], idx32[:, k, :], ident32[:, q::4],
                                            start=True, stop=True)
                    last.then_inc(s["slots"], 1)
        s.close()

    def run_experts(tag, gate, w1, w2, idx16, gate_slot, tok_slot, b1T):
        s = Sems(tag)
        seeded = {n: Counter(s[n], 16) for n in (
            "sel", "g_hi", "g_lo", "gelu", "h_lo", "b2add", "eo_lo", "xadd", "g", "x_lo", "R", "E", "A", "put")}
        with nc.Block() as block:
            @block.sync
            def _(e):
                for n in seeded.values():
                    e.sem_inc(n.handle, n.start)
        GB = 16
        GT = GB * N // P
        ROWS = GB * CAP
        RT = ROWS // P
        NG = B // GB
        with ExitStack() as c:
            b2_rep = sb(c, "b2_rep", [P, NE, D], F32)
            xnf = sb(c, "xnfe", [P, 2, D], F32)
            xn = sb(c, "xne", [P, 2, 2, D], F16)
            pick = sb(c, "pick", [P, 2, P], F16)
            sel = sb(c, "sel", [P, 2, NE * CAP], F16)
            xg = sb(c, "xg", [P, 2, NE, ROWS], F16)
            g32 = sb(c, "g32", [P, FT, ROWS], F32)
            h = sb(c, "h", [P, 2, 2, FT, ROWS], F16)
            put = sb(c, "put", [P, 2, RT, 256], F16)
            eo32 = sb(c, "eo32", [P, RT, D], F32)
            eo = sb(c, "eo", [P, 2, 2, RT, D], F16)
            psH = ps(c, "psH", [P, 4, 512], F32)
            psE = ps(c, "psE", [P, RT, D], F32)
            psA = ps(c, "psA", [P, GT, D], F32)
            psR = ps(c, "psR", [P, 512], F32)
            sl = load = None

            def expert_steps(G, e, body, first, last, lo, hi, unroll):
                base = G * NE
                for k in range(first, lo):
                    body(k, None, Step(base, 1, k), k % 2)
                n = (hi - lo) // unroll
                with e.Fori(0, n) as i:
                    for u in range(unroll):
                        body(None, i * unroll + (lo + u), Step(base + i * unroll, 1, lo + u), u % 2)
                for k in range(lo + n * unroll, last):
                    body(k, None, Step(base, 1, k), k % 2)

            def at(k, reg, off=0):
                return (reg + off, True) if k is None else (k + off, 0 <= k + off < NE)

            with nc.Block() as block:
                @block.sync
                def _(e):
                    e.dma_start(b2_rep[:], I["L0_ffn_b2"].rearrange("e d -> (e d)").partition_broadcast(P)
                                .rearrange("p (e d) -> p e d", d=D)).then_inc(s["b2"], 16)

                @block.tensor
                def _(e):
                    with e.Fori(0, NG) as G:
                        for k in range(GT + 1):
                            if k < GT:
                                t = Step(G * GT, 1, k)
                                wait(e, s["pick"], t)
                                wait(e, seeded["sel"], t - 1)
                                e.matmul(psR[:], pick[:, k % 2, :], idx16[:], start=True, stop=True)\
                                 .then_inc(s["R"], 1)
                            if k >= 1:
                                t, par = Step(G * GT, 1, k - 1), (k - 1) % 2
                                wait(e, seeded["sel"], t)
                                wait(e, seeded["x_lo"], t)
                                wait(e, seeded["g_hi"], t - 1, 2)
                                wait(e, seeded["g_lo"], t - 1, 2)
                                for bp in range(2):
                                    for hl in range(2):
                                        q = slice(64 * bp, 64 * bp + 64)
                                        last = e.matmul(psH[:, 2 * bp + hl, :], xn[q, par, hl, :], sel[q, par, :],
                                                        start=True, stop=True)
                                last.then_inc(s["g"], 1)
                        wait(e, seeded["g_hi"], Step(G * GT, 1, GT - 1), 2)
                        wait(e, seeded["g_lo"], Step(G * GT, 1, GT - 1), 2)

                        def body(k, reg, j, par):
                            x1, ok = at(k, reg, 1)
                            if ok:
                                for ft in range(FT):
                                    wait(e, seeded["gelu"], j, FT, ft + 1 - FT)
                                    last = matmul3(e, psH[:, ft, :],
                                                   [w1[:, hl, bass.ds(x1, 1), ft * P:ft * P + P]
                                                    .rearrange("p o f -> p (o f)") for hl in range(2)],
                                                   [xg[:, hl, bass.ds(x1, 1), :].rearrange("p o f -> p (o f)")
                                                    for hl in range(2)])
                                    last.then_inc(s["H"], 1)
                            x0, ok = at(k, reg)
                            if ok:
                                wait(e, seeded["h_lo"], j, 2)
                                wait(e, seeded["b2add"], j - 1)
                                for r in range(RT):
                                    for ft in range(FT):
                                        last = matmul3(e, psE[:, r, :],
                                                       [h[:, par, hl, ft, r * P:r * P + P] for hl in range(2)],
                                                       [w2[:, hl, bass.ds(x0, 1), ft, :].rearrange("p o f -> p (o f)")
                                                        for hl in range(2)], ft == 0, ft == FT - 1)
                                last.then_inc(s["E"], 1)
                            x9, ok = at(k, reg, -1)
                            if ok:
                                wait(e, seeded["put"], j - 1, RT)
                                wait(e, seeded["eo_lo"], j - 1)
                                if k == 1:
                                    wait(e, seeded["xadd"], Step(G, 1, -1))
                                for r in range(RT):
                                    for q in range(2):
                                        for hl in range(2):
                                            a = 2 * r + q
                                            last = e.matmul(psA[:, a, :], put[:, 1 - par, r, q * P:q * P + P],
                                                            eo[:, 1 - par, hl, r, :],
                                                            start=k == 1 and a % 4 == 0 and hl == 0,
                                                            stop=k == NE and hl == 1, skip_group_check=True)
                                last.then_inc(s["A"], 1)
                        expert_steps(G, e, body, -1, NE + 1, 2, NE - 2, 2)

                def gathered(bp, hl, k):
                    a = (2 * k + bp) * CAP
                    return (xg[:, hl, :, a:a + CAP], psH[:, 2 * bp + hl, :].rearrange("p (e c) -> p e c", c=CAP))

                @block.scalar
                def _(e):
                    with e.Fori(0, NG) as G:
                        for k in range(GT + 1):
                            if k < GT:
                                t = Step(G * GT, 1, k)
                                queue_norm(None, e, s, t, k % 2, xnf, xn, seeded["g"])
                            if k >= 1:
                                t = Step(G * GT, 1, k - 1)
                                wait(e, seeded["g"], t)
                                for bp in range(2):
                                    to, frm = gathered(bp, 0, k - 1)
                                    e.activation(to, frm, ACT.Copy).then_inc(s["g_hi"], 1)

                        def body(k, reg, j, par):
                            x1, ok = at(k, reg, 1)
                            if ok:
                                for ft in range(FT):
                                    wait(e, s["H"], j + 1, FT, ft + 1 - FT)
                                    if ft % 2 == 0:
                                        wait(e, seeded["h_lo"], j, 2, ft // 2 - 1)
                                    e.activation(g32[:, ft, :], psH[:, ft, :], ACT.Gelu_apprx_tanh,
                                                 bias=b1T[:, bass.ds(x1 * FT + ft, 1)]).then_inc(s["gelu"], 1)
                                    if ft % 2 == 1:
                                        wait(e, seeded["gelu"], j + 1, FT, ft + 1 - FT)
                                        wait(e, seeded["E"], j - 1)
                                        e.activation(h[:, 1 - par, 0, ft - 1:ft + 1, :], g32[:, ft - 1:ft + 1, :],
                                                     ACT.Copy).then_inc(s["h_hi"], 1)
                            x0, ok = at(k, reg)
                            if ok:
                                wait(e, s["gated"], j)
                                wait(e, seeded["A"], j - 2)
                                e.activation(eo[:, par, 0], eo32[:], ACT.Copy).then_inc(s["eo_hi"], 1)
                        expert_steps(G, e, body, -1, NE, 2, NE - 2, 2)

                @block.gpsimd
                def _(e):
                    with e.Fori(0, NG) as G:
                        def body(k, reg, j, par):
                            x0, ok = at(k, reg)
                            if ok:
                                wait(e, seeded["b2add"], j)
                                g4 = gate_slot[:, bass.ds(x0, 1), bass.ds(G * RT, RT)].rearrange("p o r -> p (o r)")
                                e.tensor_tensor(eo32[:], eo32[:], g4.unsqueeze(2).broadcast_to([P, RT, D]),
                                                ALU.mult).then_inc(s["gated"], 1)
                        expert_steps(G, e, body, 0, NE, 2, NE - 2, 2)

                @block.vector
                def _(e):
                    e.wait_ge(s["b2"], 16)
                    with e.Fori(0, NG) as G:
                        for k in range(GT + 1):
                            if k < GT:
                                t = Step(G * GT, 1, k)
                                wait(e, seeded["R"], t - 2)
                                e.tensor_copy(pick[:, k % 2].rearrange("p (b n) -> p b n", n=N),
                                              ident16[:, bass.ds(t.times(2), 2)].unsqueeze(2)
                                              .broadcast_to([P, 2, N])).then_inc(s["pick"], 1)
                                queue_norm(e, None, s, t, k % 2, xnf, xn, None, seeded["x_lo"])
                                wait(e, seeded["R"], t)
                                wait(e, seeded["g"], t - 2)
                                e.tensor_scalar(sel[:, k % 2, :], psR[:], token_of_p[:], None, ALU.is_equal)\
                                 .then_inc(s["sel"], 1)
                            if k >= 1:
                                t = Step(G * GT, 1, k - 1)
                                wait(e, seeded["g"], t)
                                for bp in range(2):
                                    to, frm = gathered(bp, 1, k - 1)
                                    e.tensor_copy(to, frm).then_inc(s["g_lo"], 1)

                        def body(k, reg, j, par):
                            x1, ok = at(k, reg, 1)
                            if ok:
                                for q in range(2):
                                    wait(e, s["h_hi"], j + 1, 2, q - 1)
                                    wait(e, seeded["E"], j - 1)
                                    e.tensor_tensor(h[:, 1 - par, 1, 2 * q:2 * q + 2, :], g32[:, 2 * q:2 * q + 2, :],
                                                    h[:, 1 - par, 0, 2 * q:2 * q + 2, :], ALU.subtract)\
                                     .then_inc(s["h_lo"], 1)
                            x0, ok = at(k, reg)
                            if ok:
                                wait(e, seeded["A"], j - 2)
                                for r in range(RT):
                                    e.tensor_scalar(put[:, par, r, :], iota256[:],
                                                    tok_slot[:, bass.ds(x0, 1), bass.ds(G * RT + r, 1)]
                                                    .rearrange("p o r -> p (o r)"),
                                                    None, ALU.is_equal).then_inc(s["put"], 1)
                                wait(e, seeded["E"], j)
                                wait(e, seeded["eo_lo"], j - 1)
                                e.tensor_tensor(eo32[:], psE[:], b2_rep[:, bass.ds(x0, 1), :]
                                                .broadcast_to([P, RT, D]), ALU.add).then_inc(s["b2add"], 1)
                                wait(e, s["eo_hi"], j)
                                e.tensor_tensor(eo[:, par, 1], eo32[:], eo[:, par, 0], ALU.subtract)\
                                 .then_inc(s["eo_lo"], 1)
                        expert_steps(G, e, body, -1, NE, 2, NE - 2, 2)
                        wait(e, seeded["A"], Step(G * NE, 1, NE - 1))
                        for q in range(2):
                            xs = x[:, bass.ds(G * GT + 4 * q, 4), :]
                            last = e.scalar_tensor_tensor(xs, psA[:, 4 * q:4 * q + 4, :], gate, xs, ALU.mult, ALU.add)
                        last.then_inc(s["xadd"], 1)
        s.close()

    def routed(tag, so):
        norm_statistics(tag + "n")
        s = Sems(tag)
        with ExitStack() as c:
            w1 = sb(c, "rw1", [P, 2, NE1, D], F16)
            w2 = sb(c, "rw2", [P, 2, NE1, D], F16)
            b1s = sb(c, "b1s", [P, B, TOPK], F32)
            b2s = sb(c, "b2s", [P, B], F32)
            erow = sb(c, "erow", [1, B * TOPK], U32)
            with ExitStack() as cr:
                raw = sb(cr, "rraw", [P, 2, NE1, D], F32)
                wr32 = sb(cr, "wr32", [P, NE1], F32)
                wr = sb(cr, "wr", [P, 2, NE1], F16)
                br = sb(cr, "br", [P, NE1], F32)
                b12 = sb(cr, "b12", [NE1, 2, D], F32)
                x0 = sb(cr, "x0", [P, D], F32)
                st = sb(cr, "st", [P, 6], F32)
                mv = sb(cr, "mv", [P, 2], F32)
                sd = sb(cr, "sd", [P, 2], F32)
                xn0 = sb(cr, "xn0", [P, D], F32)
                xh0 = sb(cr, "xh0", [P, 2, D], F16)
                xT0 = sb(cr, "xT0", [P, 2, P], F16)
                sc = sb(cr, "sc", [P, NE1], F32)
                best = sb(cr, "best", [P, 8], F32)
                bi = sb(cr, "bi", [P, 8], U32)
                bf = sb(cr, "bf", [P, 8], F32)
                oh = sb(cr, "oh", [P, TOPK, NE1], F32)
                i8 = sb(cr, "i8", [P, NE1], F32)
                ohT = sb(cr, "ohT", [NE1, TOPK, B], F32)
                psX0 = ps(cr, "psX0", [P, 2, P], F16)
                psC = ps(cr, "psC", [P, 512], F32)
                psB = ps(cr, "psB", [P, 512], F32)
                dram = nc.dram_tensor("choices", [B, TOPK], U32)
                with nc.Block() as block:
                    @block.sync
                    def _(e):
                        load_all(e, s["w"], [(raw[:, 0], I["L1_ffn_W1"].rearrange("e d f -> d e f")),
                                             (raw[:, 1], I["L1_ffn_W2"].rearrange("e d f -> d e f"))])
                        load_all(e, s["c"], [(wr32[:], I["L1_ffn_Wr"]), (br[:], I["L1_ffn_br"].partition_broadcast(P)),
                                             (b12[:, 0], I["L1_ffn_b1"]), (b12[:, 1], I["L1_ffn_b2"])])
                        load_all(e, s["x0"], [(x0[bp::2, :], x[64 * bp:64 * bp + 1, :, :]) for bp in range(2)])
                        e.wait_ge(s["bi"], 1)
                        e.dma_start(dram.ap(), bi[:, 0:TOPK]).then_inc(s["choices"], 16)
                        e.wait_ge(s["choices"], 16)
                        e.dma_start(erow[:], dram.ap().rearrange("b k -> (b k)").unsqueeze(0)).then_inc(s["erow"], 16)
                        e.wait_ge(s["erow"], 16)

                    @block.gpsimd
                    def _(e):
                        e.iota(i8[:], [[1, NE1]], base=0, channel_multiplier=0,
                               allow_small_or_imprecise_dtypes=True).then_inc(s["i8"], 1)

                    parts = [(wr32[:], wr[:, 0], wr[:, 1]), (xn0[:], xh0[:, 0], xh0[:, 1]),
                             (raw[:, 0], w1[:, 0], w1[:, 1]), (raw[:, 1], w2[:, 0], w2[:, 1])]

                    @block.scalar
                    def _(e):
                        e.wait_ge(s["var"], 1)
                        e.activation(sd[:, 0:1], mv[:, 1:2], ACT.Sqrt, bias=eps_col[:]).then_inc(s["sd"], 1)
                        e.wait_ge(s["c"], 64)
                        split(e, None, s, 0, *parts[0])
                        e.wait_ge(s["ln0"], 1)
                        split(e, None, s, 1, *parts[1])
                        e.wait_ge(s["w"], 32)
                        split(e, None, s, 2, *parts[2])
                        split(e, None, s, 3, *parts[3])

                    @block.vector
                    def _(e):
                        e.wait_ge(s["x0"], 32)
                        e.bn_stats(st[:], x0[:]).then_inc(s["st"], 1)
                        e.wait_ge(s["st"], 1)
                        e.bn_aggr(mv[:], st[:]).then_inc(s["var"], 1)
                        e.wait_ge(s["sd"], 1)
                        e.reciprocal(sd[:, 1:2], sd[:, 0:1]).then_inc(s["rs"], 1)
                        e.wait_ge(s["rs"], 1)
                        e.tensor_scalar(xn0[:], x0[:], mv[:, 0:1], sd[:, 1:2], ALU.subtract, ALU.mult)\
                         .then_inc(s["ln0"], 1)
                        split(None, e, s, 0, *parts[0])
                        split(None, e, s, 1, *parts[1])
                        e.wait_ge(s["X0"], 1)
                        e.tensor_copy(xT0[:], psX0[:]).then_inc(s["xT0"], 1)
                        e.wait_ge(s["C"], 1)
                        e.tensor_tensor(sc[:], psC[:, 0:NE1], br[:], ALU.add).then_inc(s["sc"], 1)
                        e.wait_ge(s["sc"], 1)
                        e.max(best[:], sc[:]).then_inc(s["best"], 1)
                        e.wait_ge(s["best"], 1)
                        e.max_index(bi[:], best[:], sc[:]).then_inc(s["bi"], 1)
                        e.wait_ge(s["bi"], 1)
                        e.tensor_copy(bf[:], bi[:]).then_inc(s["bf"], 1)
                        e.wait_ge(s["bf"], 1)
                        e.wait_ge(s["i8"], 1)
                        for k in range(TOPK):
                            e.tensor_scalar(oh[:, k, :], i8[:], bf[:, k:k + 1], None, ALU.is_equal)\
                             .then_inc(s["oh"], 1)
                        e.wait_ge(s["ohP"], 1)
                        e.tensor_copy(ohT[:], psB[0:NE1, 0:TOPK * B].rearrange("p (k b) -> p k b", b=B))\
                         .then_inc(s["ohT"], 1)
                        e.wait_ge(s["bP"], 1)
                        e.tensor_copy(b1s[:].rearrange("p b k -> p k b"),
                                      psC[:, 0:TOPK * B].rearrange("p (k b) -> p k b", b=B))
                        e.tensor_copy(b2s[:], psC[:, TOPK * B:TOPK * B + B])
                        split(None, e, s, 2, *parts[2])
                        split(None, e, s, 3, *parts[3])

                    @block.tensor
                    def _(e):
                        e.wait_ge(s["w_lo"], 2)
                        for hl in range(2):
                            last = e.transpose(psX0[:, hl, :], xh0[:, hl, :], ident16[:])
                        last.then_inc(s["X0"], 1)
                        e.wait_ge(s["xT0"], 1)
                        matmul3(e, psC[:, 0:NE1], (xT0[:, 0], xT0[:, 1]), (wr[:, 0], wr[:, 1])).then_inc(s["C"], 1)
                        e.wait_ge(s["oh"], TOPK)
                        for k in range(TOPK):
                            last = e.matmul(psB[0:NE1, k * B:k * B + B], oh[:, k, :], ident32[:], start=True, stop=True)
                        last.then_inc(s["ohP"], 1)
                        e.wait_ge(s["ohT"], 1)
                        e.matmul(psC[:, 0:TOPK * B], b12[:, 0, :], ohT[:].rearrange("p k b -> p (k b)"),
                                 start=True, stop=True)
                        for k in range(TOPK):
                            last = e.matmul(psC[:, TOPK * B:TOPK * B + B], b12[:, 1, :], ohT[:, k, :],
                                            start=k == 0, stop=k == TOPK - 1)
                        last.then_inc(s["bP"], 1)

            xnf = sb(c, "xnfr", [P, 2, D], F32)
            xn = sb(c, "xnr", [P, 2, 2, D], F16)
            xT = sb(c, "xTr", [P, 2, 2, P], F16)
            a32 = sb(c, "a32", [P, 4, N], F32)
            g32 = sb(c, "g32r", [P, 4, N], F32)
            h = sb(c, "hr", [P, 2, 2, 4, N], F16)
            y32 = sb(c, "y32", [P, 2, N], F32)
            psX = ps(c, "psXr", [P, 2, P], F16)
            psH = ps(c, "psHr", [P, 4, N], F32)
            psO = ps(c, "psOr", [P, 2, N], F32)
            psZ = ps(c, "psZr", [P, P], F32)
            with nc.Block() as block:
                @block.tensor
                def _(e):
                    def experts(t):
                        return [e.value_load(erow[0:1, bass.ds(t.times(4, q), 1)], min_val=0, max_val=NE1 - 1)
                                for q in range(4)]

                    def body(j):
                        if (j + 1).inside(NT):
                            par = (j + 1).mod(2)
                            wait(e, s["x_lo"], j + 1)
                            wait(e, s["xT"], j)
                            for hl in range(2):
                                last = e.transpose(psX[:, hl, :], xn[:, par, hl, :], ident16[:])
                            last.then_inc(s["X"], 1)
                        if j.inside(NT):
                            par = j.mod(2)
                            ids = experts(j)
                            wait(e, s["xT"], j)
                            wait(e, s["bias"], j - 1)
                            for q in range(4):
                                b = q // 2
                                last = matmul3(e, psH[:, q, :],
                                               [w1[:, hl, bass.ds(ids[q], 1), :].rearrange("p o f -> p (o f)")
                                                for hl in range(2)],
                                               [xT[:, par, hl, N * b:N * b + N] for hl in range(2)])
                            last.then_inc(s["H"], 1)
                        if (j - 1).inside(NT):
                            par = (j - 1).mod(2)
                            ids = experts(j - 1)
                            wait(e, s["h_lo"], j - 1)
                            wait(e, s["y"], j - 2)
                            for q in range(4):
                                b, k = q // 2, q % 2
                                last = matmul3(e, psO[:, b, :],
                                               [w2[:, hl, bass.ds(ids[q], 1), :].rearrange("p o f -> p (o f)")
                                                for hl in range(2)],
                                               [h[:, par, hl, q, :] for hl in range(2)], k == 0, k == TOPK - 1)
                            last.then_inc(s["O"], 1)
                            wait(e, s["y"], j - 1)
                            wait(e, s["res"], j - 2)
                            e.transpose(psZ[:], y32[:].rearrange("p b n -> p (b n)"), ident32[:]).then_inc(s["Z"], 1)
                    pipeline(e, body, -1, NT + 1, 2, NT - 4, 2)

                @block.scalar
                def _(e):
                    def body(j):
                        if (j + 2).inside(NT):
                            queue_norm(None, e, s, j + 2, (j + 2).mod(2), xnf, xn, s["X"])
                        if j.inside(NT):
                            par = j.mod(2)
                            wait(e, s["bias"], j)
                            wait(e, s["h_lo"], j - 1)
                            e.activation(g32[:], a32[:], ACT.Gelu, bias=zero_col[:]).then_inc(s["gelu"], 1)
                            wait(e, s["gelu"], j)
                            wait(e, s["O"], j - 2)
                            e.activation(h[:, par, 0], g32[:], ACT.Copy).then_inc(s["h_hi"], 1)
                    pipeline(e, body, -2, NT, 4, NT - 4, 2)

                @block.vector
                def _(e):
                    def body(j):
                        if (j + 2).inside(NT):
                            queue_norm(e, None, s, j + 2, (j + 2).mod(2), xnf, xn, None)
                        if (j + 1).inside(NT):
                            wait(e, s["X"], j + 1)
                            e.tensor_copy(xT[:, (j + 1).mod(2)], psX[:]).then_inc(s["xT"], 1)
                        if j.inside(NT):
                            par = j.mod(2)
                            wait(e, s["H"], j)
                            wait(e, s["gelu"], j - 1)
                            bias = b1s[:, bass.ds(j.times(2), 2), :].rearrange("p b k -> p (b k)")
                            e.tensor_tensor(a32[:], psH[:], bias.unsqueeze(2).broadcast_to([P, 4, N]), ALU.add)\
                             .then_inc(s["bias"], 1)
                            wait(e, s["h_hi"], j)
                            e.tensor_tensor(h[:, par, 1], g32[:], h[:, par, 0], ALU.subtract).then_inc(s["h_lo"], 1)
                        if (j - 1).inside(NT):
                            t = j - 1
                            wait(e, s["O"], t)
                            wait(e, s["Z"], t - 1)
                            e.tensor_tensor(y32[:], psO[:], b2s[:, bass.ds(t.times(2), 2)].unsqueeze(2)
                                            .broadcast_to([P, 2, N]), ALU.add).then_inc(s["y"], 1)
                            wait(e, s["Z"], t)
                            e.scalar_tensor_tensor(tile_of(t, x), psZ[:], half_g[:], tile_of(t, x),
                                                   ALU.mult, ALU.add).then_inc(s["res"], 1)
                    pipeline(e, body, -2, NT + 1, 4, NT - 4, 2)

                @block.sync
                def _(e):
                    for k in range(0, NT, 8):
                        e.wait_ge(s["res"], k + 8)
                        e.dma_start(ov[:, k:k + 8, :], x[:, k:k + 8, :]).then_inc(so, 16)
                    e.wait_ge(so, 16 * NT // 8)
        s.close()

    S0.close()
    attention("a0", 1, I["L0_xattn_Wq"], I["L0_xattn_Wk"], I["L0_xattn_Wv"], I["L0_xattn_Wo"],
              I["L0_xattn_bo"], tanh_g[:, 0:1])
    expert_choice("m", tanh_g[:, 2:3])
    attention("a1", 2, I["L1_xattn_Wq"], I["L1_xattn_Wk"], I["L1_xattn_Wv"], I["L1_xattn_Wo"],
              I["L1_xattn_bo"], tanh_g[:, 1:2])
    routed("r", sem("out"))


_OUTS = [((B, N, D), "float32")]


def kernel(**inputs):
    import numpy as _np
    import concourse.bacc as _bacc
    from concourse import mybir as _mybir
    from concourse.bass_utils import run_bass_kernel_spmd as _run

    nc = _bacc.Bacc("TRN2", target_bir_lowering=False, num_devices=1)
    arrays, args = {}, {}
    for name, a in inputs.items():
        a = _np.ascontiguousarray(a)
        if a.ndim == 0:
            a = a.reshape(1)
        arrays[f"in_{name}_dram"] = a
        args[name] = nc.dram_tensor(f"in_{name}_dram", a.shape, _mybir.dt.from_np(a.dtype), kind="ExternalInput").ap()
    shape, dtype = _OUTS[0]
    o = nc.dram_tensor("out_0_dram", shape, _mybir.dt.from_np(_np.dtype(dtype)), kind="ExternalOutput").ap()
    program(nc, args, o)
    r = _run(nc, [arrays], core_ids=[0])
    return r.results[0]["out_0_dram"]
```

```python
from contextlib import ExitStack

import concourse.bass as bass
from concourse import mybir

F32 = mybir.dt.float32
F16 = mybir.dt.float16
U32 = mybir.dt.uint32
I32 = mybir.dt.int32
ALU = mybir.AluOpType
ACT = mybir.ActivationFunctionType
AX = mybir.AxisListType

P = 128
B, N, D, DC = 128, 64, 128, 96
NT = B * N // P
DH = 64
NE, CAP, DFF = 16, 32, 512
FT = DFF // P
ITERS = 6
NE1, TOPK = 8, 2
EPS = 1e-5


class Step:

    def __init__(self, reg, mult, off):
        self.reg, self.mult, self.off = reg, mult, off

    def __add__(self, k):
        return Step(self.reg, self.mult, self.off + k)

    def __sub__(self, k):
        return self + (-k)

    def div(self, g):
        return Step(self.reg, self.mult // g, self.off // g)

    def mod(self, m):
        assert self.reg is None or self.mult % m == 0
        return self.off % m

    def inside(self, n):
        return True if self.reg is not None else 0 <= self.off < n

    def upto(self, n):
        return self if self.reg is not None or self.off <= n else Step(None, 0, n)

    def times(self, k, add=0):
        if self.reg is None:
            return self.off * k + add
        return self.reg * (self.mult * k) + (self.off * k + add)

    @property
    def value(self):
        return self.times(1)


class Counter:

    def __init__(self, handle, start):
        self.handle, self.start = handle, start


def wait(eng, sem, step, per=1, add=0):
    if isinstance(sem, Counter):
        sem, add = sem.handle, add + sem.start
    if step.reg is None and step.times(per, per + add) <= 0:
        return
    eng.wait_ge(sem, step.times(per, per + add))


def pipeline(eng, body, first, last, lo, hi, unroll):
    a = -(-lo // unroll) * unroll
    n = max(0, (hi - a) // unroll)
    b = a + n * unroll
    for j in range(first, a):
        body(Step(None, 0, j))
    if n:
        with eng.Fori(0, n) as i:
            for u in range(unroll):
                body(Step(i, unroll, a + u))
    for j in range(b, last):
        body(Step(None, 0, j))


def program(nc, I, out):
    with ExitStack() as whole:
        _build(nc, whole, I, out)


def _build(nc, whole, I, out):
    made = {}

    def sb(ctx, name, shape, dt):
        made[name] = made.get(name, 0) + 1
        return ctx.enter_context(nc.sbuf_tensor(f"{name}_{made[name]}", shape, dt))

    def ps(ctx, name, shape, dt):
        made[name] = made.get(name, 0) + 1
        return ctx.enter_context(nc.psum_tensor(f"{name}_{made[name]}", shape, dt))

    def sem(name):
        return nc.alloc_semaphore(name=name)

    class Sems:

        def __init__(self, stage):
            self.stage, self.all = stage, {}

        def __getitem__(self, name):
            if name not in self.all:
                self.all[name] = sem(f"{self.stage}_{name}")
            return self.all[name]

        def close(self):
            nc.clear_and_free_semaphores(list(self.all.values()))
            nc.all_engine_barrier()

    def load_all(eng, s, pairs):
        for to, frm in pairs:
            eng.dma_start(to, frm).then_inc(s, 16)
        return 16 * len(pairs)

    x = sb(whole, "x", [P, NT, D], F32)
    ident16 = sb(whole, "ident16", [P, P], F16)
    ident32 = sb(whole, "ident32", [P, P], F32)
    token_of_p = sb(whole, "token_of_p", [P, 1], F32)
    block_of_p = sb(whole, "block_of_p", [P, 1], F32)
    iota256 = sb(whole, "iota256", [P, 256], F16)
    eps_col = sb(whole, "eps_col", [P, 1], F32)
    zero_col = sb(whole, "zero_col", [P, 1], F32)
    gates = sb(whole, "gates", [P, 4], F32)
    tanh_g = sb(whole, "tanh_g", [P, 4], F32)
    half_g = sb(whole, "half_g", [P, 1], F32)
    stats = sb(whole, "stats", [P, NT, 6], F32)
    mean = sb(whole, "mean", [P, NT], F32)
    rstd = sb(whole, "rstd", [P, NT], F32)
    lnt = sb(whole, "lnt", [P, 3, NT], F32)

    xv = I["x"].rearrange("b n d -> (b n) d").rearrange("(t p) d -> p t d", p=P)
    cv = I["ctx_768"].rearrange("b n d -> (b n) d").rearrange("(t p) d -> p t d", p=P)
    ov = out.rearrange("b n d -> (b n) d").rearrange("(t p) d -> p t d", p=P)

    S0 = Sems("init")
    with nc.Block() as block:
        @block.sync
        def _(e):
            n = load_all(e, S0["x"], [(x[:, c:c + 16, :], xv[:, c:c + 16, :]) for c in range(0, NT, 16)])
            e.wait_ge(S0["x"], n)

        @block.scalar
        def _(e):
            n = load_all(e, S0["gates"], [(gates[:, 0:2], I["g_xattn"].partition_broadcast(P)),
                                        (gates[:, 2:4], I["g_ffn"].partition_broadcast(P))])
            e.wait_ge(S0["gates"], n)
            e.wait_ge(S0["zero"], 1)
            e.activation(tanh_g[:], gates[:], ACT.Tanh, bias=zero_col[:]).then_inc(S0["tanh"], 1)
            e.wait_ge(S0["tanh"], 1)
            e.activation(half_g[:], tanh_g[:, 3:4], ACT.Copy, scale=1.0 / TOPK)

        @block.vector
        def _(e):
            e.memset(zero_col[:], 0.0).then_inc(S0["zero"], 1)
            e.memset(eps_col[:], EPS)
            for q in range(4):
                e.memset(block_of_p[32 * q:32 * q + 32, :], float(N * q))
            e.wait_ge(S0["iota"], 1)
            e.tensor_scalar(token_of_p[64:P, :], token_of_p[64:P, :], -float(N), None, ALU.add)

        @block.gpsimd
        def _(e):
            e.memset(ident16[:], 0.0).then_inc(S0["id"], 1)
            e.memset(ident32[:], 0.0).then_inc(S0["id"], 1)
            e.wait_ge(S0["id"], 2)
            for m in (ident16, ident32):
                e.affine_select(out=m[:], in_=m[:], compare_op=ALU.not_equal, fill=1.0, base=0,
                                pattern=[[-1, P]], channel_multiplier=1)
            e.iota(token_of_p[:], [[0, 1]], base=0, channel_multiplier=1,
                   allow_small_or_imprecise_dtypes=True).then_inc(S0["iota"], 1)
            e.iota(iota256[:], [[1, 256]], base=0, channel_multiplier=0,
                   allow_small_or_imprecise_dtypes=True)

    def split(e_act, e_dve, s, k, raw, hi, lo):
        if e_act is not None:
            e_act.activation(hi, raw, ACT.Copy).then_inc(s["w_hi"], 1)
        if e_dve is not None:
            e_dve.wait_ge(s["w_hi"], k + 1)
            e_dve.tensor_tensor(lo, raw, hi, ALU.subtract).then_inc(s["w_lo"], 1)

    def products(pairs):
        (lh, ll), (rh, rl) = pairs
        return [(lh, rh), (lh, rl), (ll, rh)]

    def matmul3(e, to, left, right, start=True, stop=True):
        three = products((left, right))
        for n, (a, b) in enumerate(three):
            last = e.matmul(to, a, b, start=start and n == 0, stop=stop and n == 2)
        return last

    def norm_statistics(tag):
        s = Sems(tag)
        with nc.Block() as block:
            @block.vector
            def _(e):
                with e.Fori(0, NT // 4) as i:
                    for u in range(4):
                        e.bn_stats(stats[:, bass.ds(i * 4 + u, 1), :].rearrange("p o s -> p (o s)"),
                                   x[:, bass.ds(i * 4 + u, 1), :].rearrange("p o d -> p (o d)"))\
                         .then_inc(s["bn"], 1)
                e.wait_ge(s["bn"], NT)
                me, mo = stats[:, :, 1], stats[:, :, 4]
                e.tensor_tensor(lnt[:, 0, :], me, mo, ALU.subtract).then_inc(s["v"], 1)
                e.tensor_tensor(lnt[:, 1, :], stats[:, :, 2], stats[:, :, 5], ALU.add).then_inc(s["v"], 1)
                e.tensor_tensor(lnt[:, 2, :], me, mo, ALU.add).then_inc(s["v"], 1)
                e.wait_ge(s["v"], 3)
                e.tensor_scalar(mean[:], lnt[:, 2, :], 0.5, None, ALU.mult)
                e.scalar_tensor_tensor(lnt[:, 0, :], lnt[:, 0, :], D / 4.0, lnt[:, 0, :],
                                       ALU.mult, ALU.mult).then_inc(s["v"], 1)
                e.wait_ge(s["v"], 4)
                e.tensor_tensor(lnt[:, 1, :], lnt[:, 1, :], lnt[:, 0, :], ALU.add).then_inc(s["v"], 1)
                e.wait_ge(s["sqrt"], 1)
                e.reciprocal(rstd[:], lnt[:, 2, :])

            @block.scalar
            def _(e):
                e.wait_ge(s["v"], 5)
                e.activation(lnt[:, 2, :], lnt[:, 1, :], ACT.Sqrt, bias=eps_col[:], scale=1.0 / D)\
                 .then_inc(s["sqrt"], 1)
        s.close()

    def tile_of(t, tensor):
        return tensor[:, bass.ds(t.value, 1), :].rearrange("p o d -> p (o d)")

    def column_of(t, tensor):
        return tensor[:, bass.ds(t.value, 1)]

    def attention(tag, G, Wq, Wk, Wv, Wo, bo, gate):
        U = NT * G
        INNER = 512 * G
        norm_statistics(tag + "n")
        s = Sems(tag)
        with ExitStack() as c:
            ctx32 = sb(c, "ctx32", [P, NT, DC], F32)
            raw = sb(c, "raw", [P, 4, INNER], F32)
            wq = sb(c, "wq", [P, 2, INNER], F16)
            wk = sb(c, "wk", [DC, 2, INNER], F16)
            wv = sb(c, "wv", [DC, 2, INNER], F16)
            wo = sb(c, "wo", [P, 2, 4 * G, D], F16)
            bo_rep = sb(c, "bo_rep", [P, D], F32)
            xcf = sb(c, "xcf", [P, 2, D + DC], F32)
            xc = sb(c, "xc", [P, 2, 2, D + DC], F16)
            xT = sb(c, "xT", [P, 2, 2, P], F16)
            cT = sb(c, "cT", [DC, 2, 2, P], F16)
            qT = sb(c, "qT", [P, 4, P], F32)
            kT = sb(c, "kT", [P, 4, P], F32)
            vB = sb(c, "vB", [P, 2, 2, 8, P], F16)
            E = sb(c, "E", [P, 2, 4, 2, N], F32)
            Ph = sb(c, "Ph", [P, 2, 2, 4, P], F16)
            PT = sb(c, "PT", [P, 2, 4, P], F16)
            top = sb(c, "top", [P, 2, 4], F32)
            den = sb(c, "den", [P, 2, 8], F32)
            rden = sb(c, "rden", [P, 2, 8], F32)
            oT = sb(c, "oT", [P, G, 2, 4, P], F16)
            psQ = ps(c, "psQ", [P, 4, P], F32)
            psK = ps(c, "psK", [P, 4, P], F32)
            psV = ps(c, "psV", [P, 8, DH], F32)
            psS = ps(c, "psS", [P, 2, 512], F32)
            psT = ps(c, "psT", [P, 2, 4, P], F16)
            psO = ps(c, "psO", [P, 4, P], F32)
            psXY = ps(c, "psXY", [P, 512], F32)
            psX = psXY[:, 0:256].bitcast(F16).rearrange("p (k t) -> p k t", k=4)
            psY = psXY[:, 256:384]

            with nc.Block() as block:
                weights = [(raw[:, 0, :], Wq), (raw[0:DC, 1, :], Wk), (raw[0:DC, 2, :], Wv),
                           (raw[:, 3, :].rearrange("p (k d) -> p k d", d=D), Wo.rearrange("(k p) d -> p k d", p=P))]
                parts = [(raw[:, 0, :], wq[:, 0, :], wq[:, 1, :]),
                         (raw[0:DC, 1, :], wk[:, 0, :], wk[:, 1, :]),
                         (raw[0:DC, 2, :], wv[:, 0, :], wv[:, 1, :]),
                         (raw[:, 3, :], wo[:, 0].rearrange("p k d -> p (k d)"), wo[:, 1].rearrange("p k d -> p (k d)"))]

                @block.sync
                def _(e):
                    load_all(e, s["w"], weights + [(bo_rep[:], bo.partition_broadcast(P))])
                    n = load_all(e, s["ctx"], [(ctx32[:, k:k + 16, :], cv[:, k:k + 16, :]) for k in range(0, NT, 16)])
                    e.wait_ge(s["ctx"], n)

                @block.scalar
                def _(e):
                    e.wait_ge(s["w"], 16 * 5)
                    for k, p in enumerate(parts):
                        split(e, None, s, k, *p)

                @block.vector
                def _(e):
                    e.memset(vB[:].rearrange("p a b c d -> p (a b c d)").bitcast(U32), 0)
                    e.wait_ge(s["w"], 16 * 5)
                    e.tensor_scalar(bo_rep[:], bo_rep[:], gate, None, ALU.mult)
                    for k, p in enumerate(parts):
                        split(None, e, s, k, *p)

            def half(hp):
                return slice(64 * hp, 64 * hp + 64)

            def vblock(hl, par, hp):
                return vB[half(hp), par, hl, :, half(hp)]

            with nc.Block() as block:
                @block.tensor
                def _(e):
                    def body(j):
                        if j.inside(U):
                            t = j.div(G)
                            g, tp = j.mod(2 * G) % G, j.mod(2 * G) // G
                            wait(e, s["q"], j)
                            wait(e, s["k"], j)
                            wait(e, s["sub"], j - 1)
                            wait(e, s["xT"], t)
                            wait(e, s["v_lo"], j - 1, 2)
                            for hp in range(2):
                                for b in range(2):
                                    w = [wv[:, hl, 512 * g:512 * g + 512].rearrange(
                                        "p (k h d) -> p k h d", h=2, d=DH)[:, :, hp, :] for hl in range(2)]
                                    last = matmul3(e, psV[half(hp), 4 * b:4 * b + 4, :],
                                                   (cT[:, tp, 0, half(b)], cT[:, tp, 1, half(b)]), w)
                            last.then_inc(s["V"], 1)
                            for hp in range(2):
                                for pair in range(4):
                                    for b in range(2):
                                        last = e.matmul(psS[half(b), hp, 64 * pair:64 * pair + 64],
                                                        qT[half(hp), pair, half(b)], kT[half(hp), pair, half(b)],
                                                        start=True, stop=True)
                            last.then_inc(s["S"], 1)
                        if (j - 2).inside(U) and (j - 2).mod(2 * G) % G == G - 1:
                            t = (j - 2).div(G)
                            wait(e, s["o_lo"], j - 2)
                            wait(e, s["xT"], (t + 4 - G).upto(NT - 1))
                            for g in range(G):
                                for pair in range(4):
                                    last = matmul3(e, psY, (oT[:, g, 0, pair, :], oT[:, g, 1, pair, :]),
                                                   (wo[:, 0, 4 * g + pair, :], wo[:, 1, 4 * g + pair, :]),
                                                   g == 0 and pair == 0, g == G - 1 and pair == 3)
                            last.then_inc(s["Y"], 1)

                        def project(dst, w, src, done, name):
                            g, tp = (j + 1).mod(2 * G) % G, (j + 1).mod(2 * G) // G
                            wait(e, s["xT"], (j + 1).div(G))
                            wait(e, s[done], j)
                            for pair in range(4):
                                a = 512 * g + 128 * pair
                                last = matmul3(e, dst[:, pair, :], (w[:, 0, a:a + P], w[:, 1, a:a + P]),
                                               (src[:, tp, 0, :], src[:, tp, 1, :]))
                            last.then_inc(s[name], 1)

                        if (j + 1).inside(U):
                            project(psQ, wq, xT, "q", "Q")
                        if (j - 1).inside(U):
                            par = (j - 1).mod(2)
                            wait(e, s["p_lo"], j - 1)
                            wait(e, s["pt"], j - 2)
                            for hl in range(2):
                                for pair in range(4):
                                    last = e.transpose(psT[:, hl, pair, :], Ph[:, par, hl, pair, :], ident16[:])
                            last.then_inc(s["T"], 1)
                        if (j + 1).inside(U):
                            project(psK, wk, cT, "k", "K")
                        if (j + 2).inside(U) and (j + 2).mod(2 * G) % G == 0:
                            t, tp = (j + 2).div(G), (j + 2).mod(2 * G) // G
                            wait(e, s["x_lo"], t)
                            wait(e, s["res"], t - 5 + G)
                            for hl in range(2):
                                e.transpose(psX[:, hl, :], xc[:, tp, hl, 0:D], ident16[:])
                            for hl in range(2):
                                last = e.transpose(psX[0:DC, 2 + hl, :], xc[:, tp, hl, D:D + DC], ident16[:])
                            last.then_inc(s["X"], 1)
                        if (j - 1).inside(U):
                            par = (j - 1).mod(2)
                            wait(e, s["pt"], j - 1)
                            wait(e, s["v_lo"], j - 1, 2)
                            wait(e, s["o_lo"], j - 2)
                            for pair in range(4):
                                for b in range(2):
                                    last = matmul3(e, psO[:, pair, half(b)],
                                                   (vB[:, par, 0, 4 * b + pair, :], vB[:, par, 1, 4 * b + pair, :]),
                                                   (PT[:, 0, pair, half(b)], PT[:, 1, pair, half(b)]))
                            last.then_inc(s["PV"], 1)
                    pipeline(e, body, -2, U + 2, 4, U - 4, 2 * G)

                @block.scalar
                def _(e):
                    def body(j):
                        if j.inside(U):
                            par = j.mod(2)
                            wait(e, s["V"], j)
                            wait(e, s["PV"], j - 2)
                            for hp in range(2):
                                e.activation(vblock(0, par, hp), psV[half(hp)], ACT.Copy).then_inc(s["v_hi"], 1)
                        if (j - 1).inside(U):
                            par = (j - 1).mod(2)
                            wait(e, s["mul"], j - 1)
                            wait(e, s["T"], j - 3)
                            e.activation(Ph[:, par, 0].rearrange("p k (h l) -> p k h l", h=2), E[:, par],
                                         ACT.Copy).then_inc(s["p_hi"], 1)
                        if j.inside(U):
                            par = j.mod(2)
                            wait(e, s["sub"], j)
                            e.activation(E[:, par], E[:, par], ACT.Exp, bias=zero_col[:], scale=DH ** -0.5)\
                             .then_inc(s["exp"], 1)
                        if (j + 1).inside(U):
                            wait(e, s["Q"], j + 1)
                            e.activation(qT[:], psQ[:], ACT.Copy).then_inc(s["q"], 1)
                            wait(e, s["K"], j + 1)
                            e.activation(kT[:], psK[:], ACT.Copy).then_inc(s["k"], 1)
                        if (j + 2).inside(U) and (j + 2).mod(2 * G) % G == 0:
                            t, tp = (j + 2).div(G), (j + 2).mod(2 * G) // G
                            wait(e, s["X"], t)
                            e.activation(xT[:, tp], psX[:, 0:2, :], ACT.Copy)
                            e.activation(cT[:, tp], psX[0:DC, 2:4, :], ACT.Copy).then_inc(s["xT"], 1)
                        if (j - 1).inside(U):
                            g = (j - 1).mod(2 * G) % G
                            wait(e, s["PV"], j - 1)
                            wait(e, s["Y"], (j - 1).div(G) - 1)
                            e.activation(oT[:, g, 0], psO[:], ACT.Copy).then_inc(s["o_hi"], 1)
                        if (j + 3).inside(U) and (j + 3).mod(2 * G) % G == 0:
                            t, tp = (j + 3).div(G), (j + 3).mod(2 * G) // G
                            wait(e, s["ln"], t)
                            wait(e, s["cc"], t)
                            wait(e, s["X"], t - 2)
                            e.activation(xc[:, tp, 0], xcf[:, tp], ACT.Copy).then_inc(s["x_hi"], 1)
                    pipeline(e, body, -3, U + 1, 4, U - 4, 2 * G)

                @block.gpsimd
                def _(e):
                    def body(j):
                        if (j - 1).inside(U):
                            par = (j - 1).mod(2)
                            wait(e, s["p_hi"], j - 1)
                            e.tensor_tensor(Ph[:, par, 1].rearrange("p k t -> p (k t)"),
                                            E[:, par].rearrange("p k h l -> p (k h l)"),
                                            Ph[:, par, 0].rearrange("p k t -> p (k t)"), ALU.subtract)\
                             .then_inc(s["p_lo"], 1)
                        if (j + 3).inside(U) and (j + 3).mod(2 * G) % G == 0:
                            t, tp = (j + 3).div(G), (j + 3).mod(2 * G) // G
                            wait(e, s["x_lo"], t - 2)
                            e.tensor_copy(xcf[:, tp, D:D + DC], tile_of(t, ctx32)).then_inc(s["cc"], 1)
                        if (j + 2).inside(U) and (j + 2).mod(2 * G) % G == 0:
                            t = (j + 2).div(G)
                            wait(e, s["ln"], t)
                            e.tensor_tensor(tile_of(t, x), tile_of(t, x), bo_rep[:], ALU.add).then_inc(s["bo"], 1)
                        if j.inside(U):
                            par = j.mod(2)
                            wait(e, s["rden"], j)
                            e.tensor_tensor(E[:, par].rearrange("p k h l -> p (k h) l"),
                                            E[:, par].rearrange("p k h l -> p (k h) l"),
                                            rden[:, par, :].unsqueeze(2).broadcast_to([P, 8, N]), ALU.mult)\
                             .then_inc(s["mul"], 1)
                    pipeline(e, body, -3, U + 1, 4, U - 4, 2 * G)

                @block.vector
                def _(e):
                    def body(j):
                        if j.inside(U):
                            par = j.mod(2)
                            for hp in range(2):
                                wait(e, s["v_hi"], j, 2, hp - 1)
                                e.tensor_tensor(vblock(1, par, hp), psV[half(hp)], vblock(0, par, hp),
                                                ALU.subtract).then_inc(s["v_lo"], 1)
                        if (j + 2).inside(U) and (j + 2).mod(2 * G) % G == 0:
                            t, tp = (j + 2).div(G), (j + 2).mod(2 * G) // G
                            wait(e, s["x_hi"], t)
                            e.tensor_tensor(xc[:, tp, 1], xcf[:, tp], xc[:, tp, 0], ALU.subtract)\
                             .then_inc(s["x_lo"], 1)
                        if j.inside(U):
                            S = psS[:, :, 0:256].rearrange("p h (k l) -> p h k l", l=N)
                            wait(e, s["S"], j)
                            e.tensor_reduce(top[:], S, AX.X, ALU.max).then_inc(s["max"], 1)
                            wait(e, s["max"], j)
                            wait(e, s["p_lo"], j - 2)
                            e.tensor_tensor(E[:, par].rearrange("p k h l -> p h k l"), S,
                                            top[:].unsqueeze(3).broadcast_to([P, 2, 4, N]), ALU.subtract)\
                             .then_inc(s["sub"], 1)
                        if (j - 2).inside(U) and (j - 2).mod(2 * G) % G == G - 1:
                            t = (j - 2).div(G)
                            wait(e, s["Y"], t)
                            wait(e, s["bo"], t)
                            e.scalar_tensor_tensor(tile_of(t, x), psY, gate, tile_of(t, x),
                                                   ALU.mult, ALU.add).then_inc(s["res"], 1)
                        if (j - 1).inside(U):
                            wait(e, s["T"], j - 1)
                            wait(e, s["PV"], j - 2)
                            e.tensor_copy(PT[:], psT[:]).then_inc(s["pt"], 1)
                        if j.inside(U):
                            wait(e, s["exp"], j)
                            e.tensor_reduce(den[:, par, :], E[:, par].rearrange("p k h l -> p (k h) l"),
                                            AX.X, ALU.add).then_inc(s["den"], 1)
                            wait(e, s["den"], j)
                            e.reciprocal(rden[:, par, :], den[:, par, :]).then_inc(s["rden"], 1)
                        if (j + 3).inside(U) and (j + 3).mod(2 * G) % G == 0:
                            t, tp = (j + 3).div(G), (j + 3).mod(2 * G) // G
                            wait(e, s["x_lo"], t - 2)
                            e.tensor_scalar(xcf[:, tp, 0:D], tile_of(t, x), column_of(t, mean), column_of(t, rstd),
                                            ALU.subtract, ALU.mult).then_inc(s["ln"], 1)
                        if (j - 1).inside(U):
                            g = (j - 1).mod(2 * G) % G
                            wait(e, s["o_hi"], j - 1)
                            e.tensor_tensor(oT[:, g, 1], psO[:], oT[:, g, 0], ALU.subtract)\
                             .then_inc(s["o_lo"], 1)
                    pipeline(e, body, -3, U + 2, 4, U - 4, 2 * G)

        s.close()

    def queue_norm(e_dve, e_act, s, t, par, raw, pairs, read, x_lo=None):
        if e_dve is not None:
            wait(e_dve, x_lo or s["x_lo"], t - 2)
            e_dve.tensor_scalar(raw[:, par], tile_of(t, x), column_of(t, mean), column_of(t, rstd),
                                ALU.subtract, ALU.mult).then_inc(s["ln"], 1)
        if e_act is not None:
            wait(e_act, s["ln"], t)
            wait(e_act, read, t - 2)
            e_act.activation(pairs[:, par, 0], raw[:, par], ACT.Copy).then_inc(s["x_hi"], 1)
        if e_dve is not None:
            wait(e_dve, s["x_hi"], t)
            e_dve.tensor_tensor(pairs[:, par, 1], raw[:, par], pairs[:, par, 0], ALU.subtract)\
                 .then_inc(s["x_lo"], 1)

    def expert_choice(tag, gate):
        norm_statistics(tag + "n")
        with ExitStack() as c:
            w1 = sb(c, "ew1", [P, 2, NE, DFF], F16)
            w2 = sb(c, "ew2", [P, 2, NE, FT, D], F16)
            idx16 = sb(c, "idx16", [P, NE * CAP], F16)
            gate_slot = sb(c, "gate_slot", [P, NE, 32], F32)
            tok_slot = sb(c, "tok_slot", [P, NE, 32], F32)
            b1T = sb(c, "eb1T", [P, NE * FT], F32)
            select_tokens(tag + "s", w1, w2, idx16, gate_slot, tok_slot, b1T)
            run_experts(tag + "e", gate, w1, w2, idx16, gate_slot, tok_slot, b1T)

    def select_tokens(tag, w1, w2, idx16, gate_slot, tok_slot, b1T):
        s = Sems(tag)
        with ExitStack() as c:
            lg = sb(c, "lg", [P, NE, N], F32)
            with ExitStack() as cl:
                gq32 = sb(cl, "gq32", [P, NE], F32)
                gq = sb(cl, "gq", [P, 2, NE], F16)
                xnf = sb(cl, "xnf", [P, 2, D], F32)
                xn = sb(cl, "xn", [P, 2, 2, D], F16)
                xT = sb(cl, "xTs", [P, 2, 2, P], F16)
                L = sb(cl, "L", [NE, NT, P], F32)
                psX = ps(cl, "psXs", [P, 2, 2, 512], F16)
                psL = ps(cl, "psL", [NE, 2, 512], F32)
                with nc.Block() as block:
                    @block.sync
                    def _(e):
                        with nc.allow_non_contiguous_dma("a small weight, transposed once"):
                            e.dma_start(gq32[:], I["L0_ffn_gate_query"].rearrange("e d -> d e")).then_inc(s["gq"], 16)
                        wait(e, s["l"], Step(None, 0, NT - 1))
                        for k in range(NE):
                            e.dma_start(lg[:, k, :], L[k:k + 1].rearrange("e t p -> e (t p)").rearrange(
                                "e (b n) -> e b n", n=N)).then_inc(s["lg"], 16)
                        e.wait_ge(s["lg"], 16 * NE)

                    @block.tensor
                    def _(e):
                        def body(j):
                            if (j + 1).inside(NT):
                                par = (j + 1).mod(2)
                                wait(e, s["x_lo"], j + 1)
                                wait(e, s["xT"], j - 1)
                                for hl in range(2):
                                    last = e.transpose(psX[:, par, hl, 0:P], xn[:, par, hl, :], ident16[:])
                                last.then_inc(s["X"], 1)
                            if j.inside(NT):
                                par = j.mod(2)
                                if j.reg is None:
                                    wait(e, s["gq_lo"], Step(None, 0, 0))
                                wait(e, s["xT"], j)
                                wait(e, s["l"], j - 2)
                                matmul3(e, psL[:, par, 0:P], (gq[:, 0, :], gq[:, 1, :]),
                                        (xT[:, par, 0, :], xT[:, par, 1, :])).then_inc(s["L"], 1)
                        pipeline(e, body, -1, NT, 2, NT - 4, 2)

                    @block.scalar
                    def _(e):
                        e.wait_ge(s["gq"], 16)
                        e.activation(gq[:, 0, :], gq32[:], ACT.Copy).then_inc(s["gq_hi"], 1)

                        def body(j):
                            if (j + 2).inside(NT):
                                queue_norm(None, e, s, j + 2, (j + 2).mod(2), xnf, xn, s["X"])
                            if j.inside(NT):
                                wait(e, s["L"], j)
                                e.activation(tile_of(j, L), psL[:, j.mod(2), 0:P], ACT.Copy).then_inc(s["l"], 1)
                        pipeline(e, body, -2, NT, 4, NT - 4, 2)

                    @block.vector
                    def _(e):
                        e.wait_ge(s["gq_hi"], 1)
                        e.tensor_tensor(gq[:, 1, :], gq32[:], gq[:, 0, :], ALU.subtract).then_inc(s["gq_lo"], 1)

                        def body(j):
                            if (j + 2).inside(NT):
                                queue_norm(e, None, s, j + 2, (j + 2).mod(2), xnf, xn, None)
                            if (j + 1).inside(NT):
                                par = (j + 1).mod(2)
                                wait(e, s["X"], j + 1)
                                wait(e, s["L"], j - 1)
                                e.tensor_copy(xT[:, par], psX[:, par, :, 0:P]).then_inc(s["xT"], 1)
                        pipeline(e, body, -2, NT, 4, NT - 4, 2)

            z = sb(c, "z", [P, NE, N], F32)
            m = sb(c, "m", [P, N], F32)
            total = sb(c, "total", [P, N], F32)
            temp = sb(c, "temp", [P, 3], F32)
            row = sb(c, "row", [P, N], F32)
            seen = sb(c, "seen", [P, 1], F32)
            v32 = sb(c, "v32", [P, CAP], F32)
            i32 = sb(c, "i32", [P, CAP], U32)
            vals = sb(c, "vals", [P, NE, CAP], F32)
            idx32 = sb(c, "idx32", [P, NE, CAP], F32)
            raw = sb(c, "rawe", [P, 2, 4, DFF], F32)
            psG = ps(c, "psG", [P, NE, 32], F32)
            psI = ps(c, "psI", [P, NE, 32], F32)
            w1v = I["L0_ffn_w1"].rearrange("e d f -> d e f")
            w2v = I["L0_ffn_w2"].rearrange("e (k p) d -> p e k d", p=P)
            with nc.Block() as block:
                @block.sync
                def _(e):
                    e.dma_start(temp[:, 0:1], I["L0_ffn_log_temp"].partition_broadcast(P)).then_inc(s["temp"], 16)
                    with nc.allow_non_contiguous_dma("a small bias, transposed once"):
                        e.dma_start(b1T[:], I["L0_ffn_b1"].rearrange("e (k p) -> p (e k)", p=P)).then_inc(s["b1"], 16)
                    for k in range(8):
                        if k >= 2:
                            e.wait_ge(s["w_lo"], k - 1)
                        g = 4 * (k % 4)
                        if k < 4:
                            e.dma_start(raw[:, k % 2], w1v[:, g:g + 4, :]).then_inc(s[f"raw{k % 2}"], 16)
                        else:
                            e.dma_start(raw[:, k % 2].rearrange("p e (k d) -> p e k d", d=D),
                                        w2v[:, g:g + 4]).then_inc(s[f"raw{k % 2}"], 16)
                    e.wait_ge(s["b1"], 16)

                @block.gpsimd
                def _(e):
                    for k in range(8):
                        g = 4 * (k % 4)
                        to = [w1[:, hl, g:g + 4, :] if k < 4 else
                              w2[:, hl, g:g + 4].rearrange("p e k d -> p e (k d)") for hl in range(2)]
                        e.wait_ge(s[f"raw{k % 2}"], 16 * (k // 2 + 1))
                        e.tensor_copy(to[0], raw[:, k % 2]).then_inc(s["w_hi"], 1)
                        e.wait_ge(s["w_hi"], k + 1)
                        e.tensor_tensor(to[1], raw[:, k % 2], to[0], ALU.subtract).then_inc(s["w_lo"], 1)

                views = []
                for axis, n in ((0, N), (1, NE)):
                    order = "p e n -> p n e" if axis == 0 else "p e n -> p e n"
                    views.append((axis, n, lg[:].rearrange(order), z[:].rearrange(order),
                                  m[:, 0:n].unsqueeze(2).broadcast_to([P, n, NE * N // n])))

                @block.scalar
                def _(e):
                    e.wait_ge(s["temp"], 16)
                    e.activation(temp[:, 1:2], temp[:, 0:1], ACT.Exp, bias=zero_col[:]).then_inc(s["et"], 1)
                    with e.Fori(0, ITERS) as i:
                        j = Step(i, 1, 0)
                        for axis, n, tv, zv, mb in views:
                            wait(e, s[f"z{axis}"], j)
                            e.activation(z[:], z[:], ACT.Exp, bias=zero_col[:]).then_inc(s[f"e{axis}"], 1)
                            wait(e, s[f"s{axis}"], j)
                            e.activation(total[:, 0:n], total[:, 0:n], ACT.Ln, bias=zero_col[:])\
                             .then_inc(s[f"l{axis}"], 1)
                    e.wait_ge(s["t1"], ITERS)
                    e.activation(lg[:], lg[:], ACT.Exp, bias=zero_col[:]).then_inc(s["aff"], 1)

                @block.vector
                def _(e):
                    e.wait_ge(s["et"], 1)
                    e.reciprocal(temp[:, 2:3], temp[:, 1:2]).then_inc(s["rt"], 1)
                    e.wait_ge(s["rt"], 1)
                    e.tensor_scalar(lg[:], lg[:], temp[:, 2:3], None, ALU.mult).then_inc(s["t"], 1)
                    e.wait_ge(s["t"], 1)
                    with e.Fori(0, ITERS) as i:
                        j = Step(i, 1, 0)
                        for axis, n, tv, zv, mb in views:
                            e.tensor_reduce(m[:, 0:n], tv, AX.X, ALU.max).then_inc(s[f"m{axis}"], 1)
                            wait(e, s[f"m{axis}"], j)
                            e.tensor_tensor(zv, tv, mb, ALU.subtract).then_inc(s[f"z{axis}"], 1)
                            wait(e, s[f"e{axis}"], j)
                            e.tensor_reduce(total[:, 0:n], zv, AX.X, ALU.add).then_inc(s[f"s{axis}"], 1)
                            wait(e, s[f"l{axis}"], j)
                            e.tensor_tensor(m[:, 0:n], m[:, 0:n], total[:, 0:n], ALU.add).then_inc(s[f"u{axis}"], 1)
                            wait(e, s[f"u{axis}"], j)
                            e.tensor_tensor(tv, tv, mb, ALU.subtract).then_inc(s[f"t{axis}"], 1)
                            wait(e, s[f"t{axis}"], j)
                    e.wait_ge(s["aff"], 1)
                    with e.Fori(0, NE) as i:
                        j = Step(i, 1, 0)
                        e.tensor_copy(row[:], tile_of(j, lg)).then_inc(s["row"], 1)
                        wait(e, s["row"], j)
                        e.tensor_copy(seen[:], row[:, 0:1])
                        for r in range(CAP // 8):
                            eight = slice(8 * r, 8 * r + 8)
                            e.max(v32[:, eight], row[:]).then_inc(s["top"], 1)
                            wait(e, s["top"], j, CAP // 8, r + 1 - CAP // 8)
                            e.tensor_copy(vals[:, bass.ds(j.value, 1), eight], v32[:, eight].unsqueeze(1))\
                             .then_inc(s["vals"], 1)
                            e.max_index(i32[:, eight], v32[:, eight], row[:]).then_inc(s["ti"], 1)
                            e.match_replace(row[:], v32[:, eight], row[:], -1.0).then_inc(s["rep"], 1)
                            wait(e, s["ti"], j, CAP // 8, r + 1 - CAP // 8)
                            wait(e, s["rep"], j, CAP // 8, r + 1 - CAP // 8)
                            e.tensor_copy(idx32[:, bass.ds(j.value, 1), eight], i32[:, eight].unsqueeze(1))\
                             .then_inc(s["idx"], 1)
                    e.wait_ge(s["idx"], NE * CAP // 8)
                    e.tensor_copy(idx16[:], idx32[:].rearrange("p e c -> p (e c)"))
                    e.wait_ge(s["slots"], 1)
                    e.tensor_copy(gate_slot[:], psG[:])
                    e.tensor_scalar(tok_slot[:], psI[:], block_of_p[:], None, ALU.add)

                @block.tensor
                def _(e):
                    e.wait_ge(s["vals"], NE * CAP // 8)
                    e.wait_ge(s["idx"], NE * CAP // 8)
                    for k in range(NE):
                        for q in range(4):
                            e.matmul(psG[32 * q:32 * q + 32, k, :], vals[:, k, :], ident32[:, q::4],
                                     start=True, stop=True)
                            last = e.matmul(psI[32 * q:32 * q + 32, k, :], idx32[:, k, :], ident32[:, q::4],
                                            start=True, stop=True)
                    last.then_inc(s["slots"], 1)
        s.close()

    def run_experts(tag, gate, w1, w2, idx16, gate_slot, tok_slot, b1T):
        s = Sems(tag)
        seeded = {n: Counter(s[n], 16) for n in (
            "sel", "g_hi", "g_lo", "gelu", "h_lo", "b2add", "eo_lo", "xadd", "g", "x_lo", "R", "E", "A", "put")}
        with nc.Block() as block:
            @block.sync
            def _(e):
                for n in seeded.values():
                    e.sem_inc(n.handle, n.start)
        GB = 16
        GT = GB * N // P
        ROWS = GB * CAP
        RT = ROWS // P
        NG = B // GB
        with ExitStack() as c:
            b2_rep = sb(c, "b2_rep", [P, NE, D], F32)
            xnf = sb(c, "xnfe", [P, 2, D], F32)
            xn = sb(c, "xne", [P, 2, 2, D], F16)
            pick = sb(c, "pick", [P, 2, P], F16)
            sel = sb(c, "sel", [P, 2, NE * CAP], F16)
            xg = sb(c, "xg", [P, 2, NE, ROWS], F16)
            g32 = sb(c, "g32", [P, FT, ROWS], F32)
            h = sb(c, "h", [P, 2, 2, FT, ROWS], F16)
            put = sb(c, "put", [P, 2, RT, 256], F16)
            eo32 = sb(c, "eo32", [P, RT, D], F32)
            eo = sb(c, "eo", [P, 2, 2, RT, D], F16)
            psH = ps(c, "psH", [P, 4, 512], F32)
            psE = ps(c, "psE", [P, RT, D], F32)
            psA = ps(c, "psA", [P, GT, D], F32)
            psR = ps(c, "psR", [P, 512], F32)
            sl = load = None

            def expert_steps(G, e, body, first, last, lo, hi, unroll):
                base = G * NE
                for k in range(first, lo):
                    body(k, None, Step(base, 1, k), k % 2)
                n = (hi - lo) // unroll
                with e.Fori(0, n) as i:
                    for u in range(unroll):
                        body(None, i * unroll + (lo + u), Step(base + i * unroll, 1, lo + u), u % 2)
                for k in range(lo + n * unroll, last):
                    body(k, None, Step(base, 1, k), k % 2)

            def at(k, reg, off=0):
                return (reg + off, True) if k is None else (k + off, 0 <= k + off < NE)

            with nc.Block() as block:
                @block.sync
                def _(e):
                    e.dma_start(b2_rep[:], I["L0_ffn_b2"].rearrange("e d -> (e d)").partition_broadcast(P)
                                .rearrange("p (e d) -> p e d", d=D)).then_inc(s["b2"], 16)

                @block.tensor
                def _(e):
                    with e.Fori(0, NG) as G:
                        for k in range(GT + 1):
                            if k < GT:
                                t = Step(G * GT, 1, k)
                                wait(e, s["pick"], t)
                                wait(e, seeded["sel"], t - 1)
                                e.matmul(psR[:], pick[:, k % 2, :], idx16[:], start=True, stop=True)\
                                 .then_inc(s["R"], 1)
                            if k >= 1:
                                t, par = Step(G * GT, 1, k - 1), (k - 1) % 2
                                wait(e, seeded["sel"], t)
                                wait(e, seeded["x_lo"], t)
                                wait(e, seeded["g_hi"], t - 1, 2)
                                wait(e, seeded["g_lo"], t - 1, 2)
                                for bp in range(2):
                                    for hl in range(2):
                                        q = slice(64 * bp, 64 * bp + 64)
                                        last = e.matmul(psH[:, 2 * bp + hl, :], xn[q, par, hl, :], sel[q, par, :],
                                                        start=True, stop=True)
                                last.then_inc(s["g"], 1)
                        wait(e, seeded["g_hi"], Step(G * GT, 1, GT - 1), 2)
                        wait(e, seeded["g_lo"], Step(G * GT, 1, GT - 1), 2)

                        def body(k, reg, j, par):
                            x1, ok = at(k, reg, 1)
                            if ok:
                                for ft in range(FT):
                                    wait(e, seeded["gelu"], j, FT, ft + 1 - FT)
                                    last = matmul3(e, psH[:, ft, :],
                                                   [w1[:, hl, bass.ds(x1, 1), ft * P:ft * P + P]
                                                    .rearrange("p o f -> p (o f)") for hl in range(2)],
                                                   [xg[:, hl, bass.ds(x1, 1), :].rearrange("p o f -> p (o f)")
                                                    for hl in range(2)])
                                    last.then_inc(s["H"], 1)
                            x0, ok = at(k, reg)
                            if ok:
                                wait(e, seeded["h_lo"], j, 2)
                                wait(e, seeded["b2add"], j - 1)
                                for r in range(RT):
                                    for ft in range(FT):
                                        last = matmul3(e, psE[:, r, :],
                                                       [h[:, par, hl, ft, r * P:r * P + P] for hl in range(2)],
                                                       [w2[:, hl, bass.ds(x0, 1), ft, :].rearrange("p o f -> p (o f)")
                                                        for hl in range(2)], ft == 0, ft == FT - 1)
                                last.then_inc(s["E"], 1)
                            x9, ok = at(k, reg, -1)
                            if ok:
                                wait(e, seeded["put"], j - 1, RT)
                                wait(e, seeded["eo_lo"], j - 1)
                                if k == 1:
                                    wait(e, seeded["xadd"], Step(G, 1, -1))
                                for r in range(RT):
                                    for q in range(2):
                                        for hl in range(2):
                                            a = 2 * r + q
                                            last = e.matmul(psA[:, a, :], put[:, 1 - par, r, q * P:q * P + P],
                                                            eo[:, 1 - par, hl, r, :],
                                                            start=k == 1 and a % 4 == 0 and hl == 0,
                                                            stop=k == NE and hl == 1, skip_group_check=True)
                                last.then_inc(s["A"], 1)
                        expert_steps(G, e, body, -1, NE + 1, 2, NE - 2, 2)

                def gathered(bp, hl, k):
                    a = (2 * k + bp) * CAP
                    return (xg[:, hl, :, a:a + CAP], psH[:, 2 * bp + hl, :].rearrange("p (e c) -> p e c", c=CAP))

                @block.scalar
                def _(e):
                    with e.Fori(0, NG) as G:
                        for k in range(GT + 1):
                            if k < GT:
                                t = Step(G * GT, 1, k)
                                queue_norm(None, e, s, t, k % 2, xnf, xn, seeded["g"])
                            if k >= 1:
                                t = Step(G * GT, 1, k - 1)
                                wait(e, seeded["g"], t)
                                for bp in range(2):
                                    to, frm = gathered(bp, 0, k - 1)
                                    e.activation(to, frm, ACT.Copy).then_inc(s["g_hi"], 1)

                        def outputs(k, reg, j, par):
                            if at(k, reg, -1)[1]:
                                wait(e, s["gated"], j - 1)
                                wait(e, seeded["A"], j - 3)
                                e.activation(eo[:, 1 - par, 0], eo32[:], ACT.Copy).then_inc(s["eo_hi"], 1)

                        def body(k, reg, j, par):
                            x1, ok = at(k, reg, 1)
                            if not ok:
                                outputs(k, reg, j, par)
                            if ok:
                                for ft in range(FT):
                                    if ft == 2:
                                        outputs(k, reg, j, par)
                                    wait(e, s["H"], j + 1, FT, ft + 1 - FT)
                                    if ft % 2 == 0:
                                        wait(e, seeded["h_lo"], j, 2, ft // 2 - 1)
                                    e.activation(g32[:, ft, :], psH[:, ft, :], ACT.Gelu_apprx_tanh,
                                                 bias=b1T[:, bass.ds(x1 * FT + ft, 1)]).then_inc(s["gelu"], 1)
                                    if ft % 2 == 1:
                                        wait(e, seeded["gelu"], j + 1, FT, ft + 1 - FT)
                                        wait(e, seeded["E"], j - 1)
                                        e.activation(h[:, 1 - par, 0, ft - 1:ft + 1, :], g32[:, ft - 1:ft + 1, :],
                                                     ACT.Copy).then_inc(s["h_hi"], 1)
                        expert_steps(G, e, body, -1, NE + 1, 2, NE - 2, 2)

                @block.gpsimd
                def _(e):
                    with e.Fori(0, NG) as G:
                        def body(k, reg, j, par):
                            x0, ok = at(k, reg)
                            if ok:
                                wait(e, seeded["b2add"], j)
                                g4 = gate_slot[:, bass.ds(x0, 1), bass.ds(G * RT, RT)].rearrange("p o r -> p (o r)")
                                e.tensor_tensor(eo32[:], eo32[:], g4.unsqueeze(2).broadcast_to([P, RT, D]),
                                                ALU.mult).then_inc(s["gated"], 1)
                        expert_steps(G, e, body, 0, NE, 2, NE - 2, 2)

                @block.vector
                def _(e):
                    e.wait_ge(s["b2"], 16)
                    with e.Fori(0, NG) as G:
                        for k in range(GT + 1):
                            if k < GT:
                                t = Step(G * GT, 1, k)
                                wait(e, seeded["R"], t - 2)
                                e.tensor_copy(pick[:, k % 2].rearrange("p (b n) -> p b n", n=N),
                                              ident16[:, bass.ds(t.times(2), 2)].unsqueeze(2)
                                              .broadcast_to([P, 2, N])).then_inc(s["pick"], 1)
                                queue_norm(e, None, s, t, k % 2, xnf, xn, None, seeded["x_lo"])
                                wait(e, seeded["R"], t)
                                wait(e, seeded["g"], t - 2)
                                e.tensor_scalar(sel[:, k % 2, :], psR[:], token_of_p[:], None, ALU.is_equal)\
                                 .then_inc(s["sel"], 1)
                            if k >= 1:
                                t = Step(G * GT, 1, k - 1)
                                wait(e, seeded["g"], t)
                                for bp in range(2):
                                    to, frm = gathered(bp, 1, k - 1)
                                    e.tensor_copy(to, frm).then_inc(s["g_lo"], 1)

                        def body(k, reg, j, par):
                            x0, ok = at(k, reg)
                            if ok:
                                wait(e, seeded["A"], j - 2)
                                for r in range(RT):
                                    e.tensor_scalar(put[:, par, r, :], iota256[:],
                                                    tok_slot[:, bass.ds(x0, 1), bass.ds(G * RT + r, 1)]
                                                    .rearrange("p o r -> p (o r)"),
                                                    None, ALU.is_equal).then_inc(s["put"], 1)
                            if at(k, reg, -1)[1]:
                                wait(e, s["eo_hi"], j - 1)
                                e.tensor_tensor(eo[:, 1 - par, 1], eo32[:], eo[:, 1 - par, 0], ALU.subtract)\
                                 .then_inc(s["eo_lo"], 1)
                            x1, ok = at(k, reg, 1)
                            if ok:
                                for q in range(2):
                                    wait(e, s["h_hi"], j + 1, 2, q - 1)
                                    wait(e, seeded["E"], j - 1)
                                    e.tensor_tensor(h[:, 1 - par, 1, 2 * q:2 * q + 2, :], g32[:, 2 * q:2 * q + 2, :],
                                                    h[:, 1 - par, 0, 2 * q:2 * q + 2, :], ALU.subtract)\
                                     .then_inc(s["h_lo"], 1)
                            x0, ok = at(k, reg)
                            if ok:
                                wait(e, seeded["E"], j)
                                wait(e, seeded["eo_lo"], j - 1)
                                e.tensor_tensor(eo32[:], psE[:], b2_rep[:, bass.ds(x0, 1), :]
                                                .broadcast_to([P, RT, D]), ALU.add).then_inc(s["b2add"], 1)
                        expert_steps(G, e, body, -1, NE + 1, 2, NE - 2, 2)
                        wait(e, seeded["A"], Step(G * NE, 1, NE - 1))
                        for q in range(2):
                            xs = x[:, bass.ds(G * GT + 4 * q, 4), :]
                            last = e.scalar_tensor_tensor(xs, psA[:, 4 * q:4 * q + 4, :], gate, xs, ALU.mult, ALU.add)
                        last.then_inc(s["xadd"], 1)
        s.close()

    def routed(tag, so):
        norm_statistics(tag + "n")
        s = Sems(tag)
        with ExitStack() as c:
            w1 = sb(c, "rw1", [P, 2, NE1, D], F16)
            w2 = sb(c, "rw2", [P, 2, NE1, D], F16)
            b1s = sb(c, "b1s", [P, B, TOPK], F32)
            b2s = sb(c, "b2s", [P, B], F32)
            erow = sb(c, "erow", [1, B * TOPK], U32)
            with ExitStack() as cr:
                raw = sb(cr, "rraw", [P, 2, NE1, D], F32)
                wr32 = sb(cr, "wr32", [P, NE1], F32)
                wr = sb(cr, "wr", [P, 2, NE1], F16)
                br = sb(cr, "br", [P, NE1], F32)
                b12 = sb(cr, "b12", [NE1, 2, D], F32)
                x0 = sb(cr, "x0", [P, D], F32)
                st = sb(cr, "st", [P, 6], F32)
                mv = sb(cr, "mv", [P, 2], F32)
                sd = sb(cr, "sd", [P, 2], F32)
                xn0 = sb(cr, "xn0", [P, D], F32)
                xh0 = sb(cr, "xh0", [P, 2, D], F16)
                xT0 = sb(cr, "xT0", [P, 2, P], F16)
                sc = sb(cr, "sc", [P, NE1], F32)
                best = sb(cr, "best", [P, 8], F32)
                bi = sb(cr, "bi", [P, 8], U32)
                bf = sb(cr, "bf", [P, 8], F32)
                at = sb(cr, "at", [P, TOPK], U32)
                oh = sb(cr, "oh", [P, TOPK, NE1], F32)
                i8 = sb(cr, "i8", [P, NE1], F32)
                ohT = sb(cr, "ohT", [NE1, TOPK, B], F32)
                psX0 = ps(cr, "psX0", [P, 2, P], F16)
                psC = ps(cr, "psC", [P, 512], F32)
                psB = ps(cr, "psB", [P, 512], F32)
                dram = nc.dram_tensor("choices", [B, TOPK], U32)
                with nc.Block() as block:
                    @block.sync
                    def _(e):
                        load_all(e, s["w"], [(raw[:, 0], I["L1_ffn_W1"].rearrange("e d f -> d e f")),
                                             (raw[:, 1], I["L1_ffn_W2"].rearrange("e d f -> d e f"))])
                        load_all(e, s["c"], [(wr32[:], I["L1_ffn_Wr"]), (br[:], I["L1_ffn_br"].partition_broadcast(P)),
                                             (b12[:, 0], I["L1_ffn_b1"]), (b12[:, 1], I["L1_ffn_b2"])])
                        load_all(e, s["x0"], [(x0[bp::2, :], x[64 * bp:64 * bp + 1, :, :]) for bp in range(2)])
                        e.wait_ge(s["at"], 1)
                        e.dma_start(dram.ap(), at[:]).then_inc(s["choices"], 16)
                        e.wait_ge(s["choices"], 16)
                        e.dma_start(erow[:], dram.ap().rearrange("b k -> (b k)").unsqueeze(0)).then_inc(s["erow"], 16)
                        e.wait_ge(s["erow"], 16)

                    @block.gpsimd
                    def _(e):
                        e.iota(i8[:], [[1, NE1]], base=0, channel_multiplier=0,
                               allow_small_or_imprecise_dtypes=True).then_inc(s["i8"], 1)

                    parts = [(wr32[:], wr[:, 0], wr[:, 1]), (xn0[:], xh0[:, 0], xh0[:, 1]),
                             (raw[:, 0], w1[:, 0], w1[:, 1]), (raw[:, 1], w2[:, 0], w2[:, 1])]

                    @block.scalar
                    def _(e):
                        e.wait_ge(s["var"], 1)
                        e.activation(sd[:, 0:1], mv[:, 1:2], ACT.Sqrt, bias=eps_col[:]).then_inc(s["sd"], 1)
                        e.wait_ge(s["c"], 64)
                        split(e, None, s, 0, *parts[0])
                        e.wait_ge(s["ln0"], 1)
                        split(e, None, s, 1, *parts[1])
                        e.wait_ge(s["w"], 32)
                        split(e, None, s, 2, *parts[2])
                        split(e, None, s, 3, *parts[3])

                    @block.vector
                    def _(e):
                        e.wait_ge(s["x0"], 32)
                        e.bn_stats(st[:], x0[:]).then_inc(s["st"], 1)
                        e.wait_ge(s["st"], 1)
                        e.bn_aggr(mv[:], st[:]).then_inc(s["var"], 1)
                        e.wait_ge(s["sd"], 1)
                        e.reciprocal(sd[:, 1:2], sd[:, 0:1]).then_inc(s["rs"], 1)
                        e.wait_ge(s["rs"], 1)
                        e.tensor_scalar(xn0[:], x0[:], mv[:, 0:1], sd[:, 1:2], ALU.subtract, ALU.mult)\
                         .then_inc(s["ln0"], 1)
                        split(None, e, s, 0, *parts[0])
                        split(None, e, s, 1, *parts[1])
                        e.wait_ge(s["X0"], 1)
                        e.tensor_copy(xT0[:], psX0[:]).then_inc(s["xT0"], 1)
                        e.wait_ge(s["C"], 1)
                        e.tensor_tensor(sc[:], psC[:, 0:NE1], br[:], ALU.add).then_inc(s["sc"], 1)
                        e.wait_ge(s["sc"], 1)
                        e.max(best[:], sc[:]).then_inc(s["best"], 1)
                        e.wait_ge(s["best"], 1)
                        e.max_index(bi[:], best[:], sc[:]).then_inc(s["bi"], 1)
                        e.wait_ge(s["bi"], 1)
                        e.tensor_copy(bf[:], bi[:]).then_inc(s["bf"], 1)
                        e.wait_ge(s["bf"], 1)
                        e.tensor_scalar(at[:], bf[:, 0:TOPK], float(D), None, ALU.mult).then_inc(s["at"], 1)
                        e.wait_ge(s["i8"], 1)
                        for k in range(TOPK):
                            e.tensor_scalar(oh[:, k, :], i8[:], bf[:, k:k + 1], None, ALU.is_equal)\
                             .then_inc(s["oh"], 1)
                        e.wait_ge(s["ohP"], 1)
                        e.tensor_copy(ohT[:], psB[0:NE1, 0:TOPK * B].rearrange("p (k b) -> p k b", b=B))\
                         .then_inc(s["ohT"], 1)
                        e.wait_ge(s["bP"], 1)
                        e.tensor_copy(b1s[:].rearrange("p b k -> p k b"),
                                      psC[:, 0:TOPK * B].rearrange("p (k b) -> p k b", b=B))
                        e.tensor_copy(b2s[:], psC[:, TOPK * B:TOPK * B + B])
                        split(None, e, s, 2, *parts[2])
                        split(None, e, s, 3, *parts[3])

                    @block.tensor
                    def _(e):
                        e.wait_ge(s["w_lo"], 2)
                        for hl in range(2):
                            last = e.transpose(psX0[:, hl, :], xh0[:, hl, :], ident16[:])
                        last.then_inc(s["X0"], 1)
                        e.wait_ge(s["xT0"], 1)
                        matmul3(e, psC[:, 0:NE1], (xT0[:, 0], xT0[:, 1]), (wr[:, 0], wr[:, 1])).then_inc(s["C"], 1)
                        e.wait_ge(s["oh"], TOPK)
                        for k in range(TOPK):
                            last = e.matmul(psB[0:NE1, k * B:k * B + B], oh[:, k, :], ident32[:], start=True, stop=True)
                        last.then_inc(s["ohP"], 1)
                        e.wait_ge(s["ohT"], 1)
                        e.matmul(psC[:, 0:TOPK * B], b12[:, 0, :], ohT[:].rearrange("p k b -> p (k b)"),
                                 start=True, stop=True)
                        for k in range(TOPK):
                            last = e.matmul(psC[:, TOPK * B:TOPK * B + B], b12[:, 1, :], ohT[:, k, :],
                                            start=k == 0, stop=k == TOPK - 1)
                        last.then_inc(s["bP"], 1)

            TS = 2
            BK = 2 * TS * TOPK
            STEPS = NT // TS
            xnf = sb(c, "xnfr", [P, 2, TS, D], F32)
            xn = sb(c, "xnr", [P, 2, 2, TS, D], F16)
            xT = sb(c, "xTr", [P, 2, 2, TS * P], F16)
            a32 = sb(c, "a32", [P, BK, N], F32)
            g32 = sb(c, "g32r", [P, BK, N], F32)
            h = sb(c, "hr", [P, 2, 2, BK, N], F16)
            y32 = sb(c, "y32", [P, 2, 2 * TS, N], F32)
            psX = ps(c, "psXr", [P, 2, TS, P], F16)
            psH = ps(c, "psHr", [P, 2, BK, N], F32)
            psO = ps(c, "psOr", [P, 2, 8, N], F32)
            psZ = ps(c, "psZr", [P, 2, 4, P], F32)
            w1a, w2a = (w[:].rearrange("p h e f -> p h (e f)") for w in (w1, w2))
            with nc.Block() as block:
                @block.tensor
                def _(e):
                    def experts(j):
                        return nc.values_load_multi_w_load_instructions(
                            erow[0:1, bass.ds(j.times(BK), BK)], engines=(mybir.EngineType.PE,),
                            min_val=0, max_val=(NE1 - 1) * D,
                            skip_runtime_bounds_check_because="D times an index of 8 columns that MaxIndex gave")[1]

                    def body(j):
                        if (j + 1).inside(STEPS):
                            par = (j + 1).mod(2)
                            wait(e, s["x_lo"], j + 1)
                            wait(e, s["xT"], j)
                            for hl in range(2):
                                for k in range(TS):
                                    last = e.transpose(psX[:, hl, k, :], xn[:, par, hl, k, :], ident16[:])
                            last.then_inc(s["X"], 1)
                        if (j - 2).inside(STEPS):
                            par = j.mod(2)
                            ids = experts(j - 2)
                            wait(e, s["h_lo"], j - 2)
                            wait(e, s["y"], j - 4)
                            for q in range(BK):
                                b, k = q // TOPK, q % TOPK
                                last = matmul3(e, psO[:, par, b, :],
                                               [w2a[:, hl, bass.ds(ids[q], D)] for hl in range(2)],
                                               [h[:, par, hl, q, :] for hl in range(2)], k == 0, k == TOPK - 1)
                            last.then_inc(s["O"], 1)
                        if j.inside(STEPS):
                            par = j.mod(2)
                            ids = experts(j)
                            wait(e, s["xT"], j)
                            wait(e, s["bias"], j - 2)
                            for q in range(BK):
                                b = q // TOPK
                                last = matmul3(e, psH[:, par, q, :],
                                               [w1a[:, hl, bass.ds(ids[q], D)] for hl in range(2)],
                                               [xT[:, par, hl, N * b:N * b + N] for hl in range(2)])
                            last.then_inc(s["H"], 1)
                        if (j - 3).inside(STEPS):
                            par = (j - 3).mod(2)
                            wait(e, s["y"], j - 3)
                            wait(e, s["res"], j - 5)
                            for k in range(TS):
                                last = e.transpose(psZ[:, par, k, :], y32[:, par, 2 * k:2 * k + 2, :]
                                                   .rearrange("p b n -> p (b n)"), ident32[:])
                            last.then_inc(s["Z"], 1)
                    pipeline(e, body, -1, STEPS + 3, 6, STEPS - 4, 2)

                @block.scalar
                def _(e):
                    def body(j):
                        if (j - 1).inside(STEPS):
                            par = (j - 1).mod(2)
                            wait(e, s["bias"], j - 1)
                            wait(e, s["h_lo"], j - 2)
                            e.activation(g32[:], a32[:], ACT.Gelu, bias=zero_col[:]).then_inc(s["gelu"], 1)
                            wait(e, s["gelu"], j - 1)
                            wait(e, s["O"], j - 3)
                            e.activation(h[:, par, 0], g32[:], ACT.Copy).then_inc(s["h_hi"], 1)
                        if (j + 3).inside(STEPS):
                            par = (j + 3).mod(2)
                            wait(e, s["ln"], j + 3)
                            wait(e, s["X"], j + 1)
                            e.activation(xn[:, par, 0], xnf[:, par], ACT.Copy).then_inc(s["x_hi"], 1)
                    pipeline(e, body, -3, STEPS + 1, 6, STEPS - 4, 2)

                @block.vector
                def _(e):
                    def body(j):
                        if (j - 2).inside(STEPS):
                            par = (j - 2).mod(2)
                            wait(e, s["O"], j - 2)
                            wait(e, s["Z"], j - 4)
                            e.tensor_tensor(y32[:, par], psO[:, par, 0:2 * TS, :],
                                            b2s[:, bass.ds((j - 2).times(2 * TS), 2 * TS)].unsqueeze(2)
                                            .broadcast_to([P, 2 * TS, N]), ALU.add).then_inc(s["y"], 1)
                        if (j - 1).inside(STEPS):
                            par = (j - 1).mod(2)
                            wait(e, s["h_hi"], j - 1)
                            e.tensor_tensor(h[:, par, 1], g32[:], h[:, par, 0], ALU.subtract).then_inc(s["h_lo"], 1)
                        if (j + 2).inside(STEPS):
                            par = (j + 2).mod(2)
                            wait(e, s["x_hi"], j + 2)
                            e.tensor_tensor(xn[:, par, 1], xnf[:, par], xn[:, par, 0], ALU.subtract)\
                             .then_inc(s["x_lo"], 1)
                        if (j + 1).inside(STEPS):
                            wait(e, s["X"], j + 1)
                            e.tensor_copy(xT[:, (j + 1).mod(2)], psX[:].rearrange("p h k t -> p h (k t)"))\
                             .then_inc(s["xT"], 1)
                        if j.inside(STEPS):
                            wait(e, s["H"], j)
                            wait(e, s["gelu"], j - 1)
                            bias = b1s[:, bass.ds(j.times(2 * TS), 2 * TS), :].rearrange("p b k -> p (b k)")
                            e.tensor_tensor(a32[:], psH[:, j.mod(2)], bias.unsqueeze(2).broadcast_to([P, BK, N]),
                                            ALU.add).then_inc(s["bias"], 1)
                        if (j - 3).inside(STEPS):
                            t = j - 3
                            wait(e, s["Z"], t)
                            xs = x[:, bass.ds(t.times(TS), TS), :]
                            e.scalar_tensor_tensor(xs, psZ[:, t.mod(2), 0:TS, :], half_g[:], xs,
                                                   ALU.mult, ALU.add).then_inc(s["res"], 1)
                        if (j + 3).inside(STEPS):
                            par = (j + 3).mod(2)
                            wait(e, s["x_lo"], j + 1)
                            for k in range(TS):
                                t = Step((j + 3).times(TS), 1, k)
                                last = e.tensor_scalar(xnf[:, par, k], tile_of(t, x), column_of(t, mean),
                                                       column_of(t, rstd), ALU.subtract, ALU.mult)
                            last.then_inc(s["ln"], 1)
                    pipeline(e, body, -3, STEPS + 3, 6, STEPS - 4, 2)

                @block.sync
                def _(e):
                    for k in range(0, NT, 8):
                        e.wait_ge(s["res"], (k + 8) // TS)
                        e.dma_start(ov[:, k:k + 8, :], x[:, k:k + 8, :]).then_inc(so, 16)
                    e.wait_ge(so, 16 * NT // 8)
        s.close()

    S0.close()
    attention("a0", 1, I["L0_xattn_Wq"], I["L0_xattn_Wk"], I["L0_xattn_Wv"], I["L0_xattn_Wo"],
              I["L0_xattn_bo"], tanh_g[:, 0:1])
    expert_choice("m", tanh_g[:, 2:3])
    attention("a1", 2, I["L1_xattn_Wq"], I["L1_xattn_Wk"], I["L1_xattn_Wv"], I["L1_xattn_Wo"],
              I["L1_xattn_bo"], tanh_g[:, 1:2])
    routed("r", sem("out"))


_OUTS = [((B, N, D), "float32")]


def kernel(**inputs):
    import numpy as _np
    import concourse.bacc as _bacc
    from concourse import mybir as _mybir
    from concourse.bass_utils import run_bass_kernel_spmd as _run

    nc = _bacc.Bacc("TRN2", target_bir_lowering=False, num_devices=1)
    arrays, args = {}, {}
    for name, a in inputs.items():
        a = _np.ascontiguousarray(a)
        if a.ndim == 0:
            a = a.reshape(1)
        arrays[f"in_{name}_dram"] = a
        args[name] = nc.dram_tensor(f"in_{name}_dram", a.shape, _mybir.dt.from_np(a.dtype), kind="ExternalInput").ap()
    shape, dtype = _OUTS[0]
    o = nc.dram_tensor("out_0_dram", shape, _mybir.dt.from_np(_np.dtype(dtype)), kind="ExternalOutput").ap()
    program(nc, args, o)
    r = _run(nc, [arrays], core_ids=[0])
    return r.results[0]["out_0_dram"]
```

```python
from contextlib import ExitStack

import concourse.bass as bass
from concourse import mybir

F32 = mybir.dt.float32
F16 = mybir.dt.float16
U32 = mybir.dt.uint32
I32 = mybir.dt.int32
ALU = mybir.AluOpType
ACT = mybir.ActivationFunctionType
AX = mybir.AxisListType

P = 128
B, N, D, DC = 128, 64, 128, 96
NT = B * N // P
DH = 64
NE, CAP, DFF = 16, 32, 512
FT = DFF // P
ITERS = 6
NE1, TOPK = 8, 2
EPS = 1e-5


class Step:

    def __init__(self, reg, mult, off):
        self.reg, self.mult, self.off = reg, mult, off

    def __add__(self, k):
        return Step(self.reg, self.mult, self.off + k)

    def __sub__(self, k):
        return self + (-k)

    def div(self, g):
        return Step(self.reg, self.mult // g, self.off // g)

    def mod(self, m):
        assert self.reg is None or self.mult % m == 0
        return self.off % m

    def inside(self, n):
        return True if self.reg is not None else 0 <= self.off < n

    def upto(self, n):
        return self if self.reg is not None or self.off <= n else Step(None, 0, n)

    def times(self, k, add=0):
        if self.reg is None:
            return self.off * k + add
        return self.reg * (self.mult * k) + (self.off * k + add)

    @property
    def value(self):
        return self.times(1)


class Counter:

    def __init__(self, handle, start):
        self.handle, self.start = handle, start


def wait(eng, sem, step, per=1, add=0):
    if isinstance(sem, Counter):
        sem, add = sem.handle, add + sem.start
    if step.reg is None and step.times(per, per + add) <= 0:
        return
    eng.wait_ge(sem, step.times(per, per + add))


def pipeline(eng, body, first, last, lo, hi, unroll):
    a = -(-lo // unroll) * unroll
    n = max(0, (hi - a) // unroll)
    b = a + n * unroll
    for j in range(first, a):
        body(Step(None, 0, j))
    if n:
        with eng.Fori(0, n) as i:
            for u in range(unroll):
                body(Step(i, unroll, a + u))
    for j in range(b, last):
        body(Step(None, 0, j))


def program(nc, I, out):
    with ExitStack() as whole:
        _build(nc, whole, I, out)


def _build(nc, whole, I, out):
    made = {}

    def sb(ctx, name, shape, dt):
        made[name] = made.get(name, 0) + 1
        return ctx.enter_context(nc.sbuf_tensor(f"{name}_{made[name]}", shape, dt))

    def ps(ctx, name, shape, dt):
        made[name] = made.get(name, 0) + 1
        return ctx.enter_context(nc.psum_tensor(f"{name}_{made[name]}", shape, dt))

    def sem(name):
        return nc.alloc_semaphore(name=name)

    class Sems:

        def __init__(self, stage):
            self.stage, self.all = stage, {}

        def __getitem__(self, name):
            if name not in self.all:
                self.all[name] = sem(f"{self.stage}_{name}")
            return self.all[name]

        def close(self):
            nc.clear_and_free_semaphores(list(self.all.values()))
            nc.all_engine_barrier()

    def load_all(eng, s, pairs):
        for to, frm in pairs:
            eng.dma_start(to, frm).then_inc(s, 16)
        return 16 * len(pairs)

    x = sb(whole, "x", [P, NT, D], F32)
    ident16 = sb(whole, "ident16", [P, P], F16)
    ident32 = sb(whole, "ident32", [P, P], F32)
    token_of_p = sb(whole, "token_of_p", [P, 1], F32)
    block_of_p = sb(whole, "block_of_p", [P, 1], F32)
    iota = sb(whole, "iota", [P, P], F16)
    eps_col = sb(whole, "eps_col", [P, 1], F32)
    zero_col = sb(whole, "zero_col", [P, 1], F32)
    gates = sb(whole, "gates", [P, 4], F32)
    tanh_g = sb(whole, "tanh_g", [P, 4], F32)
    half_g = sb(whole, "half_g", [P, 1], F32)
    stats = sb(whole, "stats", [P, NT, 6], F32)
    mean = sb(whole, "mean", [P, NT], F32)
    rstd = sb(whole, "rstd", [P, NT], F32)

    xv = I["x"].rearrange("b n d -> (b n) d").rearrange("(t p) d -> p t d", p=P)
    cv = I["ctx_768"].rearrange("b n d -> (b n) d").rearrange("(t p) d -> p t d", p=P)
    ov = out.rearrange("b n d -> (b n) d").rearrange("(t p) d -> p t d", p=P)

    def tile_of(t, tensor):
        return tensor[:, bass.ds(t.value, 1), :].rearrange("p o d -> p (o d)")

    def column_of(t, tensor):
        return tensor[:, bass.ds(t.value, 1)]

    def queue_stats(e, t):
        return e.bn_stats(tile_of(t, stats), tile_of(t, x))

    S0 = Sems("init")
    with nc.Block() as block:
        @block.scalar
        def _(e):
            n = load_all(e, S0["gates"], [(gates[:, 0:2], I["g_xattn"].partition_broadcast(P)),
                                        (gates[:, 2:4], I["g_ffn"].partition_broadcast(P))])
            e.wait_ge(S0["gates"], n)
            e.wait_ge(S0["zero"], 1)
            e.activation(tanh_g[:], gates[:], ACT.Tanh, bias=zero_col[:]).then_inc(S0["tanh"], 1)
            e.wait_ge(S0["tanh"], 1)
            e.activation(half_g[:], tanh_g[:, 3:4], ACT.Copy, scale=1.0 / TOPK)

        @block.vector
        def _(e):
            e.memset(zero_col[:], 0.0).then_inc(S0["zero"], 1)
            e.memset(eps_col[:], EPS)
            for q in range(4):
                e.memset(block_of_p[32 * q:32 * q + 32, :], float(N * (q % 2)))
            e.wait_ge(S0["iota"], 1)
            e.tensor_scalar(token_of_p[64:P, :], token_of_p[64:P, :], -float(N), None, ALU.add)

        @block.gpsimd
        def _(e):
            e.memset(ident16[:], 0.0).then_inc(S0["id"], 1)
            e.memset(ident32[:], 0.0).then_inc(S0["id"], 1)
            e.wait_ge(S0["id"], 2)
            for m in (ident16, ident32):
                e.affine_select(out=m[:], in_=m[:], compare_op=ALU.not_equal, fill=1.0, base=0,
                                pattern=[[-1, P]], channel_multiplier=1)
            e.iota(token_of_p[:], [[0, 1]], base=0, channel_multiplier=1,
                   allow_small_or_imprecise_dtypes=True).then_inc(S0["iota"], 1)
            e.iota(iota[:], [[1, P]], base=0, channel_multiplier=0,
                   allow_small_or_imprecise_dtypes=True)

    def split(e_act, e_dve, s, k, raw, hi, lo):
        if e_act is not None:
            e_act.activation(hi, raw, ACT.Copy).then_inc(s["w_hi"], 1)
        if e_dve is not None:
            e_dve.wait_ge(s["w_hi"], k + 1)
            e_dve.tensor_tensor(lo, raw, hi, ALU.subtract).then_inc(s["w_lo"], 1)

    def products(pairs):
        (lh, ll), (rh, rl) = pairs
        return [(lh, rh), (lh, rl), (ll, rh)]

    def matmul3(e, to, left, right, start=True, stop=True, **flags):
        three = products((left, right))
        for n, (a, b) in enumerate(three):
            last = e.matmul(to, a, b, start=start and n == 0, stop=stop and n == 2, **flags)
        return last

    def queue_norm_vector(e, s, lnt):
        me, mo = stats[:, :, 1], stats[:, :, 4]
        e.tensor_tensor(lnt[:, 0, :], me, mo, ALU.subtract).then_inc(s["v"], 1)
        e.tensor_tensor(lnt[:, 1, :], stats[:, :, 2], stats[:, :, 5], ALU.add).then_inc(s["v"], 1)
        e.tensor_tensor(lnt[:, 2, :], me, mo, ALU.add).then_inc(s["v"], 1)
        e.wait_ge(s["v"], 3)
        e.tensor_scalar(mean[:], lnt[:, 2, :], 0.5, None, ALU.mult)
        e.scalar_tensor_tensor(lnt[:, 0, :], lnt[:, 0, :], D / 4.0, lnt[:, 0, :],
                               ALU.mult, ALU.mult).then_inc(s["v"], 1)
        e.wait_ge(s["v"], 4)
        e.tensor_tensor(lnt[:, 1, :], lnt[:, 1, :], lnt[:, 0, :], ALU.add).then_inc(s["v"], 1)
        e.wait_ge(s["sqrt"], 1)
        e.reciprocal(rstd[:], lnt[:, 2, :])

    def queue_norm_scalar(e, s, lnt):
        e.wait_ge(s["v"], 5)
        e.activation(lnt[:, 2, :], lnt[:, 1, :], ACT.Sqrt, bias=eps_col[:], scale=1.0 / D).then_inc(s["sqrt"], 1)

    def load_x(e, s):
        for c in range(0, NT, 16):
            e.dma_start(x[:, c:c + 16, :], xv[:, c:c + 16, :]).then_inc(s[f"x{c}"], 16)

    def queue_first_stats(e, s):
        for c in range(0, NT, 16):
            e.wait_ge(s[f"x{c}"], 16)
            with e.Fori(0, 2) as i:
                for u in range(8):
                    last = queue_stats(e, Step(i, 8, c + u))
                    last.then_inc(s["stats"], 1)
        e.wait_ge(s["stats"], NT)

    def norm_statistics(tag):
        s = Sems(tag)
        with ExitStack() as c:
            lnt = sb(c, "lnt", [P, 3, NT], F32)
            with nc.Block() as block:
                @block.vector
                def _(e):
                    queue_norm_vector(e, s, lnt)

                @block.scalar
                def _(e):
                    queue_norm_scalar(e, s, lnt)
        s.close()

    def attention(tag, G, Wq, Wk, Wv, Wo, bo, gate, first=False):
        U = NT * G
        INNER = 512 * G
        s = Sems(tag)
        with ExitStack() as c:
            lnt = sb(c, "lnt", [P, 3, NT], F32)
            ctx32 = sb(c, "ctx32", [P, NT, DC], F32)
            raw = sb(c, "raw", [P, 4, INNER], F32)
            wq = sb(c, "wq", [P, 2, INNER], F16)
            wk = sb(c, "wk", [DC, 2, INNER], F16)
            wv = sb(c, "wv", [DC, 2, INNER], F16)
            wo = sb(c, "wo", [P, 2, 4 * G, D], F16)
            bo_rep = sb(c, "bo_rep", [P, D], F32)
            xcf = sb(c, "xcf", [P, 2, D + DC], F32)
            xc = sb(c, "xc", [P, 2, 2, D + DC], F16)
            xT = sb(c, "xT", [P, 2, 2, P], F16)
            cT = sb(c, "cT", [DC, 2, 2, P], F16)
            qT = sb(c, "qT", [P, 4, P], F32)
            kT = sb(c, "kT", [P, 4, P], F32)
            vB = sb(c, "vB", [P, 2, 2, 8, P], F16)
            E = sb(c, "E", [P, 2, 4, 2, N], F32)
            Ph = sb(c, "Ph", [P, 2, 2, 4, P], F16)
            PT = sb(c, "PT", [P, 2, 4, P], F16)
            top = sb(c, "top", [P, 2, 4], F32)
            den = sb(c, "den", [P, 2, 8], F32)
            rden = sb(c, "rden", [P, 2, 8], F32)
            oT = sb(c, "oT", [P, G, 2, 4, P], F16)
            psQ = ps(c, "psQ", [P, 4, P], F32)
            psK = ps(c, "psK", [P, 4, P], F32)
            psV = ps(c, "psV", [P, 8, DH], F32)
            psS = ps(c, "psS", [P, 2, 512], F32)
            psT = ps(c, "psT", [P, 2, 4, P], F16)
            psO = ps(c, "psO", [P, 4, P], F32)
            psXY = ps(c, "psXY", [P, 512], F32)
            psX = psXY[:, 0:256].bitcast(F16).rearrange("p (k t) -> p k t", k=4)
            psY = psXY[:, 256:384]

            CT = 4

            def load_context(e, first, last):
                for t in range(first, last, CT):
                    e.dma_start(ctx32[:, t:t + CT, :], cv[:, t:t + CT, :]).then_inc(s["ctx"], 16)
                    e.wait_ge(s["ctx"], 16 * (t // CT + 1))
                    e.sem_inc(s["ctx_tiles"], CT)

            with nc.Block() as block:
                weights = [(raw[:, 0, :], Wq), (raw[0:DC, 1, :], Wk), (raw[0:DC, 2, :], Wv),
                           (raw[:, 3, :].rearrange("p (k d) -> p k d", d=D), Wo.rearrange("(k p) d -> p k d", p=P))]
                parts = [(raw[:, 0, :], wq[:, 0, :], wq[:, 1, :]),
                         (raw[0:DC, 1, :], wk[:, 0, :], wk[:, 1, :]),
                         (raw[0:DC, 2, :], wv[:, 0, :], wv[:, 1, :]),
                         (raw[:, 3, :], wo[:, 0].rearrange("p k d -> p (k d)"), wo[:, 1].rearrange("p k d -> p (k d)"))]

                @block.sync
                def _(e):
                    load_all(e, s["w"], weights + [(bo_rep[:], bo.partition_broadcast(P))])
                    if first:
                        load_x(e, s)
                    load_context(e, 0, 8)

                @block.scalar
                def _(e):
                    if not first:
                        queue_norm_scalar(e, s, lnt)
                    e.wait_ge(s["w"], 16 * 5)
                    for k, p in enumerate(parts):
                        split(e, None, s, k, *p)
                    if first:
                        queue_norm_scalar(e, s, lnt)

                @block.vector
                def _(e):
                    if not first:
                        queue_norm_vector(e, s, lnt)
                    e.memset(vB[:].rearrange("p a b c d -> p (a b c d)").bitcast(U32), 0)
                    e.wait_ge(s["w"], 16 * 5)
                    e.tensor_scalar(bo_rep[:], bo_rep[:], gate, None, ALU.mult)
                    for k, p in enumerate(parts):
                        split(None, e, s, k, *p)
                    if first:
                        queue_first_stats(e, s)
                        queue_norm_vector(e, s, lnt)

            def half(hp):
                return slice(64 * hp, 64 * hp + 64)

            def vblock(hl, par, hp):
                return vB[half(hp), par, hl, :, half(hp)]

            with nc.Block() as block:
                @block.sync
                def _(e):
                    load_context(e, 8, NT)

                @block.tensor
                def _(e):
                    def body(j):
                        if j.inside(U):
                            t = j.div(G)
                            g, tp = j.mod(2 * G) % G, j.mod(2 * G) // G
                            wait(e, s["xT"], t)
                            wait(e, s["v_lo"], j - 1, 2)
                            for hp in range(2):
                                for b in range(2):
                                    if (hp, b) == (1, 1):
                                        wait(e, s["q"], j)
                                        wait(e, s["k"], j)
                                        wait(e, s["sub"], j - 1)
                                    w = [wv[:, hl, 512 * g:512 * g + 512].rearrange(
                                        "p (k h d) -> p k h d", h=2, d=DH)[:, :, hp, :] for hl in range(2)]
                                    last = matmul3(e, psV[half(hp), 4 * b:4 * b + 4, :],
                                                   (cT[:, tp, 0, half(b)], cT[:, tp, 1, half(b)]), w)
                            last.then_inc(s["V"], 1)
                            for hp in range(2):
                                for pair in range(4):
                                    for b in range(2):
                                        last = e.matmul(psS[half(b), hp, 64 * pair:64 * pair + 64],
                                                        qT[half(hp), pair, half(b)], kT[half(hp), pair, half(b)],
                                                        start=True, stop=True)
                            last.then_inc(s["S"], 1)
                        if (j - 2).inside(U) and (j - 2).mod(2 * G) % G == G - 1:
                            t = (j - 2).div(G)
                            wait(e, s["o_lo"], j - 2)
                            wait(e, s["xT"], (t + 4 - G).upto(NT - 1))
                            for g in range(G):
                                for pair in range(4):
                                    last = matmul3(e, psY, (oT[:, g, 0, pair, :], oT[:, g, 1, pair, :]),
                                                   (wo[:, 0, 4 * g + pair, :], wo[:, 1, 4 * g + pair, :]),
                                                   g == 0 and pair == 0, g == G - 1 and pair == 3)
                            last.then_inc(s["Y"], 1)

                        def project(dst, w, src, done, name):
                            g, tp = (j + 1).mod(2 * G) % G, (j + 1).mod(2 * G) // G
                            wait(e, s["xT"], (j + 1).div(G))
                            wait(e, s[done], j)
                            for pair in range(4):
                                a = 512 * g + 128 * pair
                                last = matmul3(e, dst[:, pair, :], (w[:, 0, a:a + P], w[:, 1, a:a + P]),
                                               (src[:, tp, 0, :], src[:, tp, 1, :]))
                            last.then_inc(s[name], 1)

                        if (j + 1).inside(U):
                            project(psQ, wq, xT, "q", "Q")
                        def transpose_probabilities():
                            par = (j - 1).mod(2)
                            wait(e, s["p_lo"], j - 1)
                            wait(e, s["pt"], j - 2)
                            for hl in range(2):
                                for pair in range(4):
                                    last = e.transpose(psT[:, hl, pair, :], Ph[:, par, hl, pair, :], ident16[:])
                            last.then_inc(s["T"], 1)

                        early = (j - 2).mod(2 * G) % G == G - 1
                        if early and (j - 1).inside(U):
                            transpose_probabilities()
                        if (j + 1).inside(U):
                            project(psK, wk, cT, "k", "K")
                        if not early and (j - 1).inside(U):
                            transpose_probabilities()
                        if (j + 2).inside(U) and (j + 2).mod(2 * G) % G == 0:
                            t, tp = (j + 2).div(G), (j + 2).mod(2 * G) // G
                            wait(e, s["x_lo"], t)
                            wait(e, s["res"], t - 5 + G)
                            for hl in range(2):
                                e.transpose(psX[:, hl, :], xc[:, tp, hl, 0:D], ident16[:])
                            for hl in range(2):
                                last = e.transpose(psX[0:DC, 2 + hl, :], xc[:, tp, hl, D:D + DC], ident16[:])
                            last.then_inc(s["X"], 1)
                        if (j - 1).inside(U):
                            par = (j - 1).mod(2)
                            wait(e, s["pt"], j - 1)
                            wait(e, s["v_lo"], j - 1, 2)
                            wait(e, s["o_lo"], j - 2)
                            for pair in range(4):
                                for b in range(2):
                                    last = matmul3(e, psO[:, pair, half(b)],
                                                   (vB[:, par, 0, 4 * b + pair, :], vB[:, par, 1, 4 * b + pair, :]),
                                                   (PT[:, 0, pair, half(b)], PT[:, 1, pair, half(b)]))
                            last.then_inc(s["PV"], 1)
                    pipeline(e, body, -2, U + 2, 4, U - 4, 4)

                @block.scalar
                def _(e):
                    def body(j):
                        if j.inside(U):
                            wait(e, s["V"], j)
                            wait(e, s["PV"], j - 2)
                            e.activation(vblock(0, j.mod(2), 0), psV[half(0)], ACT.Copy).then_inc(s["v_hi"], 1)
                        if (j - 1).inside(U):
                            par = (j - 1).mod(2)
                            wait(e, s["mul"], j - 1)
                            wait(e, s["T"], j - 3)
                            e.activation(Ph[:, par, 0].rearrange("p k (h l) -> p k h l", h=2), E[:, par],
                                         ACT.Copy).then_inc(s["p_hi"], 1)
                        if j.inside(U):
                            e.activation(vblock(0, j.mod(2), 1), psV[half(1)], ACT.Copy).then_inc(s["v_hi"], 1)
                        if j.inside(U):
                            par = j.mod(2)
                            wait(e, s["sub"], j)
                            e.activation(E[:, par], E[:, par], ACT.Exp, bias=zero_col[:], scale=DH ** -0.5)\
                             .then_inc(s["exp"], 1)
                        if (j + 1).inside(U):
                            wait(e, s["Q"], j + 1)
                            e.activation(qT[:], psQ[:], ACT.Copy).then_inc(s["q"], 1)
                            wait(e, s["K"], j + 1)
                            e.activation(kT[:], psK[:], ACT.Copy).then_inc(s["k"], 1)
                        if (j + 2).inside(U) and (j + 2).mod(2 * G) % G == 0:
                            t, tp = (j + 2).div(G), (j + 2).mod(2 * G) // G
                            wait(e, s["X"], t)
                            e.activation(xT[:, tp], psX[:, 0:2, :], ACT.Copy)
                            e.activation(cT[:, tp], psX[0:DC, 2:4, :], ACT.Copy).then_inc(s["xT"], 1)
                        if (j - 1).inside(U):
                            g = (j - 1).mod(2 * G) % G
                            wait(e, s["PV"], j - 1)
                            wait(e, s["Y"], (j - 1).div(G) - 1)
                            e.activation(oT[:, g, 0], psO[:], ACT.Copy).then_inc(s["o_hi"], 1)
                        if (j + 3).inside(U) and (j + 3).mod(2 * G) % G == 0:
                            t, tp = (j + 3).div(G), (j + 3).mod(2 * G) // G
                            wait(e, s["ln"], t)
                            wait(e, s["cc"], t)
                            wait(e, s["X"], t - 2)
                            e.activation(xc[:, tp, 0], xcf[:, tp], ACT.Copy).then_inc(s["x_hi"], 1)
                    pipeline(e, body, -3, U + 1, 4, U - 4, 4)

                @block.gpsimd
                def _(e):
                    def body(j):
                        if (j - 1).inside(U):
                            par = (j - 1).mod(2)
                            wait(e, s["p_hi"], j - 1)
                            e.tensor_tensor(Ph[:, par, 1].rearrange("p k t -> p (k t)"),
                                            E[:, par].rearrange("p k h l -> p (k h l)"),
                                            Ph[:, par, 0].rearrange("p k t -> p (k t)"), ALU.subtract)\
                             .then_inc(s["p_lo"], 1)
                        if (j + 2).inside(U) and (j + 2).mod(2 * G) % G == 0:
                            t, tp = (j + 2).div(G), (j + 2).mod(2 * G) // G
                            wait(e, s["x_hi"], t)
                            e.tensor_tensor(xc[:, tp, 1], xcf[:, tp], xc[:, tp, 0], ALU.subtract)\
                             .then_inc(s["x_lo"], 1)
                        if (j + 3).inside(U) and (j + 3).mod(2 * G) % G == 0:
                            t, tp = (j + 3).div(G), (j + 3).mod(2 * G) // G
                            wait(e, s["x_lo"], t - 2)
                            wait(e, s["ctx_tiles"], t)
                            e.tensor_copy(xcf[:, tp, D:D + DC], tile_of(t, ctx32)).then_inc(s["cc"], 1)
                        if (j + 2).inside(U) and (j + 2).mod(2 * G) % G == 0:
                            t = (j + 2).div(G)
                            wait(e, s["ln"], t)
                            e.tensor_tensor(tile_of(t, x), tile_of(t, x), bo_rep[:], ALU.add).then_inc(s["bo"], 1)
                        if j.inside(U):
                            par = j.mod(2)
                            wait(e, s["rden"], j)
                            e.tensor_tensor(E[:, par].rearrange("p k h l -> p (k h) l"),
                                            E[:, par].rearrange("p k h l -> p (k h) l"),
                                            rden[:, par, :].unsqueeze(2).broadcast_to([P, 8, N]), ALU.mult)\
                             .then_inc(s["mul"], 1)
                    pipeline(e, body, -3, U + 1, 4, U - 4, 4)

                @block.vector
                def _(e):
                    def body(j):
                        def value_lo(hp):
                            wait(e, s["v_hi"], j, 2, hp - 1)
                            e.tensor_tensor(vblock(1, j.mod(2), hp), psV[half(hp)], vblock(0, j.mod(2), hp),
                                            ALU.subtract).then_inc(s["v_lo"], 1)

                        if j.inside(U):
                            par = j.mod(2)
                            value_lo(0)
                            S = psS[:, :, 0:256].rearrange("p h (k l) -> p h k l", l=N)
                            wait(e, s["S"], j)
                            e.tensor_reduce(top[:], S, AX.X, ALU.max).then_inc(s["max"], 1)
                            wait(e, s["max"], j)
                            wait(e, s["p_lo"], j - 2)
                            e.tensor_tensor(E[:, par].rearrange("p k h l -> p h k l"), S,
                                            top[:].unsqueeze(3).broadcast_to([P, 2, 4, N]), ALU.subtract)\
                             .then_inc(s["sub"], 1)
                        ends = (j - 2).inside(U) and (j - 2).mod(2 * G) % G == G - 1
                        if ends:
                            t = (j - 2).div(G)
                            wait(e, s["Y"], t)
                            wait(e, s["bo"], t)
                            e.scalar_tensor_tensor(tile_of(t, x), psY, gate, tile_of(t, x),
                                                   ALU.mult, ALU.add).then_inc(s["res"], 1)
                        early = (j - 2).mod(2 * G) % G == G - 1
                        if early and j.inside(U):
                            value_lo(1)
                        if (j - 1).inside(U):
                            wait(e, s["T"], j - 1)
                            wait(e, s["PV"], j - 2)
                            e.tensor_copy(PT[:], psT[:]).then_inc(s["pt"], 1)
                        if not early and j.inside(U):
                            value_lo(1)
                        if j.inside(U):
                            wait(e, s["exp"], j)
                            e.tensor_reduce(den[:, par, :], E[:, par].rearrange("p k h l -> p (k h) l"),
                                            AX.X, ALU.add).then_inc(s["den"], 1)
                            wait(e, s["den"], j)
                            e.reciprocal(rden[:, par, :], den[:, par, :]).then_inc(s["rden"], 1)
                        if (j + 3).inside(U) and (j + 3).mod(2 * G) % G == 0:
                            t, tp = (j + 3).div(G), (j + 3).mod(2 * G) // G
                            wait(e, s["x_lo"], t - 2)
                            e.tensor_scalar(xcf[:, tp, 0:D], tile_of(t, x), column_of(t, mean), column_of(t, rstd),
                                            ALU.subtract, ALU.mult).then_inc(s["ln"], 1)
                        if (j - 1).inside(U):
                            g = (j - 1).mod(2 * G) % G
                            wait(e, s["o_hi"], j - 1)
                            e.tensor_tensor(oT[:, g, 1], psO[:], oT[:, g, 0], ALU.subtract)\
                             .then_inc(s["o_lo"], 1)
                        if ends:
                            t = (j - 2).div(G)
                            wait(e, s["res"], t)
                            queue_stats(e, t)
                    pipeline(e, body, -3, U + 2, 4, U - 4, 4)

        s.close()

    def expert_choice(tag, gate):
        norm_statistics(tag + "n")
        with ExitStack() as c:
            w1 = sb(c, "ew1", [P, 2, NE, DFF], F16)
            w2 = sb(c, "ew2", [P, 2, NE, FT, D], F16)
            idx16 = sb(c, "idx16", [P, NE * CAP], F16)
            gate_slot = sb(c, "gate_slot", [P, NE, 32], F32)
            tok_slot = sb(c, "tok_slot", [P, NE, 32], F32)
            b1T = sb(c, "eb1T", [P, NE * FT], F32)
            b2 = sb(c, "eb2", [64, NE, D], F16)
            select_tokens(tag + "s", w1, w2, idx16, gate_slot, tok_slot, b1T, b2)
            run_experts(tag + "e", gate, w1, w2, idx16, gate_slot, tok_slot, b1T, b2)

    def select_tokens(tag, w1, w2, idx16, gate_slot, tok_slot, b1T, b2):
        s = Sems(tag)
        with ExitStack() as c:
            lg = sb(c, "lg", [P, NE, N], F32)
            with ExitStack() as cl:
                gq32 = sb(cl, "gq32", [P, NE], F32)
                gq = sb(cl, "gq", [P, 2, NE], F16)
                LT = 4
                STEPS = NT // LT
                xnf = sb(cl, "xnf", [P, 2, LT, D], F32)
                xn = sb(cl, "xn", [P, 2, 2, LT, D], F16)
                xT = sb(cl, "xTs", [P, 2, 2, LT * P], F16)
                L = sb(cl, "L", [NE, NT * P], F32)
                psX = ps(cl, "psXs", [P, 2, 2, LT, P], F16)
                psL = ps(cl, "psL", [NE, 2, LT * P], F32)
                with nc.Block() as block:
                    @block.sync
                    def _(e):
                        with nc.allow_non_contiguous_dma("a small weight, transposed once"):
                            e.dma_start(gq32[:], I["L0_ffn_gate_query"].rearrange("e d -> d e")).then_inc(s["gq"], 16)
                        wait(e, s["l"], Step(None, 0, STEPS - 1))
                        for k in range(NE):
                            e.dma_start(lg[:, k, :], L[k:k + 1].rearrange("e (b n) -> e b n", n=N))\
                             .then_inc(s["lg"], 16)
                        e.wait_ge(s["lg"], 16 * NE)

                    @block.tensor
                    def _(e):
                        def body(j):
                            if (j + 1).inside(STEPS):
                                par = (j + 1).mod(2)
                                wait(e, s["x_lo"], j + 1)
                                wait(e, s["xT"], j - 1)
                                for hl in range(2):
                                    for k in range(LT):
                                        last = e.transpose(psX[:, par, hl, k, :], xn[:, par, hl, k, :], ident16[:])
                                last.then_inc(s["X"], 1)
                            if j.inside(STEPS):
                                par = j.mod(2)
                                if j.reg is None:
                                    wait(e, s["gq_lo"], Step(None, 0, 0))
                                wait(e, s["xT"], j)
                                wait(e, s["l"], j - 2)
                                matmul3(e, psL[:, par], (gq[:, 0, :], gq[:, 1, :]),
                                        (xT[:, par, 0, :], xT[:, par, 1, :])).then_inc(s["L"], 1)
                        pipeline(e, body, -1, STEPS, 2, STEPS - 2, 2)

                    @block.scalar
                    def _(e):
                        e.wait_ge(s["gq"], 16)
                        e.activation(gq[:, 0, :], gq32[:], ACT.Copy).then_inc(s["gq_hi"], 1)

                        def body(j):
                            if (j + 2).inside(STEPS):
                                par = (j + 2).mod(2)
                                wait(e, s["ln"], j + 2)
                                wait(e, s["X"], j)
                                e.activation(xn[:, par, 0], xnf[:, par], ACT.Copy).then_inc(s["x_hi"], 1)
                            if j.inside(STEPS):
                                wait(e, s["L"], j)
                                e.activation(L[:, bass.ds(j.times(LT * P), LT * P)], psL[:, j.mod(2)], ACT.Copy)\
                                 .then_inc(s["l"], 1)
                        pipeline(e, body, -2, STEPS, 2, STEPS - 2, 2)

                    @block.gpsimd
                    def _(e):
                        def body(j):
                            par = j.mod(2)
                            wait(e, s["x_hi"], j)
                            e.tensor_tensor(xn[:, par, 1], xnf[:, par], xn[:, par, 0], ALU.subtract)\
                             .then_inc(s["x_lo"], 1)
                        pipeline(e, body, 0, STEPS, 2, STEPS - 2, 2)

                    @block.vector
                    def _(e):
                        e.wait_ge(s["gq_hi"], 1)
                        e.tensor_tensor(gq[:, 1, :], gq32[:], gq[:, 0, :], ALU.subtract).then_inc(s["gq_lo"], 1)

                        def body(j):
                            if (j + 3).inside(STEPS):
                                par = (j + 3).mod(2)
                                wait(e, s["x_lo"], j + 1)
                                for k in range(LT):
                                    t = (j + 3).times(LT, k)
                                    last = e.tensor_scalar(xnf[:, par, k], x[:, bass.ds(t, 1), :]
                                                           .rearrange("p o d -> p (o d)"),
                                                           mean[:, bass.ds(t, 1)], rstd[:, bass.ds(t, 1)],
                                                           ALU.subtract, ALU.mult)
                                last.then_inc(s["ln"], 1)
                            if (j + 1).inside(STEPS):
                                par = (j + 1).mod(2)
                                wait(e, s["X"], j + 1)
                                wait(e, s["L"], j - 1)
                                e.tensor_copy(xT[:, par], psX[:, par].rearrange("p h k t -> p h (k t)"))\
                                 .then_inc(s["xT"], 1)
                        pipeline(e, body, -3, STEPS, 2, STEPS - 4, 2)

            z = sb(c, "z", [P, NE, N], F32)
            m = sb(c, "m", [P, N], F32)
            total = sb(c, "total", [P, N], F32)
            temp = sb(c, "temp", [P, 3], F32)
            ROUNDS = CAP // 8
            row = sb(c, "row", [P, 4, N], F32)
            i32 = sb(c, "i32", [P, NE, CAP], U32)
            vals = sb(c, "vals", [P, NE, CAP], F32)
            idx32 = sb(c, "idx32", [P, NE, CAP], F32)
            raw = sb(c, "rawe", [P, 2, 4, DFF], F32)
            raw_b2 = sb(c, "raw_b2", [64, NE * D], F32)
            hi_b2 = sb(c, "hi_b2", [64, NE * D], F16)
            psG = ps(c, "psG", [P, NE, 32], F32)
            psI = ps(c, "psI", [P, NE, 32], F32)
            w1v = I["L0_ffn_w1"].rearrange("e d f -> d e f")
            w2v = I["L0_ffn_w2"].rearrange("e (k p) d -> p e k d", p=P)
            with nc.Block() as block:
                @block.sync
                def _(e):
                    e.dma_start(temp[:, 0:1], I["L0_ffn_log_temp"].partition_broadcast(P)).then_inc(s["temp"], 16)
                    with nc.allow_non_contiguous_dma("a small bias, transposed once"):
                        e.dma_start(b1T[:], I["L0_ffn_b1"].rearrange("e (k p) -> p (e k)", p=P)).then_inc(s["b1"], 16)
                    e.wait_ge(s["b2_zero"], 2)
                    for r in (0, 32):
                        e.dma_start(raw_b2[r:r + 1, :], I["L0_ffn_b2"].rearrange("e d -> (e d)").unsqueeze(0))\
                         .then_inc(s["b2"], 16)
                    for k in range(8):
                        if k >= 2:
                            e.wait_ge(s["w_lo"], k - 1)
                        g = 4 * (k % 4)
                        if k < 4:
                            e.dma_start(raw[:, k % 2], w1v[:, g:g + 4, :]).then_inc(s[f"raw{k % 2}"], 16)
                        else:
                            e.dma_start(raw[:, k % 2].rearrange("p e (k d) -> p e k d", d=D),
                                        w2v[:, g:g + 4]).then_inc(s[f"raw{k % 2}"], 16)
                    e.wait_ge(s["b1"], 16)

                @block.gpsimd
                def _(e):
                    b2_flat = b2[:].rearrange("p e d -> p (e d)")
                    e.memset(raw_b2[:], 0.0).then_inc(s["b2_zero"], 1)
                    e.memset(b2_flat, 0.0).then_inc(s["b2_zero"], 1)
                    e.wait_ge(s["b2_zero"], 2)
                    e.wait_ge(s["b2"], 32)
                    e.tensor_copy(hi_b2[:], raw_b2[:]).then_inc(s["b2_hi"], 1)
                    e.wait_ge(s["b2_hi"], 1)
                    e.tensor_copy(b2_flat[0:1], hi_b2[0:1]).then_inc(s["b2_pair"], 1)
                    e.wait_ge(s["b2_pair"], 1)
                    e.tensor_tensor(b2_flat[32:33], raw_b2[32:33], hi_b2[32:33], ALU.subtract)\
                     .then_inc(s["b2_pair"], 1)
                    e.wait_ge(s["b2_pair"], 2)
                    for k in range(8):
                        g = 4 * (k % 4)
                        to = [w1[:, hl, g:g + 4, :] if k < 4 else
                              w2[:, hl, g:g + 4].rearrange("p e k d -> p e (k d)") for hl in range(2)]
                        e.wait_ge(s[f"raw{k % 2}"], 16 * (k // 2 + 1))
                        e.tensor_copy(to[0], raw[:, k % 2]).then_inc(s["w_hi"], 1)
                        e.wait_ge(s["w_hi"], k + 1)
                        e.tensor_tensor(to[1], raw[:, k % 2], to[0], ALU.subtract).then_inc(s["w_lo"], 1)

                views = []
                for n, order in ((N, "p e n -> p n e"), (NE, "p e n -> p e n")):
                    halves = []
                    for hf in range(2):
                        q = slice(hf * n // 2, hf * n // 2 + n // 2)
                        tv, zv = (v[:].rearrange(order)[:, q, :] for v in (lg, z))
                        halves.append((tv, zv, m[:, q],
                                       m[:, q].unsqueeze(2).broadcast_to([P, n // 2, NE * N // n]), total[:, q]))
                    views.append(halves)

                @block.scalar
                def _(e):
                    e.wait_ge(s["temp"], 16)
                    e.activation(temp[:, 1:2], temp[:, 0:1], ACT.Exp, bias=zero_col[:]).then_inc(s["et"], 1)
                    with e.Fori(0, ITERS) as i:
                        j = Step(i, 1, 0)
                        for axis, halves in enumerate(views):
                            for hf, (tv, zv, mx, mb, tot) in enumerate(halves):
                                wait(e, s[f"z{axis}"], j, 2, hf - 1)
                                e.activation(zv, zv, ACT.Exp, bias=zero_col[:]).then_inc(s[f"e{axis}"], 1)
                            for hf, (tv, zv, mx, mb, tot) in enumerate(halves):
                                wait(e, s[f"s{axis}"], j, 2, hf - 1)
                                e.activation(tot, tot, ACT.Ln, bias=zero_col[:]).then_inc(s[f"l{axis}"], 1)
                    e.wait_ge(s["t1"], 2 * ITERS)
                    e.activation(lg[:], lg[:], ACT.Exp, bias=zero_col[:]).then_inc(s["aff"], 1)

                @block.vector
                def _(e):
                    e.wait_ge(s["et"], 1)
                    e.reciprocal(temp[:, 2:3], temp[:, 1:2]).then_inc(s["rt"], 1)
                    e.wait_ge(s["rt"], 1)
                    e.tensor_scalar(lg[:], lg[:], temp[:, 2:3], None, ALU.mult).then_inc(s["t"], 1)
                    e.wait_ge(s["t"], 1)
                    with e.Fori(0, ITERS) as i:
                        j = Step(i, 1, 0)
                        for axis, halves in enumerate(views):
                            for tv, zv, mx, mb, tot in halves:
                                e.tensor_reduce(mx, tv, AX.X, ALU.max).then_inc(s[f"m{axis}"], 1)
                            for hf, (tv, zv, mx, mb, tot) in enumerate(halves):
                                wait(e, s[f"m{axis}"], j, 2, hf - 1)
                                e.tensor_tensor(zv, tv, mb, ALU.subtract).then_inc(s[f"z{axis}"], 1)
                            for hf, (tv, zv, mx, mb, tot) in enumerate(halves):
                                wait(e, s[f"e{axis}"], j, 2, hf - 1)
                                e.tensor_reduce(tot, zv, AX.X, ALU.add).then_inc(s[f"s{axis}"], 1)
                            for hf, (tv, zv, mx, mb, tot) in enumerate(halves):
                                wait(e, s[f"l{axis}"], j, 2, hf - 1)
                                e.tensor_tensor(mx, mx, tot, ALU.add).then_inc(s[f"u{axis}"], 1)
                            for hf, (tv, zv, mx, mb, tot) in enumerate(halves):
                                wait(e, s[f"u{axis}"], j, 2, hf - 1)
                                e.tensor_tensor(tv, tv, mb, ALU.subtract).then_inc(s[f"t{axis}"], 1)
                            wait(e, s[f"t{axis}"], j, 2)
                    e.wait_ge(s["aff"], 1)
                    for k0 in range(0, NE, 4):
                        for r in range(ROUNDS):
                            eight = slice(8 * r, 8 * r + 8)
                            chosen = k0 * ROUNDS + 4 * r
                            taken = k0 * (ROUNDS - 1) + 4 * r
                            left = [lg[:, k0 + k, :] if r == 0 else row[:, k, :] for k in range(4)]
                            best = [vals[:, k0 + k, eight] for k in range(4)]
                            for k in range(4):
                                if r > 0:
                                    e.wait_ge(s["rep"], taken - 4 + k + 1)
                                e.max(best[k], left[k]).then_inc(s["top"], 1)
                            for k in range(4):
                                e.wait_ge(s["top"], chosen + k + 1)
                                e.max_index(i32[:, k0 + k, eight], best[k], left[k]).then_inc(s["ti"], 1)
                            if r < ROUNDS - 1:
                                for k in range(4):
                                    e.wait_ge(s["ti"], chosen + k + 1)
                                    e.match_replace(row[:, k, :], best[k], left[k], -1.0).then_inc(s["rep"], 1)
                        e.wait_ge(s["ti"], (k0 + 4) * ROUNDS)
                        e.tensor_copy(idx32[:, k0:k0 + 4], i32[:, k0:k0 + 4]).then_inc(s["idx"], 1)
                    e.wait_ge(s["idx"], NE // 4)
                    e.tensor_copy(idx16[:], idx32[:].rearrange("p e c -> p (e c)"))
                    e.wait_ge(s["slots"], 1)
                    e.tensor_copy(gate_slot[:], psG[:])
                    e.tensor_scalar(tok_slot[:], psI[:], block_of_p[:], None, ALU.add)

                @block.tensor
                def _(e):
                    for k in range(NE):
                        e.wait_ge(s["idx"], k // 4 + 1)
                        for q in range(4):
                            e.matmul(psG[32 * q:32 * q + 32, k, :], vals[:, k, :], ident32[:, q::4],
                                     start=True, stop=True)
                            last = e.matmul(psI[32 * q:32 * q + 32, k, :], idx32[:, k, :], ident32[:, q::4],
                                            start=True, stop=True)
                    last.then_inc(s["slots"], 1)
        s.close()

    def run_experts(tag, gate, w1, w2, idx16, gate_slot, tok_slot, b1T, b2):
        s = Sems(tag)
        seeded = {n: Counter(s[n], 16) for n in ("xadd", "A")}
        GB = 16
        GT = GB * N // P
        ROWS = GB * CAP
        RT = ROWS // P
        NG = B // GB
        with ExitStack() as c:
            ones = sb(c, "ones", [64, P], F16)
            xnf = sb(c, "xnfe", [P, 2, D], F32)
            xn = sb(c, "xne", [P, 2, 2, D], F16)
            pick = sb(c, "pick", [P, 2, P], F16)
            sel = sb(c, "sel", [P, 2, NE * CAP], F16)
            xg = sb(c, "xg", [P, 2, 2 * NE, ROWS], F16)
            g32 = sb(c, "g32", [P, FT, ROWS], F32)
            h = sb(c, "h", [P, 2, 2, FT, ROWS], F16)
            put = sb(c, "put", [P, RT, P], F16)
            eo32 = sb(c, "eo32", [P, RT, D], F32)
            eo = sb(c, "eo", [P, 2, RT, D], F16)
            psH = ps(c, "psH", [P, 4, 512], F32)
            psE = ps(c, "psE", [P, RT, D], F32)
            psA = ps(c, "psA", [P, 2, RT, D], F32)
            psR = ps(c, "psR", [P, 512], F32)

            with nc.Block() as block:
                @block.sync
                def _(e):
                    for n in seeded.values():
                        e.sem_inc(n.handle, n.start)

                @block.vector
                def _(e):
                    e.memset(ones[:], 1.0)

            def flat(G, per, i, mult, off):
                reg = 0 if isinstance(G, int) else G * per
                if isinstance(G, int):
                    off += G * per
                if i is not None:
                    reg = reg + i * mult
                return Step(None, 0, off) if isinstance(reg, int) else Step(reg, 1, off)

            class At:

                def __init__(self, G, e, i=None):
                    self.G, self.e, self.i = G, e, i
                    self.par = e % 2
                    self.fixed = isinstance(G, int)
                    self.j = flat(G, NE, i, 4, e)
                    self.k, self.bp = (e + 1) // 2, (e + 1) % 2
                    self.t = flat(G, GT, i, 2, GT + self.k)

                def has(self, off):
                    return not self.fixed or 0 <= NE * self.G + self.e + off < NE * NG

                def has_tile(self, off):
                    return not self.fixed or GT * (self.G + 1) + self.k + off < NT

                def expert(self, off):
                    return (self.e + off) % NE if self.i is None else self.i * 4 + (self.e + off)

                def group(self, off):
                    return self.G + (self.e + off) // NE if self.i is None else self.G

                def rows(self, hl, off):
                    return xg[:, hl, bass.ds((self.group(off) & 1) * NE + self.expert(off), 1), :]\
                        .rearrange("p o r -> p (o r)")

            def gathered(parity, hl, batch):
                return xg[:, hl, bass.ds(parity * NE, NE), bass.ds(batch * CAP, CAP)]

            def rows_of(at):
                k = at.k if at.i is None else at.i * 2 + at.k
                parity = (at.G + 1 + (at.k // GT if at.i is None else 0)) & 1
                return [gathered(parity, hl, (k % GT if at.i is None else k) * 2 + at.bp) for hl in range(2)]

            def all_steps(eng, body, after_group):
                def group(G):
                    for k in (1, 2):
                        body(At(G, k))
                    fours = (NE - 4) // 4 - (isinstance(G, int) and G == NG - 2)
                    with eng.Fori(0, fours) as i:
                        for u in range(4):
                            body(At(G, 3 + u, i))
                    for k in range(3 + 4 * fours, NE + 1):
                        body(At(G, k))
                    after_group(G)
                for k in (-1, 0):
                    body(At(0, k))
                with eng.Fori(0, NG - 2) as G:
                    group(G)
                for G in (NG - 2, NG - 1):
                    group(G)

            with nc.Block() as block:
                @block.tensor
                def _(e):
                    def batch_rows(par):
                        e.matmul(psR[:], pick[:, par, :], idx16[:], start=True, stop=True).then_inc(s["R"], 1)

                    def take(par, bp, hl, to):
                        q = slice(64 * bp, 64 * bp + 64)
                        e.matmul(to, xn[q, par, hl, :], sel[q, par, :], start=True, stop=True).then_inc(s["g"], 1)

                    for k in range(GT + 1):
                        t = Step(None, 0, k)
                        wait(e, s["pick"], t)
                        wait(e, s["sel"], t - 1)
                        batch_rows(k % 2)
                        if k < GT:
                            wait(e, s["sel"], t)
                            wait(e, s["x_lo"], t)
                            wait(e, s["g_hi"], t - 1, 2)
                            wait(e, s["g_lo"], t - 1, 2)
                            for bp in range(2):
                                for hl in range(2):
                                    take(k % 2, bp, hl, psH[:, 2 * bp + hl, :])

                    def body(a):
                        j, par = a.j, a.par
                        tpar = a.k % 2
                        if a.has(1):
                            if a.e % NE == NE - 1:
                                t = a.t - 1
                                wait(e, s["g_hi"], t, 2)
                                wait(e, s["g_lo"], t, 2)
                            for ft in range(FT):
                                if ft == 2 and a.has_tile(0):
                                    if a.bp == 0:
                                        wait(e, s["sel"], a.t)
                                        wait(e, s["x_lo"], a.t)
                                    else:
                                        wait(e, s["g_lo"], a.t, 2, -1)
                                    take(tpar, a.bp, 0, psR[:])
                                wait(e, s["gelu"], j, FT, ft + 1 - FT)
                                last = matmul3(e, psH[:, ft, :],
                                               [w1[:, hl, bass.ds(a.expert(1), 1), ft * P:ft * P + P]
                                                .rearrange("p o f -> p (o f)") for hl in range(2)],
                                               [a.rows(hl, 1) for hl in range(2)])
                                last.then_inc(s["H"], 1)
                        if a.has(0):
                            wait(e, s["h_lo"], j, 2)
                            wait(e, s["gated"], j - 1)
                            e.matmul(psE[:], ones[:], b2[:, bass.ds(a.expert(0), 1), :].broadcast_to([64, RT, D]),
                                     start=True, stop=False, skip_group_check=True)
                        for r in range(RT):
                            if r == RT // 2 and a.has_tile(0):
                                wait(e, s["g_hi"], a.t, 2, a.bp - 1)
                                take(tpar, a.bp, 1, psR[:])
                            if a.has(0):
                                for ft in range(FT):
                                    last = matmul3(e, psE[:, r, :],
                                                   [h[:, par, hl, ft, r * P:r * P + P] for hl in range(2)],
                                                   [w2[:, hl, bass.ds(a.expert(0), 1), ft, :]
                                                    .rearrange("p o f -> p (o f)") for hl in range(2)],
                                                   False, ft == FT - 1, skip_group_check=True)
                        if a.has(0):
                            last.then_inc(s["E"], 1)
                        if a.bp == 1 and a.has_tile(1):
                            wait(e, s["pick"], a.t + 1)
                            wait(e, s["g_lo"], a.t, 2)
                            batch_rows(1 - tpar)
                        if a.has(-1):
                            wait(e, s["put"], j - 1, RT)
                            wait(e, s["eo_lo"], j - 1)
                            if a.e == 1 and a.i is None:
                                wait(e, seeded["xadd"], flat(a.G, 1, None, 0, -1))
                            for r in range(RT):
                                for hl in range(2):
                                    for bp in range(2):
                                        rows = slice(64 * bp, 64 * bp + 64)
                                        last = e.matmul(psA[:, bp, r, :], put[rows, r, :], eo[rows, hl, r, :],
                                                        start=a.e == 1 and r == hl == 0,
                                                        stop=a.e == NE and hl == 1, skip_group_check=True)
                            last.then_inc(s["A"], 1)
                    all_steps(e, body, lambda G: None)

                @block.scalar
                def _(e):
                    for k in range(GT + 1):
                        t = Step(None, 0, k)
                        wait(e, s["ln"], t)
                        wait(e, s["g"], t - 2, 4)
                        e.activation(xn[:, k % 2, 0], xnf[:, k % 2], ACT.Copy).then_inc(s["x_hi"], 1)
                        if k < GT:
                            for bp in range(2):
                                wait(e, s["g"], t, 4, 2 * bp + 1 - 3)
                                e.activation(gathered(0, 1, 2 * k + bp),
                                             psH[:, 2 * bp + 1, :].rearrange("p (e c) -> p e c", c=CAP), ACT.Copy)\
                                 .then_inc(s["g_lo"], 1)

                    def body(a):
                        j, par = a.j, a.par

                        def others():
                            if a.has(-1):
                                wait(e, s["gated"], j - 1)
                                wait(e, seeded["A"], j - 2)
                                e.activation(eo[:, 0], eo32[:], ACT.Copy).then_inc(s["eo_hi"], 1)
                            if a.has_tile(0):
                                wait(e, s["g"], a.t, 4, 2 * a.bp + 1 - 3)
                                e.activation(rows_of(a)[1], psR[:].rearrange("p (e c) -> p e c", c=CAP), ACT.Copy)\
                                 .then_inc(s["g_lo"], 1)
                            if a.bp == 1 and a.has_tile(1):
                                tpar = (a.k + 1) % 2
                                wait(e, s["ln"], a.t + 1)
                                wait(e, s["g"], a.t - 1, 4)
                                e.activation(xn[:, tpar, 0], xnf[:, tpar], ACT.Copy).then_inc(s["x_hi"], 1)

                        for ft in range(FT):
                            if ft == 2:
                                others()
                            if a.has(1):
                                wait(e, s["H"], j + 1, FT, ft + 1 - FT)
                                if ft % 2 == 0:
                                    wait(e, s["h_lo"], j, 2, ft // 2 - 1)
                                e.activation(g32[:, ft, :], psH[:, ft, :], ACT.Gelu_apprx_tanh,
                                             bias=b1T[:, bass.ds(a.expert(1) * FT + ft, 1)]).then_inc(s["gelu"], 1)
                                if ft % 2 == 1:
                                    wait(e, s["gelu"], j + 1, FT, ft + 1 - FT)
                                    wait(e, s["E"], j - 1)
                                    e.activation(h[:, 1 - par, 0, ft - 1:ft + 1, :], g32[:, ft - 1:ft + 1, :],
                                                 ACT.Copy).then_inc(s["h_hi"], 1)
                    all_steps(e, body, lambda G: None)

                @block.vector
                def _(e):
                    def queue_tile(t, par):
                        wait(e, s["R"], t - 2)
                        e.tensor_copy(pick[:, par].rearrange("p (b n) -> p b n", n=N),
                                      ident16[:, bass.ds(t.times(2), 2)].unsqueeze(2)
                                      .broadcast_to([P, 2, N])).then_inc(s["pick"], 1)
                        wait(e, s["x_lo"], t - 2)
                        e.tensor_scalar(xnf[:, par], tile_of(t, x), column_of(t, mean), column_of(t, rstd),
                                        ALU.subtract, ALU.mult).then_inc(s["ln"], 1)

                    def split_tile(t, par):
                        wait(e, s["x_hi"], t)
                        e.tensor_tensor(xn[:, par, 1], xnf[:, par], xn[:, par, 0], ALU.subtract)\
                         .then_inc(s["x_lo"], 1)

                    def select(t, par):
                        wait(e, s["R"], t)
                        wait(e, s["g"], t - 2, 4)
                        e.tensor_scalar(sel[:, par, :], psR[:], token_of_p[:], None, ALU.is_equal)\
                         .then_inc(s["sel"], 1)

                    def gather_hi(t, bp, to, frm):
                        wait(e, s["g"], t, 4, 2 * bp - 3)
                        e.tensor_copy(to, frm.rearrange("p (e c) -> p e c", c=CAP)).then_inc(s["g_hi"], 1)

                    queue_tile(Step(None, 0, 0), 0)
                    for k in range(GT + 1):
                        t = Step(None, 0, k)
                        split_tile(t, k % 2)
                        select(t, k % 2)
                        if k < GT:
                            queue_tile(t + 1, 1 - k % 2)
                            for bp in range(2):
                                gather_hi(t, bp, gathered(0, 0, 2 * k + bp), psH[:, 2 * bp, :])

                    def body(a):
                        j, par = a.j, a.par
                        next_tile = a.bp == 1 and a.has_tile(1)
                        if a.has(-1):
                            wait(e, seeded["A"], j - 2)
                            for r in range(RT):
                                e.tensor_scalar(put[:, r, :], iota[:],
                                                tok_slot[:, bass.ds(a.expert(-1), 1),
                                                         bass.ds(a.group(-1) * RT + r, 1)]
                                                .rearrange("p o r -> p (o r)"),
                                                None, ALU.is_equal).then_inc(s["put"], 1)
                        if a.has_tile(0):
                            gather_hi(a.t, a.bp, rows_of(a)[0], psR[:])
                        if next_tile:
                            queue_tile(a.t + 1, (a.k + 1) % 2)
                        if a.has(-1):
                            wait(e, s["eo_hi"], j - 1)
                            e.tensor_tensor(eo[:, 1], eo32[:], eo[:, 0], ALU.subtract)\
                             .then_inc(s["eo_lo"], 1)
                        if next_tile:
                            split_tile(a.t + 1, (a.k + 1) % 2)
                        for q in range(2):
                            if a.has(1):
                                wait(e, s["h_hi"], j + 1, 2, q - 1)
                                wait(e, s["E"], j - 1)
                                e.tensor_tensor(h[:, 1 - par, 1, 2 * q:2 * q + 2, :], g32[:, 2 * q:2 * q + 2, :],
                                                h[:, 1 - par, 0, 2 * q:2 * q + 2, :], ALU.subtract)\
                                 .then_inc(s["h_lo"], 1)
                            if q == 0 and next_tile:
                                select(a.t + 1, (a.k + 1) % 2)
                        if a.has(0):
                            wait(e, s["E"], j)
                            wait(e, s["eo_lo"], j - 1)
                            g4 = gate_slot[:, bass.ds(a.expert(0), 1), bass.ds(a.group(0) * RT, RT)]\
                                .rearrange("p o r -> p (o r)")
                            e.tensor_tensor(eo32[:], psE[:], g4.unsqueeze(2).broadcast_to([P, RT, D]),
                                            ALU.mult).then_inc(s["gated"], 1)

                    def residual(G):
                        wait(e, seeded["A"], At(G, NE - 1).j)
                        for q in range(2):
                            xs = x[:].rearrange("p (t h) d -> p t h d", h=2)[:, bass.ds(G * RT, RT), q, :]
                            last = e.scalar_tensor_tensor(xs, psA[:, q], gate, xs, ALU.mult, ALU.add)
                        last.then_inc(s["xadd"], 1)
                        wait(e, seeded["xadd"], flat(G, 1, None, 0, 0))
                        for k in range(GT):
                            queue_stats(e, flat(G, GT, None, 0, k))
                    all_steps(e, body, residual)
        s.close()

    def routed(tag, so):
        norm_statistics(tag + "n")
        s = Sems(tag)
        with ExitStack() as c:
            w1 = sb(c, "rw1", [P, 2, NE1, D], F16)
            w2 = sb(c, "rw2", [P, 2, NE1, D], F16)
            b1s = sb(c, "b1s", [P, B, TOPK], F32)
            b2s = sb(c, "b2s", [P, B], F32)
            erow = sb(c, "erow", [1, B * TOPK], U32)
            with ExitStack() as cr:
                raw = sb(cr, "rraw", [P, 2, NE1, D], F32)
                wr32 = sb(cr, "wr32", [P, NE1], F32)
                wr = sb(cr, "wr", [P, 2, NE1], F16)
                br = sb(cr, "br", [P, NE1], F32)
                b12 = sb(cr, "b12", [NE1, 2, D], F32)
                x0 = sb(cr, "x0", [P, D], F32)
                st = sb(cr, "st", [P, 6], F32)
                mv = sb(cr, "mv", [P, 2], F32)
                sd = sb(cr, "sd", [P, 2], F32)
                xn0 = sb(cr, "xn0", [P, D], F32)
                xh0 = sb(cr, "xh0", [P, 2, D], F16)
                xT0 = sb(cr, "xT0", [P, 2, P], F16)
                sc = sb(cr, "sc", [P, NE1], F32)
                best = sb(cr, "best", [P, 8], F32)
                bi = sb(cr, "bi", [P, 8], U32)
                bf = sb(cr, "bf", [P, 8], F32)
                at = sb(cr, "at", [P, TOPK], U32)
                oh = sb(cr, "oh", [P, TOPK, NE1], F32)
                i8 = sb(cr, "i8", [P, NE1], F32)
                ohT = sb(cr, "ohT", [NE1, TOPK, B], F32)
                psX0 = ps(cr, "psX0", [P, 2, P], F16)
                psC = ps(cr, "psC", [P, 512], F32)
                psB = ps(cr, "psB", [P, 512], F32)
                dram = nc.dram_tensor("choices", [B, TOPK], U32)
                with nc.Block() as block:
                    @block.sync
                    def _(e):
                        load_all(e, s["w"], [(raw[:, 0], I["L1_ffn_W1"].rearrange("e d f -> d e f")),
                                             (raw[:, 1], I["L1_ffn_W2"].rearrange("e d f -> d e f"))])
                        load_all(e, s["c"], [(wr32[:], I["L1_ffn_Wr"]), (br[:], I["L1_ffn_br"].partition_broadcast(P)),
                                             (b12[:, 0], I["L1_ffn_b1"]), (b12[:, 1], I["L1_ffn_b2"])])
                        load_all(e, s["x0"], [(x0[bp::2, :], x[64 * bp:64 * bp + 1, :, :]) for bp in range(2)])
                        e.wait_ge(s["at"], 1)
                        e.dma_start(dram.ap(), at[:]).then_inc(s["choices"], 16)
                        e.wait_ge(s["choices"], 16)
                        e.dma_start(erow[:], dram.ap().rearrange("b k -> (b k)").unsqueeze(0)).then_inc(s["erow"], 16)
                        e.wait_ge(s["erow"], 16)

                    @block.gpsimd
                    def _(e):
                        e.iota(i8[:], [[1, NE1]], base=0, channel_multiplier=0,
                               allow_small_or_imprecise_dtypes=True).then_inc(s["i8"], 1)

                    parts = [(wr32[:], wr[:, 0], wr[:, 1]), (xn0[:], xh0[:, 0], xh0[:, 1]),
                             (raw[:, 0], w1[:, 0], w1[:, 1]), (raw[:, 1], w2[:, 0], w2[:, 1])]

                    @block.scalar
                    def _(e):
                        e.wait_ge(s["var"], 1)
                        e.activation(sd[:, 0:1], mv[:, 1:2], ACT.Sqrt, bias=eps_col[:]).then_inc(s["sd"], 1)
                        e.wait_ge(s["c"], 64)
                        split(e, None, s, 0, *parts[0])
                        e.wait_ge(s["ln0"], 1)
                        split(e, None, s, 1, *parts[1])
                        e.wait_ge(s["w"], 32)
                        split(e, None, s, 2, *parts[2])
                        split(e, None, s, 3, *parts[3])

                    @block.vector
                    def _(e):
                        e.wait_ge(s["x0"], 32)
                        e.bn_stats(st[:], x0[:]).then_inc(s["st"], 1)
                        e.wait_ge(s["st"], 1)
                        e.bn_aggr(mv[:], st[:]).then_inc(s["var"], 1)
                        e.wait_ge(s["sd"], 1)
                        e.reciprocal(sd[:, 1:2], sd[:, 0:1]).then_inc(s["rs"], 1)
                        e.wait_ge(s["rs"], 1)
                        e.tensor_scalar(xn0[:], x0[:], mv[:, 0:1], sd[:, 1:2], ALU.subtract, ALU.mult)\
                         .then_inc(s["ln0"], 1)
                        split(None, e, s, 0, *parts[0])
                        split(None, e, s, 1, *parts[1])
                        e.wait_ge(s["X0"], 1)
                        e.tensor_copy(xT0[:], psX0[:]).then_inc(s["xT0"], 1)
                        e.wait_ge(s["C"], 1)
                        e.tensor_tensor(sc[:], psC[:, 0:NE1], br[:], ALU.add).then_inc(s["sc"], 1)
                        e.wait_ge(s["sc"], 1)
                        e.max(best[:], sc[:]).then_inc(s["best"], 1)
                        e.wait_ge(s["best"], 1)
                        e.max_index(bi[:], best[:], sc[:]).then_inc(s["bi"], 1)
                        e.wait_ge(s["bi"], 1)
                        e.tensor_copy(bf[:], bi[:]).then_inc(s["bf"], 1)
                        e.wait_ge(s["bf"], 1)
                        e.tensor_scalar(at[:], bf[:, 0:TOPK], float(D), None, ALU.mult).then_inc(s["at"], 1)
                        e.wait_ge(s["i8"], 1)
                        for k in range(TOPK):
                            e.tensor_scalar(oh[:, k, :], i8[:], bf[:, k:k + 1], None, ALU.is_equal)\
                             .then_inc(s["oh"], 1)
                        e.wait_ge(s["ohP"], 1)
                        e.tensor_copy(ohT[:], psB[0:NE1, 0:TOPK * B].rearrange("p (k b) -> p k b", b=B))\
                         .then_inc(s["ohT"], 1)
                        e.wait_ge(s["bP"], 1)
                        e.tensor_copy(b1s[:].rearrange("p b k -> p k b"),
                                      psC[:, 0:TOPK * B].rearrange("p (k b) -> p k b", b=B))
                        e.tensor_copy(b2s[:], psC[:, TOPK * B:TOPK * B + B])
                        split(None, e, s, 2, *parts[2])
                        split(None, e, s, 3, *parts[3])

                    @block.tensor
                    def _(e):
                        e.wait_ge(s["w_lo"], 2)
                        for hl in range(2):
                            last = e.transpose(psX0[:, hl, :], xh0[:, hl, :], ident16[:])
                        last.then_inc(s["X0"], 1)
                        e.wait_ge(s["xT0"], 1)
                        matmul3(e, psC[:, 0:NE1], (xT0[:, 0], xT0[:, 1]), (wr[:, 0], wr[:, 1])).then_inc(s["C"], 1)
                        e.wait_ge(s["oh"], TOPK)
                        for k in range(TOPK):
                            last = e.matmul(psB[0:NE1, k * B:k * B + B], oh[:, k, :], ident32[:], start=True, stop=True)
                        last.then_inc(s["ohP"], 1)
                        e.wait_ge(s["ohT"], 1)
                        e.matmul(psC[:, 0:TOPK * B], b12[:, 0, :], ohT[:].rearrange("p k b -> p (k b)"),
                                 start=True, stop=True)
                        for k in range(TOPK):
                            last = e.matmul(psC[:, TOPK * B:TOPK * B + B], b12[:, 1, :], ohT[:, k, :],
                                            start=k == 0, stop=k == TOPK - 1)
                        last.then_inc(s["bP"], 1)

            TS = 2
            BK = 2 * TS * TOPK
            STEPS = NT // TS
            xnf = sb(c, "xnfr", [P, 2, TS, D], F32)
            xn = sb(c, "xnr", [P, 2, 2, TS, D], F16)
            xT = sb(c, "xTr", [P, 2, 2, TS * P], F16)
            a32 = sb(c, "a32", [P, BK, N], F32)
            g32 = sb(c, "g32r", [P, BK, N], F32)
            h = sb(c, "hr", [P, 2, 2, BK, N], F16)
            y32 = sb(c, "y32", [P, 2, 2 * TS, N], F32)
            psX = ps(c, "psXr", [P, 2, TS, P], F16)
            psH = ps(c, "psHr", [P, 2, BK, N], F32)
            psO = ps(c, "psOr", [P, 2, 8, N], F32)
            psZ = ps(c, "psZr", [P, 2, 4, P], F32)
            w1a, w2a = (w[:].rearrange("p h e f -> p h (e f)") for w in (w1, w2))
            with nc.Block() as block:
                @block.tensor
                def _(e):
                    def experts(j):
                        return nc.values_load_multi_w_load_instructions(
                            erow[0:1, bass.ds(j.times(BK), BK)], engines=(mybir.EngineType.PE,),
                            min_val=0, max_val=(NE1 - 1) * D,
                            skip_runtime_bounds_check_because="D times an index of 8 columns that MaxIndex gave")[1]

                    def body(j):
                        if (j + 1).inside(STEPS):
                            par = (j + 1).mod(2)
                            wait(e, s["x_lo"], j + 1)
                            wait(e, s["xT"], j)
                            for hl in range(2):
                                for k in range(TS):
                                    last = e.transpose(psX[:, hl, k, :], xn[:, par, hl, k, :], ident16[:])
                            last.then_inc(s["X"], 1)
                        if (j - 2).inside(STEPS):
                            par = j.mod(2)
                            ids = experts(j - 2)
                            wait(e, s["h_lo"], j - 2)
                            wait(e, s["y"], j - 4)
                            for q in range(BK):
                                b, k = q // TOPK, q % TOPK
                                last = matmul3(e, psO[:, par, b, :],
                                               [w2a[:, hl, bass.ds(ids[q], D)] for hl in range(2)],
                                               [h[:, par, hl, q, :] for hl in range(2)], k == 0, k == TOPK - 1)
                            last.then_inc(s["O"], 1)
                        if j.inside(STEPS):
                            par = j.mod(2)
                            ids = experts(j)
                            wait(e, s["xT"], j)
                            wait(e, s["bias"], j - 2)
                            for q in range(BK):
                                b = q // TOPK
                                last = matmul3(e, psH[:, par, q, :],
                                               [w1a[:, hl, bass.ds(ids[q], D)] for hl in range(2)],
                                               [xT[:, par, hl, N * b:N * b + N] for hl in range(2)])
                            last.then_inc(s["H"], 1)
                        if (j - 3).inside(STEPS):
                            par = (j - 3).mod(2)
                            wait(e, s["y"], j - 3)
                            wait(e, s["res"], j - 5)
                            for k in range(TS):
                                last = e.transpose(psZ[:, par, k, :], y32[:, par, 2 * k:2 * k + 2, :]
                                                   .rearrange("p b n -> p (b n)"), ident32[:])
                            last.then_inc(s["Z"], 1)
                    pipeline(e, body, -1, STEPS + 3, 6, STEPS - 4, 2)

                @block.scalar
                def _(e):
                    def body(j):
                        if (j - 1).inside(STEPS):
                            par = (j - 1).mod(2)
                            wait(e, s["bias"], j - 1)
                            wait(e, s["h_lo"], j - 2)
                            e.activation(g32[:], a32[:], ACT.Gelu, bias=zero_col[:]).then_inc(s["gelu"], 1)
                            wait(e, s["gelu"], j - 1)
                            wait(e, s["O"], j - 3)
                            e.activation(h[:, par, 0], g32[:], ACT.Copy).then_inc(s["h_hi"], 1)
                        if (j + 3).inside(STEPS):
                            par = (j + 3).mod(2)
                            wait(e, s["ln"], j + 3)
                            wait(e, s["X"], j + 1)
                            e.activation(xn[:, par, 0], xnf[:, par], ACT.Copy).then_inc(s["x_hi"], 1)
                    pipeline(e, body, -3, STEPS + 1, 6, STEPS - 4, 2)

                @block.vector
                def _(e):
                    def body(j):
                        if (j - 2).inside(STEPS):
                            par = (j - 2).mod(2)
                            wait(e, s["O"], j - 2)
                            wait(e, s["Z"], j - 4)
                            e.tensor_tensor(y32[:, par], psO[:, par, 0:2 * TS, :],
                                            b2s[:, bass.ds((j - 2).times(2 * TS), 2 * TS)].unsqueeze(2)
                                            .broadcast_to([P, 2 * TS, N]), ALU.add).then_inc(s["y"], 1)
                        if (j - 1).inside(STEPS):
                            par = (j - 1).mod(2)
                            wait(e, s["h_hi"], j - 1)
                            e.tensor_tensor(h[:, par, 1], g32[:], h[:, par, 0], ALU.subtract).then_inc(s["h_lo"], 1)
                        if (j + 2).inside(STEPS):
                            par = (j + 2).mod(2)
                            wait(e, s["x_hi"], j + 2)
                            e.tensor_tensor(xn[:, par, 1], xnf[:, par], xn[:, par, 0], ALU.subtract)\
                             .then_inc(s["x_lo"], 1)
                        if (j + 1).inside(STEPS):
                            wait(e, s["X"], j + 1)
                            e.tensor_copy(xT[:, (j + 1).mod(2)], psX[:].rearrange("p h k t -> p h (k t)"))\
                             .then_inc(s["xT"], 1)
                        if j.inside(STEPS):
                            wait(e, s["H"], j)
                            wait(e, s["gelu"], j - 1)
                            bias = b1s[:, bass.ds(j.times(2 * TS), 2 * TS), :].rearrange("p b k -> p (b k)")
                            e.tensor_tensor(a32[:], psH[:, j.mod(2)], bias.unsqueeze(2).broadcast_to([P, BK, N]),
                                            ALU.add).then_inc(s["bias"], 1)
                        if (j - 3).inside(STEPS):
                            t = j - 3
                            wait(e, s["Z"], t)
                            xs = x[:, bass.ds(t.times(TS), TS), :]
                            e.scalar_tensor_tensor(xs, psZ[:, t.mod(2), 0:TS, :], half_g[:], xs,
                                                   ALU.mult, ALU.add).then_inc(s["res"], 1)
                        if (j + 3).inside(STEPS):
                            par = (j + 3).mod(2)
                            wait(e, s["x_lo"], j + 1)
                            for k in range(TS):
                                t = Step((j + 3).times(TS), 1, k)
                                last = e.tensor_scalar(xnf[:, par, k], tile_of(t, x), column_of(t, mean),
                                                       column_of(t, rstd), ALU.subtract, ALU.mult)
                            last.then_inc(s["ln"], 1)
                    pipeline(e, body, -3, STEPS + 3, 6, STEPS - 4, 2)

                @block.sync
                def _(e):
                    for k in range(0, NT, 8):
                        e.wait_ge(s["res"], (k + 8) // TS)
                        e.dma_start(ov[:, k:k + 8, :], x[:, k:k + 8, :]).then_inc(so, 16)
                    e.wait_ge(so, 16 * NT // 8)
        s.close()

    S0.close()
    attention("a0", 1, I["L0_xattn_Wq"], I["L0_xattn_Wk"], I["L0_xattn_Wv"], I["L0_xattn_Wo"],
              I["L0_xattn_bo"], tanh_g[:, 0:1], first=True)
    expert_choice("m", tanh_g[:, 2:3])
    attention("a1", 2, I["L1_xattn_Wq"], I["L1_xattn_Wk"], I["L1_xattn_Wv"], I["L1_xattn_Wo"],
              I["L1_xattn_bo"], tanh_g[:, 1:2])
    routed("r", sem("out"))


_OUTS = [((B, N, D), "float32")]


def kernel(**inputs):
    import numpy as _np
    import concourse.bacc as _bacc
    from concourse import mybir as _mybir
    from concourse.bass_utils import run_bass_kernel_spmd as _run

    nc = _bacc.Bacc("TRN2", target_bir_lowering=False, num_devices=1)
    arrays, args = {}, {}
    for name, a in inputs.items():
        a = _np.ascontiguousarray(a)
        if a.ndim == 0:
            a = a.reshape(1)
        arrays[f"in_{name}_dram"] = a
        args[name] = nc.dram_tensor(f"in_{name}_dram", a.shape, _mybir.dt.from_np(a.dtype), kind="ExternalInput").ap()
    shape, dtype = _OUTS[0]
    o = nc.dram_tensor("out_0_dram", shape, _mybir.dt.from_np(_np.dtype(dtype)), kind="ExternalOutput").ap()
    program(nc, args, o)
    r = _run(nc, [arrays], core_ids=[0])
    return r.results[0]["out_0_dram"]
```
